# Optimizing a Trainium2 kernel written in Bass

```python
import numpy as np
import jax
import jax.numpy as jnp

def _softmax(x, axis=-1):
    return jax.nn.softmax(x, axis=axis)

def _gelu(x):
    return jax.nn.gelu(x, approximate=True)

def _silu(x):
    return jax.nn.silu(x)

def _sigmoid(x):
    return jax.nn.sigmoid(x)

def _layernorm(x, axis=-1, eps=1e-05):
    m = jnp.mean(x, axis=axis, keepdims=True)
    v = jnp.var(x, axis=axis, keepdims=True)
    return (x - m) / jnp.sqrt(v + eps)

def _scatter_add(tgt, idx, src, axis=0):
    return tgt.at[idx].add(src)

def _segment_sum(src, seg, n):
    return jax.ops.segment_sum(src, seg, n)
kernel_name = 'mk_seq_preln_d1_jaxref_r8_592c4d'

def setup_inputs(seed: int=0):
    np.random.seed(seed)
    _w = jnp.asarray

    def _L0_attn_setup():
        import jax, jax.numpy as jnp
        import numpy as np
        D_MODEL = 256
        N_HEAD = 16
        MLP_HIDDEN = 704
        NORMALIZER = 16.0

        def rmsnorm(x, w, eps=1e-05):
            return x * jax.lax.rsqrt(jnp.mean(x * x, axis=-1, keepdims=True) + eps) * w

        def _reference_tuple_inner(x, Wq, Wk, Wkg1, Wkg2, bkg2, Wv, Wg, bg, Wo, ln1_w, ln2_w, W1, W3, W2):
            B, L, d = x.shape
            H = N_HEAD
            hd = d // H
            kd = d // 2 // H
            scaling = (d // H) ** (-0.5)
            xn = rmsnorm(x, ln1_w)
            q = xn @ Wq
            k = xn @ Wk * scaling
            gk = jax.nn.log_sigmoid(xn @ Wkg1 @ Wkg2 + bkg2) / NORMALIZER
            v = xn @ Wv
            g = xn @ Wg + bg
            split = lambda t, dh: t.reshape(B, L, H, dh).transpose(1, 0, 2, 3)
            qh, kh, gh = (split(q, kd), split(k, kd), split(gk, kd))
            vh = split(v, hd)
            S0 = jnp.zeros((B, H, kd, hd), x.dtype)

            def step(S, inp):
                qt, kt, vt, gt = inp
                S = S * jnp.exp(gt)[..., None] + kt[..., None] * vt[..., None, :]
                ot = jnp.einsum('bhk,bhkd->bhd', qt, S)
                return (S, ot)
            Sf, o = jax.lax.scan(step, S0, (qh, kh, vh, gh))
            mu = jnp.mean(o, axis=-1, keepdims=True)
            var = jnp.var(o, axis=-1, keepdims=True)
            o = (o - mu) * jax.lax.rsqrt(var + 1e-05)
            o = o.transpose(1, 0, 2, 3).reshape(B, L, d)
            o = jax.nn.silu(g) * o
            x = x + o @ Wo
            xn2 = rmsnorm(x, ln2_w)
            x = x + jax.nn.silu(xn2 @ W1) * (xn2 @ W3) @ W2
            return (x, Sf)
        key = jax.random.key(seed)
        d, B, L, Hd = (D_MODEL, 2, 512, MLP_HIDDEN)
        ks = jax.random.split(key, 12)
        w = lambda k, shape, s=0.02: jax.random.normal(k, shape, jnp.float32) * s
        return {'x': jax.random.normal(ks[0], (B, L, d), jnp.float32), 'Wq': w(ks[1], (d, d // 2)), 'Wk': w(ks[2], (d, d // 2)), 'Wkg1': w(ks[3], (d, 16)), 'Wkg2': w(ks[4], (16, d // 2)), 'bkg2': jnp.zeros((d // 2,), jnp.float32), 'Wv': w(ks[5], (d, d)), 'Wg': w(ks[6], (d, d)), 'bg': jnp.zeros((d,), jnp.float32), 'Wo': w(ks[7], (d, d)), 'ln1_w': jnp.ones((d,), jnp.float32), 'ln2_w': jnp.ones((d,), jnp.float32), 'W1': w(ks[8], (d, Hd)), 'W3': w(ks[9], (d, Hd)), 'W2': w(ks[10], (Hd, d))}
    _L0_attn_in = _L0_attn_setup()

    def _L0_ffn_setup():
        import jax, jax.numpy as jnp
        import numpy as np
        from functools import partial
        E = 8
        K = 2
        H = 256
        F = 1024

        def _moe_forward(x, gate_w, gate_b, fc1_w, fc1_b, fc2_w, fc2_b, alpha):
            B_, S_, H_ = x.shape
            xf = x.reshape(-1, H_)
            logits = xf @ gate_w + gate_b
            top_val, top_idx = jax.lax.top_k(logits, K)
            gate_score = jax.nn.softmax(top_val, axis=-1)
            onehot = jax.nn.one_hot(top_idx, E, dtype=xf.dtype)
            comb = jnp.einsum('tk,tke->et', gate_score, onehot) * alpha[:, None]

            def body(acc, p):
                w1, b1, w2, b2, w = p
                h = jax.nn.gelu(xf @ w1 + b1, approximate=False)
                y = h @ w2 + b2
                return (acc + y * w[:, None], None)
            out0 = jnp.zeros_like(xf)
            out, _ = jax.lax.scan(body, out0, (fc1_w, fc1_b, fc2_w, fc2_b, comb))
            return out.reshape(B_, S_, H_)
        key = jax.random.key(seed)
        ks = jax.random.split(key, 8)
        s = 0.02
        return {'hidden_states': jax.random.normal(ks[0], (2, 256, H), jnp.float32), 'gate_w': jax.random.normal(ks[1], (H, E), jnp.float32) * s, 'gate_b': jax.random.normal(ks[2], (E,), jnp.float32) * s, 'fc1_w': jax.random.normal(ks[3], (E, H, F), jnp.float32) * s, 'fc1_b': jax.random.normal(ks[4], (E, F), jnp.float32) * s, 'fc2_w': jax.random.normal(ks[5], (E, F, H), jnp.float32) * s, 'fc2_b': jax.random.normal(ks[6], (E, H), jnp.float32) * s, 'alpha': jax.random.normal(ks[7], (E,), jnp.float32)}
    _L0_ffn_in = _L0_ffn_setup()
    _d = {'L0_attn_x': _L0_attn_in['x'], 'L0_attn_Wq': _L0_attn_in['Wq'], 'L0_attn_Wk': _L0_attn_in['Wk'], 'L0_attn_Wkg1': _L0_attn_in['Wkg1'], 'L0_attn_Wkg2': _L0_attn_in['Wkg2'], 'L0_attn_bkg2': _L0_attn_in['bkg2'], 'L0_attn_Wv': _L0_attn_in['Wv'], 'L0_attn_Wg': _L0_attn_in['Wg'], 'L0_attn_bg': _L0_attn_in['bg'], 'L0_attn_Wo': _L0_attn_in['Wo'], 'L0_attn_ln1_w': _L0_attn_in['ln1_w'], 'L0_attn_ln2_w': _L0_attn_in['ln2_w'], 'L0_attn_W1': _L0_attn_in['W1'], 'L0_attn_W3': _L0_attn_in['W3'], 'L0_attn_W2': _L0_attn_in['W2'], 'L0_ffn_gate_w': _L0_ffn_in['gate_w'], 'L0_ffn_gate_b': _L0_ffn_in['gate_b'], 'L0_ffn_fc1_w': _L0_ffn_in['fc1_w'], 'L0_ffn_fc1_b': _L0_ffn_in['fc1_b'], 'L0_ffn_fc2_w': _L0_ffn_in['fc2_w'], 'L0_ffn_fc2_b': _L0_ffn_in['fc2_b'], 'L0_ffn_alpha': _L0_ffn_in['alpha']}
    _x0 = _d['L0_attn_x']
    _d['L0_attn_x'] = jax.random.normal(jax.random.fold_in(jax.random.key(seed), 1), (4, 512, 256), dtype=_x0.dtype)
    del _x0
    return _d

def reference(L0_attn_x, L0_attn_Wq, L0_attn_Wk, L0_attn_Wkg1, L0_attn_Wkg2, L0_attn_bkg2, L0_attn_Wv, L0_attn_Wg, L0_attn_bg, L0_attn_Wo, L0_attn_ln1_w, L0_attn_ln2_w, L0_attn_W1, L0_attn_W3, L0_attn_W2, L0_ffn_gate_w, L0_ffn_gate_b, L0_ffn_fc1_w, L0_ffn_fc1_b, L0_ffn_fc2_w, L0_ffn_fc2_b, L0_ffn_alpha):

    def _L0_attn_ref(x, Wq, Wk, Wkg1, Wkg2, bkg2, Wv, Wg, bg, Wo, ln1_w, ln2_w, W1, W3, W2):
        import jax, jax.numpy as jnp
        import numpy as np
        D_MODEL = 256
        N_HEAD = 16
        MLP_HIDDEN = 704
        NORMALIZER = 16.0

        def rmsnorm(x, w, eps=1e-05):
            return x * jax.lax.rsqrt(jnp.mean(x * x, axis=-1, keepdims=True) + eps) * w

        def _reference_tuple_inner(x, Wq, Wk, Wkg1, Wkg2, bkg2, Wv, Wg, bg, Wo, ln1_w, ln2_w, W1, W3, W2):
            B, L, d = x.shape
            H = N_HEAD
            hd = d // H
            kd = d // 2 // H
            scaling = (d // H) ** (-0.5)
            xn = rmsnorm(x, ln1_w)
            q = xn @ Wq
            k = xn @ Wk * scaling
            gk = jax.nn.log_sigmoid(xn @ Wkg1 @ Wkg2 + bkg2) / NORMALIZER
            v = xn @ Wv
            g = xn @ Wg + bg
            split = lambda t, dh: t.reshape(B, L, H, dh).transpose(1, 0, 2, 3)
            qh, kh, gh = (split(q, kd), split(k, kd), split(gk, kd))
            vh = split(v, hd)
            S0 = jnp.zeros((B, H, kd, hd), x.dtype)

            def step(S, inp):
                qt, kt, vt, gt = inp
                S = S * jnp.exp(gt)[..., None] + kt[..., None] * vt[..., None, :]
                ot = jnp.einsum('bhk,bhkd->bhd', qt, S)
                return (S, ot)
            Sf, o = jax.lax.scan(step, S0, (qh, kh, vh, gh))
            mu = jnp.mean(o, axis=-1, keepdims=True)
            var = jnp.var(o, axis=-1, keepdims=True)
            o = (o - mu) * jax.lax.rsqrt(var + 1e-05)
            o = o.transpose(1, 0, 2, 3).reshape(B, L, d)
            o = jax.nn.silu(g) * o
            x = x + o @ Wo
            xn2 = rmsnorm(x, ln2_w)
            x = x + jax.nn.silu(xn2 @ W1) * (xn2 @ W3) @ W2
            return (x, Sf)
        return _reference_tuple_inner(x, Wq, Wk, Wkg1, Wkg2, bkg2, Wv, Wg, bg, Wo, ln1_w, ln2_w, W1, W3, W2)[0]

    def _L0_ffn_ref(hidden_states, gate_w, gate_b, fc1_w, fc1_b, fc2_w, fc2_b, alpha):
        import jax, jax.numpy as jnp
        import numpy as np
        from functools import partial
        E = 8
        K = 2
        H = 256
        F = 1024

        def _moe_forward(x, gate_w, gate_b, fc1_w, fc1_b, fc2_w, fc2_b, alpha):
            B_, S_, H_ = x.shape
            xf = x.reshape(-1, H_)
            logits = xf @ gate_w + gate_b
            top_val, top_idx = jax.lax.top_k(logits, K)
            gate_score = jax.nn.softmax(top_val, axis=-1)
            onehot = jax.nn.one_hot(top_idx, E, dtype=xf.dtype)
            comb = jnp.einsum('tk,tke->et', gate_score, onehot) * alpha[:, None]

            def body(acc, p):
                w1, b1, w2, b2, w = p
                h = jax.nn.gelu(xf @ w1 + b1, approximate=False)
                y = h @ w2 + b2
                return (acc + y * w[:, None], None)
            out0 = jnp.zeros_like(xf)
            out, _ = jax.lax.scan(body, out0, (fc1_w, fc1_b, fc2_w, fc2_b, comb))
            return out.reshape(B_, S_, H_)
        return _moe_forward(hidden_states, gate_w, gate_b, fc1_w, fc1_b, fc2_w, fc2_b, alpha)
    x = L0_attn_x
    x = x + _L0_attn_ref(_layernorm(x, axis=-1), L0_attn_Wq, L0_attn_Wk, L0_attn_Wkg1, L0_attn_Wkg2, L0_attn_bkg2, L0_attn_Wv, L0_attn_Wg, L0_attn_bg, L0_attn_Wo, L0_attn_ln1_w, L0_attn_ln2_w, L0_attn_W1, L0_attn_W3, L0_attn_W2)
    x = x + _L0_ffn_ref(_layernorm(x, axis=-1), L0_ffn_gate_w, L0_ffn_gate_b, L0_ffn_fc1_w, L0_ffn_fc1_b, L0_ffn_fc2_w, L0_ffn_fc2_b, L0_ffn_alpha)
    return x

_drawn_inputs = setup_inputs


def setup_inputs(seed=0):
    import zlib

    import numpy as np

    out = dict(_drawn_inputs(seed))
    spreads = {'L0_attn_bkg2': (0.0, 0.8),
     'L0_attn_bg': (0.0, 0.8),
     'L0_attn_ln1_w': (1.0, 0.6),
     'L0_attn_ln2_w': (1.0, 0.6)}
    factors = {'L0_attn_Wkg1': 8.0,
     'L0_attn_Wkg2': 8.0,
     'L0_attn_W1': 3.49,
     'L0_attn_W3': 3.455,
     'L0_attn_W2': 3.454,
     'L0_ffn_gate_b': 18.867,
     'L0_ffn_fc1_b': 36.941,
     'L0_ffn_fc2_b': 7.109}
    for name, (base, spread) in spreads.items():
        noise = np.random.default_rng([zlib.crc32(name.encode()), seed]).standard_normal(out[name].shape)
        drawn = base * np.exp(spread * noise) if base else spread * noise
        out[name] = jnp.asarray(drawn.astype(out[name].dtype))
    for name, factor in factors.items():
        out[name] = (out[name] * factor).astype(out[name].dtype)
    return out
```

```python
from contextlib import ExitStack

import concourse.bass as bass
from concourse import mybir

F32 = mybir.dt.float32
F32R = mybir.dt.float32r
BF16 = mybir.dt.bfloat16
I32 = mybir.dt.int32
U32 = mybir.dt.uint32
ALU = mybir.AluOpType
ACT = mybir.ActivationFunctionType
AX = mybir.AxisListType

P = 128


def build(nc, x, Wq, Wk, Wkg1, Wkg2, bkg2, Wv, Wg, bg, Wo, ln1_w, ln2_w, W1, W3, W2,
          gate_w, gate_b, fc1_w, fc1_b, fc2_w, fc2_b, alpha, out):
    B, L, D = x.shape
    HK = Wq.shape[1]
    H = 16
    KD = HK // H
    HD = D // H
    MLP = W1.shape[1]
    E, _, F = fc1_w.shape
    T = B * L
    TT = L // P
    KB = D // P
    MB = -(-MLP // P)
    MLAST = MLP - (MB - 1) * P
    FB = F // P
    DB = P // H
    LOWRANK = Wkg1.shape[1]
    SCALE = float(HD) ** -0.5
    EPS = 1e-5
    NORMALIZER = 16.0
    MIN_TILES = 3
    NV = E * FB + 2 * KB + 1
    COLS = T // P + 2
    NOWHERE = 1 << 20

    x_rows = x.rearrange("b l d -> (b l) d")
    out_rows = out.rearrange("b l d -> (b l) d")
    x_tiles = x_rows.rearrange("(n p) d -> p n d", p=P)
    out_tiles = out_rows.rearrange("(n p) d -> p n d", p=P)

    normed_dram = nc.dram_tensor("normed_rows", [T, D], F32, kind="Internal").ap()
    normed_tiles = normed_dram.rearrange("(n p) d -> p n d", p=P)
    table_dram = nc.dram_tensor("routing_table", [P * E * COLS, 4], I32, kind="Internal").ap()
    table_view = table_dram.rearrange("(p c) w -> p c w", p=P)

    with ExitStack() as ctx:
        names = set()

        def sb(name, shape, dt=F32, scope=ctx):
            return scope.enter_context(nc.sbuf_tensor(name, shape, dt))

        def psum(name, shape, dt=F32):
            return ctx.enter_context(nc.psum_tensor(name, shape, dt))

        def sem(name):
            return ctx.enter_context(nc.semaphore(name))

        ring = [psum("ring0", [P, L]), psum("ring1", [P, L])]
        mix_ps = psum("mix_ps", [P, TT, D])
        up_ps = [psum("up0_ps", [P, L]), psum("up1_ps", [P, L])]
        res_ps = psum("res_ps", [P, TT, D])

        ident = sb("ident", [P, P])
        cols = sb("cols", [P, E * FB + 2 * KB + 1])
        B1_C, LN1_C, LN2_C, BK_C = 0, E * FB, E * FB + KB, E * FB + 2 * KB
        b2_bc = sb("b2_bc", [P, E, D])
        bounds = sb("bounds", [P, 3, E + 1], I32)
        eps = sb("eps", [P, 1])
        unit = sb("unit", [P, 1])
        one = ExitStack()
        ctx.enter_context(one)

        def s1(name, shape, dt=F32):
            return sb(name, shape, dt, one)

        xin = s1("xin", [P, TT, D])
        y = s1("y", [P, TT, D])
        zn = s1("zn", [P, TT, D])
        znT = [s1(f"znT{i}", [P, KB, L], F32R) for i in range(2)]
        kg1_sb = s1("kg1_sb", [LOWRANK, L])
        soft = s1("soft", [P, L])
        lsig = s1("lsig", [P, L])
        decay = s1("decay", [P, L])
        vT = [s1(f"vT{i}", [P, KB, L], F32R) for i in range(2)]
        kv = [s1(f"kv{i}", [P, L]) for i in range(2)]
        k_sb = s1("k_sb", [P, L])
        g_sb = s1("g_sb", [P, TT, D])
        g_den = s1("g_den", [P, TT, D])
        q_sb = s1("q_sb", [P, L])
        state = [s1(f"state{i}", [P, L]) for i in range(2)]
        qs = [s1(f"qs{i}", [P, L]) for i in range(2)]
        wqk = [s1(f"wqk{i}", [P, 2, KB, HK], F32R) for i in range(2)]
        wkg1 = [s1(f"wkg1{i}", [P, KB, P // LOWRANK, LOWRANK], F32R) for i in range(2)]
        wkg2 = s1("wkg2", [LOWRANK, HK])
        wv = [s1(f"wv{i}", [P, KB, HD, H], F32R) for i in range(2)]
        wg = [s1(f"wg{i}", [P, KB, D], F32R) for i in range(2)]
        spread = s1("spread", [P, DB, P], F32R)
        gather_k = s1("gather_k", [P, H])
        bg_bc = s1("bg_bc", [P, D])
        stats = s1("stats", [P, TT, 6])
        mv = s1("mv", [P, TT, 2])
        small = s1("small", [P, 8, TT])
        wo = [s1(f"wo{i}", [P, KB, D], F32R) for i in range(2)]
        w1 = [s1(f"w1{i}", [P, KB, MB * P], F32R) for i in range(2)]
        w3 = [s1(f"w3{i}", [P, KB, MB * P], F32R) for i in range(2)]
        w2 = [s1(f"w2{i}", [P, MB, D], F32R) for i in range(2)]
        silu_g = s1("silu_g", [P, TT, D])
        y_keep = s1("y_keep", [P, TT, D])
        x_keep = s1("x_keep", [P, TT, D])
        x1x = s1("x1x", [P, TT, D])
        gate_sb = s1("gate_sb", [P, KB, E])
        gb_bc = s1("gb_bc", [P, E])
        al_bc = s1("al_bc", [P, E])
        earlier = s1("earlier", [P, P], BF16)
        ones_bf = s1("ones_bf", [P, P], BF16)
        eight = s1("eight", [P, E])
        token_id = s1("token_id", [P, T // P], I32)
        steps128 = s1("steps128", [P, T // P])
        first_slot = s1("first_slot", [P, E])
        o_sum = s1("o_sum", [P, 4, TT, H])
        rms = s1("rms", [P, 2, TT])
        x1_sq = s1("x1_sq", [P, D])
        stats2 = s1("stats2", [P, TT, 6])
        mv2 = s1("mv2", [P, TT, 2])
        small2 = s1("small2", [P, 2, TT])
        logit = s1("logit", [P, TT, E])
        top = s1("top", [P, TT, 8])
        topi = s1("topi", [P, TT, 8], U32)
        topf = s1("topf", [P, TT, 2])
        chosen = s1("chosen", [P, 2, TT, E])
        picked = s1("picked", [P, 2, TT, E])
        mask = s1("mask", [P, TT, E], BF16)
        taken = s1("taken", [P, E])
        taken_t = s1("taken_t", [P, E])
        taken_bf = s1("taken_bf", [P, E], BF16)
        score = s1("score", [P, 6, TT])
        pos = s1("pos", [P, 3, 2, TT])
        pos_i = s1("pos_i", [P, 3, 2, TT], I32)
        pos_f = s1("pos_f", [P, 2, 2, TT])
        where = s1("where", [P, 2, TT], I32)
        record = s1("record", [P, 2, TT, 4], I32)
        fill = s1("fill", [P, E * COLS, 4], I32)
        over = s1("over", [P, E, T // P])
        tiles_f = s1("tiles_f", [P, E])
        cum_f = s1("cum_f", [P, E])
        with ExitStack() as early:
            vec_rows = sb("vec_rows", [NV, P], F32, early)
            raw_qk = sb("raw_qk", [P, 2, KB, HK], F32, early)
            raw_kg1 = sb("raw_kg1", [P, KB, LOWRANK], F32, early)
            raw_v = sb("raw_v", [P, KB, D], F32, early)
            raw_g = sb("raw_g", [P, KB, D], F32, early)
            raw_o = sb("raw_o", [P, KB, D], F32, early)
            raw_1 = sb("raw_1", [P, KB, MB * P], F32, early)
            raw_3 = sb("raw_3", [P, KB, MB * P], F32, early)
            raw_2 = sb("raw_2", [P, MB, D], F32, early)
            spread_f = sb("spread_f", [P, DB, P], F32, early)
        o_sb = s1("o_sb", [P, TT, H, HD])
        o_sq = s1("o_sq", [P, TT, H, HD])
        ogT = [s1(f"ogT{i}", [P, KB, L], F32R) for i in range(2)]
        x1 = s1("x1", [P, TT, D])
        zn2 = s1("zn2", [P, TT, D])
        act1 = s1("act1", [P, L])
        prod = s1("prod", [P, L])
        hT = [[s1(f"hT{j}{i}", [P, L], F32R) for i in range(2)] for j in range(2)]
        x2 = s1("x2", [P, TT, D])
        x3 = s1("x3", [P, TT, D])
        x3T = s1("x3T", [P, KB, L])
        one.close()

        raw_e1 = sb("raw_e1", [P, KB, F])
        raw_e2 = sb("raw_e2", [P, FB, D])
        ew1 = [[sb(f"ew1_{s}{i}", [P, KB, F], F32R) for i in range(2)] for s in range(2)]
        ew2 = [[sb(f"ew2_{s}{i}", [P, FB, D], F32R) for i in range(2)] for s in range(2)]
        table_all = sb("table_all", [P, E * COLS, 4], I32)
        table = sb("table", [P, E * COLS, 4], I32)
        row_in = sb("row_in", [P, 1], I32)
        row_out = sb("row_out", [P, 1], I32)
        landing = sb("landing", [P, D])
        xt = sb("xt", [P, D])
        xT = [sb(f"xT{i}", [P, KB, P], F32R) for i in range(2)]
        hid = sb("hid", [P, FB, P])
        hidT = [sb(f"hidT{i}", [P, FB, P], F32R) for i in range(2)]
        y_sum = sb("y_sum", [P, D])
        y_out = sb("y_out", [P, D])

        ld_x = sem("ld_x")
        ld_vec = sem("ld_vec")
        ld_small = sem("ld_small")
        ld_qk = sem("ld_qk")
        ld_v = sem("ld_v")
        ld_g = sem("ld_g")
        ld_o = sem("ld_o")
        ld_w1 = sem("ld_w1")
        ld_w3 = sem("ld_w3")
        ld_w2 = sem("ld_w2")
        ones_set = sem("ones_set")
        dve_set = sem("dve_set")
        pads_set = sem("pads_set")
        const_ready = sem("const_ready")
        spread_ready = sem("spread_ready")
        vecT_ps = sem("vecT_ps")
        vec_ready = sem("vec_ready")
        split_a = sem("split_a")
        split_raw = sem("split_raw")
        w_attn = sem("w_attn")
        w_mlp = sem("w_mlp")
        w_mlp_raw = sem("w_mlp_raw")
        ln_stat = sem("ln_stat")
        ln_var = sem("ln_var")
        ln_ms = sem("ln_ms")
        ln_rstd = sem("ln_rstd")
        ln_rms = sem("ln_rms")
        y_ready = sem("y_ready")
        zn_ready = sem("zn_ready")
        znT_ps = sem("znT_ps")
        znT_hi = sem("znT_hi")
        znT_lo = sem("znT_lo")
        kg1_ps = sem("kg1_ps")
        kg1_ready = sem("kg1_ready")
        q_ps = sem("q_ps")
        q_ready = sem("q_ready")
        k_ps = sem("k_ps")
        k_ready = sem("k_ready")
        z_ps = sem("z_ps")
        z_abs = sem("z_abs")
        z_min = sem("z_min")
        z_exp = sem("z_exp")
        z_ln = sem("z_ln")
        lsig_ready = sem("lsig_ready")
        decay_ready = sem("decay_ready")
        v_ps = sem("v_ps")
        v_hi = sem("v_hi")
        v_lo = sem("v_lo")
        g_ps = sem("g_ps")
        g_ready = sem("g_ready")
        g_exp = sem("g_exp")
        g_chain = sem("g_chain")
        silu_ready = sem("silu_ready")
        kept = sem("kept")
        vrep_ps = sem("vrep_ps")
        kv_ready = sem("kv_ready")
        state_ready = sem("state_ready")
        qs_ready = sem("qs_ready")
        qs_used = sem("qs_used")
        o_copied = sem("o_copied")
        gn_chain = sem("gn_chain")
        gn_var = sem("gn_var")
        gn_ln = sem("gn_ln")
        gn_rstd = sem("gn_rstd")
        og_ready = sem("og_ready")
        ogT_ps = sem("ogT_ps")
        ogT_hi = sem("ogT_hi")
        ogT_lo = sem("ogT_lo")
        wo_ps = sem("wo_ps")
        x1_ready = sem("x1_ready")
        x1x_ready = sem("x1x_ready")
        x1_squares = sem("x1_squares")
        rms_ln = sem("rms_ln")
        rms_ready = sem("rms_ready")
        zn2_ready = sem("zn2_ready")
        zn2T_ps = sem("zn2T_ps")
        zn2T_hi = sem("zn2T_hi")
        zn2T_lo = sem("zn2T_lo")
        h1_ps = sem("h1_ps")
        h3_ps = sem("h3_ps")
        act1_ready = sem("act1_ready")
        prod_ready = sem("prod_ready")
        hT_hi = sem("hT_hi")
        hT_lo = sem("hT_lo")
        hT_used = sem("hT_used")
        x2_ready = sem("x2_ready")
        x2_stored = sem("x2_stored")
        ln2_stat = sem("ln2_stat")
        ln2_var = sem("ln2_var")
        ln2_ln = sem("ln2_ln")
        ln2_rstd = sem("ln2_rstd")
        x3_ready = sem("x3_ready")
        x3_stored = sem("x3_stored")
        x3T_ps = sem("x3T_ps")
        x3T_ready = sem("x3T_ready")
        gate_ps = sem("gate_ps")
        route_chain = sem("route_chain")
        score_diff = sem("score_diff")
        score_exp = sem("score_exp")
        mask_ready = sem("mask_ready")
        slot_ps = sem("slot_ps")
        record_ready = sem("record_ready")
        filled = sem("filled")
        recorded = sem("recorded")
        count_ps = sem("count_ps")
        bounds_ready = sem("bounds_ready")
        bounds_chain = sem("bounds_chain")
        w_mlp_hi = sem("w_mlp_hi")
        ld_e1 = sem("ld_e1")
        ld_e2 = sem("ld_e2")
        ld_table = sem("ld_table")
        packed = sem("packed")
        high_made = sem("high_made")
        ew1_split = sem("ew1_split")
        ew2_split = sem("ew2_split")
        row_in_ready = sem("row_in_ready")
        gathered = sem("gathered")
        xt_ready = sem("xt_ready")
        xT_ps = sem("xT_ps")
        xT_hi = sem("xT_hi")
        xT_lo = sem("xT_lo")
        fc1_ps = sem("fc1_ps")
        gelu_done = sem("gelu_done")
        hid_hi = sem("hid_hi")
        hid_lo = sem("hid_lo")
        fc2_ps = sem("fc2_ps")
        y_summed = sem("y_summed")
        y_weighed = sem("y_weighed")
        y_free = sem("y_free")
        row_out_ready = sem("row_out_ready")
        added = sem("added")

        passed = {e: sem(f"passed_{n}") for e, n in [
            (nc.sync.engine, "sp"), (nc.gpsimd.engine, "pool"), (nc.vector.engine, "dve"),
            (nc.scalar.engine, "act"), (nc.tensor.engine, "pe")]}

        def product(dst, a, b, start, stop, **kw):
            nc.tensor.matmul(dst, a[0], b[0], start=start, stop=False, **kw)
            nc.tensor.matmul(dst, a[0], b[1], start=False, stop=False, **kw)
            return nc.tensor.matmul(dst, a[1], b[0], start=False, stop=stop, **kw)

        def late(eng, s, v):
            if not (isinstance(v, int) and v <= 0):
                settled(eng, s, v)

        def settled(eng, s, v):
            eng.wait_ge(s, v)
            if not isinstance(v, int):
                eng.sem_inc(passed[eng.engine], 1)

        def first_tile(eng, e, less=0):
            if e == 0:
                return 0 - less
            most = 2 * T // P + MIN_TILES * E
            return eng.value_load(bounds[0:1, less, e:e + 1], min_val=MIN_TILES - less, max_val=most)

        block = ctx.enter_context(nc.Block())

        @block.sync
        def _(sp):
            sp.dma_start(xin[:], x_tiles[:, 0:TT, :]).then_inc(ld_x, 16)
            sp.dma_start(raw_qk[:, 0], Wq.rearrange("(k p) n -> p k n", p=P)).then_inc(ld_qk, 16)
            sp.dma_start(raw_qk[:, 1], Wk.rearrange("(k p) n -> p k n", p=P)).then_inc(ld_qk, 16)
            sp.dma_start(raw_kg1[:], Wkg1.rearrange("(k p) n -> p k n", p=P)).then_inc(ld_qk, 16)
            sp.dma_start(raw_v[:], Wv.rearrange("(k p) n -> p k n", p=P)).then_inc(ld_v, 16)
            nb = E * FB
            sp.dma_start(vec_rows[0:nb, :], fc1_b.rearrange("e (f p) -> (e f) p", p=P)).then_inc(ld_vec, 16)
            sp.dma_start(vec_rows[nb:nb + KB, :], ln1_w.rearrange("(k p) -> k p", p=P)).then_inc(ld_vec, 16)
            sp.dma_start(vec_rows[nb + KB:nb + 2 * KB, :], ln2_w.rearrange("(k p) -> k p", p=P)).then_inc(ld_vec, 16)
            sp.dma_start(vec_rows[nb + 2 * KB:NV, :], bkg2.rearrange("(k p) -> k p", p=P)).then_inc(ld_vec, 16)
            sp.dma_start(wkg2[:], Wkg2).then_inc(ld_small, 16)
            sp.dma_start(bg_bc[:], bg.partition_broadcast(P)).then_inc(ld_small, 16)
            sp.dma_start(gb_bc[:], gate_b.partition_broadcast(P)).then_inc(ld_small, 16)
            sp.dma_start(al_bc[:], alpha.partition_broadcast(P)).then_inc(ld_small, 16)
            sp.dma_start(gate_sb[:], gate_w.rearrange("(k p) n -> p k n", p=P)).then_inc(ld_small, 16)
            sp.dma_start(raw_g[:], Wg.rearrange("(k p) n -> p k n", p=P)).then_inc(ld_g, 16)
            sp.dma_start(raw_o[:], Wo.rearrange("(k p) n -> p k n", p=P)).then_inc(ld_o, 16)
            sp.dma_start(raw_1[:, :, 0:MLP], W1.rearrange("(k p) n -> p k n", p=P)).then_inc(ld_w1, 16)
            sp.dma_start(raw_3[:, :, 0:MLP], W3.rearrange("(k p) n -> p k n", p=P)).then_inc(ld_w3, 16)
            sp.dma_start(raw_2[:, 0:MB - 1, :],
                         W2[0:(MB - 1) * P, :].rearrange("(k p) n -> p k n", p=P)).then_inc(ld_w2, 16)
            sp.dma_start(raw_2[0:MLAST, MB - 1, :], W2[(MB - 1) * P:MLP, :]).then_inc(ld_w2, 16)
            sp.dma_start(b2_bc[:], fc2_b.partition_broadcast(P)).then_inc(ld_small, 16)
            sp.wait_ge(pads_set, 4)
            sp.dma_start(table_view, fill[:]).then_inc(filled, 16)

            def store(b):
                settled(sp, x2_ready, 2 * (b + 1))
                sp.dma_start(out_tiles[:, bass.ds(TT * b, TT), :], x2[:]).then_inc(x2_stored, 16)
                settled(sp, x3_ready, TT * (b + 1))
                sp.dma_start(normed_tiles[:, bass.ds(TT * b, TT), :], x3[:]).then_inc(x3_stored, 16)

            def load(b):
                settled(sp, kept, 2 * b)
                settled(sp, zn_ready, TT * b)
                sp.dma_start(xin[:], x_tiles[:, bass.ds(TT * b, TT), :]).then_inc(ld_x, 16)

            load(1)
            with sp.Fori(0, B - 2) as b:
                store(b)
                load(b + 2)
            store(B - 2)
            store(B - 1)

            for e in range(E):
                if e == 0:
                    sp.wait_ge(qs_used, HD * B)
                else:
                    sp.wait_ge(ew1_split, e)
                sp.dma_start(raw_e1[:], fc1_w[e].rearrange("(k p) n -> p k n", p=P)).then_inc(ld_e1, 16)
                if e > 0:
                    sp.wait_ge(ew2_split, e)
                sp.dma_start(raw_e2[:], fc2_w[e].rearrange("(k p) n -> p k n", p=P)).then_inc(ld_e2, 16)
                if e == 0:
                    sp.wait_ge(recorded, 16 * 2 * TT * B)
                    sp.dma_start(table_all[:], table_view).then_inc(ld_table, 16)

        @block.gpsimd
        def _(pool):
            nc.gpsimd.memset(spread_f[:], 1.0).then_inc(ones_set, 1)
            nc.gpsimd.memset(ident[:], 0.0).then_inc(ones_set, 1)
            nc.gpsimd.memset(gather_k[:], 1.0).then_inc(ones_set, 1)
            nc.gpsimd.memset(ones_bf[:], 1.0).then_inc(ones_set, 1)
            nc.gpsimd.memset(earlier[:], 1.0).then_inc(ones_set, 1)
            nc.gpsimd.memset(raw_1[:, :, MLP:MB * P], 0.0).then_inc(pads_set, 1)
            nc.gpsimd.memset(raw_3[:, :, MLP:MB * P], 0.0).then_inc(pads_set, 1)
            pool.wait_ge(ones_set, 5)
            nc.gpsimd.affine_select(out=ident[:], in_=ident[:], compare_op=ALU.not_equal, fill=1.0, base=0,
                                    pattern=[[-1, P]], channel_multiplier=1).then_inc(const_ready, 1)
            nc.gpsimd.affine_select(out=spread_f[:].rearrange("p j (h k) -> p j h k", k=KD),
                                    in_=spread_f[:].rearrange("p j (h k) -> p j h k", k=KD),
                                    compare_op=ALU.is_equal, fill=0.0, base=0,
                                    pattern=[[-H, DB], [-1, H], [0, KD]], channel_multiplier=1).then_inc(const_ready, 1)
            nc.gpsimd.affine_select(out=gather_k[:], in_=gather_k[:], compare_op=ALU.is_ge, fill=0.0, base=0,
                                    pattern=[[-KD, H]], channel_multiplier=1).then_inc(const_ready, 1)
            pool.wait_ge(const_ready, 3)
            nc.gpsimd.affine_select(out=gather_k[:], in_=gather_k[:], compare_op=ALU.is_ge, fill=0.0, base=KD - 1,
                                    pattern=[[KD, H]], channel_multiplier=-1).then_inc(const_ready, 1)
            nc.gpsimd.affine_select(out=earlier[:], in_=earlier[:], compare_op=ALU.is_gt, fill=0.0, base=0,
                                    pattern=[[1, P]], channel_multiplier=-1).then_inc(const_ready, 1)
            nc.gpsimd.iota(eight[:], pattern=[[1, E]], base=0, channel_multiplier=0,
                           allow_small_or_imprecise_dtypes=True).then_inc(const_ready, 1)
            nc.gpsimd.iota(steps128[:], pattern=[[P, T // P]], base=0, channel_multiplier=0,
                           allow_small_or_imprecise_dtypes=True).then_inc(const_ready, 1)
            nc.gpsimd.iota(first_slot[:], pattern=[[COLS, E]], base=0, channel_multiplier=0,
                           allow_small_or_imprecise_dtypes=True).then_inc(const_ready, 1)
            nc.gpsimd.iota(token_id[:], pattern=[[P, T // P]], base=0, channel_multiplier=1).then_inc(const_ready, 1)
            nc.gpsimd.memset(record[:], 0).then_inc(const_ready, 1)
            nc.gpsimd.memset(fill[:], 0).then_inc(pads_set, 1)
            pool.wait_ge(pads_set, 3)
            nc.gpsimd.memset(fill[:, :, 1:2], NOWHERE).then_inc(pads_set, 1)

            def keep(b):
                settled(pool, y_ready, TT * (b + 1))
                late(pool, x1_ready, 2 * b)
                nc.gpsimd.tensor_copy(y_keep[:], y[:]).then_inc(kept, 1)
                late(pool, x1x_ready, b)
                nc.gpsimd.tensor_copy(x_keep[:], xin[:]).then_inc(kept, 1)

            def query(b, d):
                settled(pool, state_ready, HD * b + d + 1)
                if d == 0:
                    settled(pool, q_ready, b + 1)
                late(pool, qs_used, HD * b + d - 1)
                nc.gpsimd.tensor_tensor(qs[d % 2][:], state[d % 2][:], q_sb[:], ALU.mult).then_inc(qs_ready, 1)

            def write_records(b):
                settled(pool, record_ready, b + 1)
                pool.wait_ge(filled, 16)
                for k in range(2):
                    for t in range(TT):
                        nc.gpsimd.indirect_dma_start(
                            out=table_dram, out_offset=bass.IndirectOffsetOnAxis(ap=where[:, k, t:t + 1], axis=0),
                            in_=record[:, k, t, :], in_offset=None).then_inc(recorded, 16)

            def residual(b):
                settled(pool, x1_ready, 2 * (b + 1))
                settled(pool, kept, 2 * (b + 1))
                late(pool, x2_ready, 2 * b)
                nc.gpsimd.tensor_tensor(x1x[:], x1[:], x_keep[:], ALU.add).then_inc(x1x_ready, 1)

            keep(0)
            for d in range(HD):
                query(0, d)
            with pool.Fori(0, B - 1) as b:
                residual(b)
                keep(b + 1)
                for d in range(HD):
                    query(b + 1, d)
                write_records(b)
            residual(B - 1)
            write_records(B - 1)

            def split(raw, loaded, w, done, e):
                pool.wait_ge(loaded, 16 * (e + 1))
                nc.gpsimd.tensor_copy(w[e % 2][0][:], raw[:]).then_inc(high_made, 1)
                high.append(0)
                pool.wait_ge(high_made, len(high))
                nc.gpsimd.tensor_tensor(w[e % 2][1][:], raw[:], w[e % 2][0][:].bitcast(F32),
                                        ALU.subtract).then_inc(done, 1)

            def fetch(i):
                nc.gpsimd.tensor_copy(row_in[:], table[:, bass.ds(i, 1), 0]).then_inc(row_in_ready, 1)
                settled(pool, row_in_ready, i + 1)
                nc.gpsimd.indirect_dma_start(
                    out=landing[:], out_offset=None, in_=normed_dram,
                    in_offset=bass.IndirectOffsetOnAxis(ap=row_in[:], axis=0)).then_inc(gathered, 16)

            def hand_over(i, first=False):
                settled(pool, gathered, 16 * (i + 1))
                if not first:
                    settled(pool, xT_ps, i)
                nc.gpsimd.tensor_copy(xt[:], landing[:]).then_inc(xt_ready, 1)
                settled(pool, xt_ready, i + 1)
                fetch(i + 1)

            def add_rows(j):
                settled(pool, y_weighed, j + 2)
                nc.gpsimd.tensor_copy(row_out[:], table[:, bass.ds(j, 1), 1]).then_inc(row_out_ready, 1)
                settled(pool, row_out_ready, j + 1)
                nc.gpsimd.indirect_dma_start(
                    out=out_rows, out_offset=bass.IndirectOffsetOnAxis(ap=row_out[:], axis=0), in_=y_out[:],
                    in_offset=None, bounds_check=T - 1, oob_is_err=False, compute_op=ALU.add).then_inc(added, 16)
                settled(pool, added, 16 * (j + 1))
                pool.sem_inc(y_free, 1)

            high = []
            pool.wait_ge(bounds_ready, 3)
            split(raw_e1, ld_e1, ew1, ew1_split, 0)
            split(raw_e2, ld_e2, ew2, ew2_split, 0)
            pool.wait_ge(x3_stored, 16 * B)
            pool.wait_ge(x2_stored, 16 * B)
            pool.wait_ge(packed, E)
            pool.sem_inc(y_free, 1)
            fetch(0)
            for e in range(E):
                back = first_tile(pool, e, less=2)
                for k in range(2):
                    hand_over(back + k + 2, first=e == 0 and k == 0)
                    if e > 0:
                        add_rows(back + k)
                if e + 1 < E:
                    split(raw_e1, ld_e1, ew1, ew1_split, e + 1)
                with pool.Fori(first_tile(pool, e), first_tile(pool, e + 1, less=2)) as i:
                    hand_over(i + 2)
                    add_rows(i)
                if e + 1 < E:
                    split(raw_e2, ld_e2, ew2, ew2_split, e + 1)
            back = first_tile(pool, E, less=2)
            hand_over(back + 2)
            add_rows(back)
            add_rows(back + 1)
            settled(pool, gathered, 16 * (back + 4))

        @block.tensor
        def _(pe):
            pe.wait_ge(ld_vec, 64)
            pe.wait_ge(const_ready, 9)
            nc.tensor.transpose(up_ps[0][:, 0:NV], vec_rows[:], ident[0:NV, 0:NV]).then_inc(vecT_ps, 1)

            def attn_in(b):
                pe.wait_ge(zn_ready, TT * (b + 1))
                for kb in range(KB):
                    late(pe, kv_ready, HD * b)
                    for t in range(TT):
                        last = nc.tensor.transpose(ring[kb][:, t * P:(t + 1) * P], zn[:, t, kb * P:(kb + 1) * P], ident[:])
                    last.then_inc(znT_ps, 1)
                pe.wait_ge(znT_lo, KB * (b + 1))
                if isinstance(b, int) and b == 0:
                    pe.wait_ge(w_attn, 2)
                for kb in range(KB):
                    last = product(ring[0][:], [w[:, kb].rearrange("p r c -> p (r c)") for w in wkg1],
                                   [z[:, kb, :] for z in znT], kb == 0, kb == KB - 1)
                last.then_inc(kg1_ps, 1)
                for kb in range(KB):
                    last = product(ring[1][:], [w[:, 0, kb, :] for w in wqk], [z[:, kb, :] for z in znT],
                                   kb == 0, kb == KB - 1)
                last.then_inc(q_ps, 1)
                pe.wait_ge(kg1_ready, b + 1)
                pe.wait_ge(ld_small, 16 * 6)
                nc.tensor.matmul(ring[0][:], wkg2[:], kg1_sb[:], start=True, stop=True).then_inc(z_ps, 1)
                pe.wait_ge(q_ready, b + 1)
                for kb in range(KB):
                    last = product(ring[1][:], [w[:, 1, kb, :] for w in wqk], [z[:, kb, :] for z in znT],
                                   kb == 0, kb == KB - 1)
                last.then_inc(k_ps, 1)
                for m in range(2):
                    if m == 0:
                        pe.wait_ge(z_min, b + 1)
                        if isinstance(b, int) and b == 0:
                            pe.wait_ge(w_attn, 3)
                    else:
                        pe.wait_ge(k_ready, b + 1)
                    for kb in range(KB):
                        last = product(ring[m][:],
                                       [w[:, kb, m * DB:(m + 1) * DB, :].rearrange("p d h -> p (d h)") for w in wv],
                                       [z[:, kb, :] for z in znT], kb == 0, kb == KB - 1)
                    last.then_inc(v_ps, 1)
                for m in range(2):
                    pe.wait_ge(v_lo, 2 * b + m + 1)
                    if m == 0 and isinstance(b, int) and b == 0:
                        pe.wait_ge(w_attn, 4)
                    for t in range(2 * m, 2 * m + 2):
                        for kb in range(KB):
                            last = product(ring[m][:, (t % 2) * D:(t % 2 + 1) * D],
                                           [z[:, kb, t * P:(t + 1) * P] for z in znT],
                                           [w[:, kb, :] for w in wg], kb == 0, kb == KB - 1)
                    last.then_inc(g_ps, 1)

            def spread_v(b, d):
                if d < 2:
                    pe.wait_ge(g_ready, 2 * b + d + 1)
                else:
                    pe.wait_ge(kv_ready, HD * b + d - 1)
                if d == 0 and isinstance(b, int) and b == 0:
                    pe.wait_ge(spread_ready, 1)
                m, j = divmod(d, DB)
                nc.tensor.matmul(ring[d % 2][:], spread[:, j, :], vT[0][:, m, :], start=True, stop=False)
                nc.tensor.matmul(ring[d % 2][:], spread[:, j, :], vT[1][:, m, :],
                                 start=False, stop=True).then_inc(vrep_ps, 1)

            def sum_keys(b, d):
                pe.wait_ge(qs_ready, HD * b + d + 1)
                if d == 0:
                    late(pe, o_copied, 2 * b)
                for t in range(TT):
                    last = nc.tensor.matmul(mix_ps[:, t, d * H:(d + 1) * H], qs[d % 2][:, t * P:(t + 1) * P],
                                            gather_k[:], start=True, stop=True)
                last.then_inc(qs_used, 1)

            def out_proj(b):
                pe.wait_ge(og_ready, b + 1)
                for kb in range(KB):
                    if kb == 0:
                        late(pe, record_ready, b)
                    for t in range(TT):
                        last = nc.tensor.transpose(
                            up_ps[kb][:, t * P:(t + 1) * P],
                            o_sb[:, t].rearrange("p h d -> p (h d)")[:, kb * P:(kb + 1) * P], ident[:])
                    last.then_inc(ogT_ps, 1)
                pe.wait_ge(ogT_lo, KB * (b + 1))
                late(pe, x2_ready, 2 * b)
                for t in range(TT):
                    for kb in range(KB):
                        last = product(res_ps[:, t, :], [z[:, kb, t * P:(t + 1) * P] for z in ogT],
                                       [w[:, kb, :] for w in wo], kb == 0, kb == KB - 1)
                    last.then_inc(wo_ps, 1)

            def mlp_in(b):
                pe.wait_ge(zn2_ready, TT * (b + 1))
                for kb in range(KB):
                    for t in range(TT):
                        last = nc.tensor.transpose(up_ps[kb][:, t * P:(t + 1) * P], zn2[:, t, kb * P:(kb + 1) * P], ident[:])
                    last.then_inc(zn2T_ps, 1)
                pe.wait_ge(zn2T_lo, KB * (b + 1))

            def mlp_up(b, f):
                if f > 0:
                    pe.wait_ge(act1_ready, MB * b + f)
                for kb in range(KB):
                    last = product(up_ps[0][:], [w[:, kb, f * P:(f + 1) * P] for w in w1], [z[:, kb, :] for z in ogT],
                                   kb == 0, kb == KB - 1)
                last.then_inc(h1_ps, 1)

            def mlp_gate(b, f):
                if f > 0:
                    pe.wait_ge(prod_ready, MB * b + f)
                for kb in range(KB):
                    last = product(up_ps[1][:], [w[:, kb, f * P:(f + 1) * P] for w in w3], [z[:, kb, :] for z in ogT],
                                   kb == 0, kb == KB - 1)
                last.then_inc(h3_ps, 1)

            def mlp_down(b, f):
                pe.wait_ge(hT_lo, MB * b + f + 1)
                if f == 0:
                    pe.wait_ge(x1_ready, 2 * (b + 1))
                K = P if f < MB - 1 else MLAST
                for t in range(TT):
                    last = product(res_ps[:, t, :], [z[0:K, t * P:(t + 1) * P] for z in hT[f % 2]],
                                   [w[0:K, f, :] for w in w2], f == 0 and t % 2 == 0, f == MB - 1,
                                   skip_group_check=True)
                last.then_inc(hT_used, 1)

            def route(b):
                pe.wait_ge(x3_ready, TT * (b + 1))
                pe.wait_ge(prod_ready, MB * (b + 1))
                for kb in range(KB):
                    for t in range(TT):
                        last = nc.tensor.transpose(up_ps[kb][:, t * P:(t + 1) * P], x3[:, t, kb * P:(kb + 1) * P], ident[:])
                    last.then_inc(x3T_ps, 1)
                pe.wait_ge(x3T_ready, KB * (b + 1))
                for t in range(TT):
                    for kb in range(KB):
                        last = nc.tensor.matmul(up_ps[0][:, t * E:(t + 1) * E], x3T[:, kb, t * P:(t + 1) * P],
                                                gate_sb[:, kb, :], start=kb == 0, stop=kb == KB - 1)
                last.then_inc(gate_ps, 1)
                pe.wait_ge(mask_ready, 2 * b + 1)
                for t in range(TT):
                    dst = up_ps[1][:, t * E:(t + 1) * E]
                    nc.tensor.matmul(dst, earlier[:], mask[:, t, :], start=True, stop=False)
                    for t2 in range(t):
                        nc.tensor.matmul(dst, ones_bf[:], mask[:, t2, :], start=False, stop=False)
                    last = nc.tensor.matmul(dst, ones_bf[:], taken_bf[:], start=False, stop=True)
                last.then_inc(slot_ps, 1)

            attn_in(0)
            for d in range(HD):
                spread_v(0, d)
                if d >= 1:
                    sum_keys(0, d - 1)
            sum_keys(0, HD - 1)

            def ffn_step(b, d):
                f = d // 2
                if f < MB:
                    if d % 2 == 0:
                        mlp_up(b, f)
                    else:
                        mlp_gate(b, f)
                        if f >= 1:
                            mlp_down(b, f - 1)
                elif d == 2 * MB:
                    mlp_down(b, MB - 1)

            pe.wait_ge(w_mlp, 4)
            with pe.Fori(0, B - 1) as b:
                attn_in(b + 1)
                out_proj(b)
                mlp_in(b)
                for d in range(HD):
                    spread_v(b + 1, d)
                    if d >= 1:
                        sum_keys(b + 1, d - 1)
                    ffn_step(b, d)
                sum_keys(b + 1, HD - 1)
                route(b)
            out_proj(B - 1)
            mlp_in(B - 1)
            for d in range(HD):
                ffn_step(B - 1, d)
            route(B - 1)
            pe.wait_ge(mask_ready, 2 * B)
            pe.wait_ge(record_ready, B)
            nc.tensor.matmul(up_ps[1][:, 0:E], ones_bf[:], taken_bf[:], start=True, stop=True).then_inc(count_ps, 1)

            def turn(i, first=False):
                pe.wait_ge(xt_ready, i + 1)
                if not first:
                    pe.wait_ge(xT_lo, i)
                for kb in range(KB):
                    last = nc.tensor.transpose(ring[0][:, kb * P:(kb + 1) * P], xt[:, kb * P:(kb + 1) * P], ident[:])
                last.then_inc(xT_ps, 1)

            def fc1(before, e):
                pe.wait_ge(xT_lo, before + 2)
                for half in range(2):
                    late(pe, gelu_done, FB * before + FB // 2 * (1 + half))
                    for f in range(FB // 2 * half, FB // 2 * (half + 1)):
                        c = f % (FB // 2) * P
                        for kb in range(KB):
                            last = product(up_ps[half][:, c:c + P], [w[:, kb, f * P:(f + 1) * P] for w in ew1[e % 2]],
                                           [z[:, kb, :] for z in xT], kb == 0, kb == KB - 1)
                    last.then_inc(fc1_ps, 1)

            def fc2(i, e):
                pe.wait_ge(hid_lo, i + 1)
                pe.wait_ge(y_summed, i + 1)
                for f in range(FB):
                    last = product(ring[1][:, 0:D], [z[:, f, :] for z in hidT], [w[:, f, :] for w in ew2[e % 2]],
                                   f == 0, f == FB - 1)
                last.then_inc(fc2_ps, 1)

            pe.wait_ge(packed, E)
            turn(0, first=True)
            for e in range(E):
                before = first_tile(pe, e, less=1)
                pe.wait_ge(ew1_split, e + 1)
                fc1(before, e)
                turn(before + 2)
                if e > 0:
                    fc2(before, e - 1)
                pe.wait_ge(ew2_split, e + 1)
                with pe.Fori(first_tile(pe, e), first_tile(pe, e + 1, less=1)) as i:
                    fc1(i, e)
                    turn(i + 2)
                    fc2(i, e)
            fc2(first_tile(pe, E, less=1), E - 1)

        @block.scalar
        def _(act):
            act.wait_ge(vecT_ps, 1)
            nc.scalar.copy(cols[:], up_ps[0][:, 0:NV]).then_inc(vec_ready, 1)
            act.wait_ge(vec_ready, 1)

            def attn_norm(b):
                act.wait_ge(ln_var, TT * (b + 1))
                nc.scalar.activation(small[:, 0, :], mv[:, :, 1], ACT.Ln, bias=eps[:, 0:1]).then_inc(ln_rstd, 1)
                act.wait_ge(ln_rstd, 3 * b + 1)
                nc.scalar.activation(small[:, 1, :], small[:, 0, :], ACT.Exp, scale=-1.0).then_inc(ln_rstd, 1)
                nc.scalar.activation(small[:, 2, :], small[:, 0, :], ACT.Exp, scale=-0.5).then_inc(ln_rstd, 1)
                act.wait_ge(ln_ms, b + 1)
                nc.scalar.activation(small[:, 4, :], small[:, 3, :], ACT.Ln, bias=eps[:, 0:1]).then_inc(ln_rms, 1)
                act.wait_ge(ln_rms, 2 * b + 1)
                nc.scalar.activation(small[:, 5, :], small[:, 4, :], ACT.Exp, scale=-0.5).then_inc(ln_rms, 1)

            def attn_in(b):
                for kb in range(KB):
                    act.wait_ge(znT_ps, KB * b + kb + 1)
                    nc.scalar.activation(znT[0][:, kb, :], ring[kb][:], ACT.Copy,
                                         scale=cols[:, LN1_C + kb:LN1_C + kb + 1]).then_inc(znT_hi, 1)
                act.wait_ge(kg1_ps, b + 1)
                nc.scalar.copy(kg1_sb[:], ring[0][0:LOWRANK, :]).then_inc(kg1_ready, 1)
                act.wait_ge(q_ps, b + 1)
                late(act, qs_ready, HD * b)
                nc.scalar.copy(q_sb[:], ring[1][:]).then_inc(q_ready, 1)
                act.wait_ge(z_ps, b + 1)
                late(act, lsig_ready, b)
                nc.scalar.activation(soft[:], ring[0][:], ACT.Abs, bias=cols[:, BK_C:BK_C + 1]).then_inc(z_abs, 1)
                act.wait_ge(z_abs, b + 1)
                nc.scalar.activation(soft[:], soft[:], ACT.Exp, scale=-1.0).then_inc(z_exp, 1)
                act.wait_ge(z_exp, b + 1)
                nc.scalar.activation(soft[:], soft[:], ACT.Ln, bias=unit[:, 0:1]).then_inc(z_ln, 1)
                act.wait_ge(k_ps, b + 1)
                late(act, kv_ready, HD * b)
                nc.scalar.mul(k_sb[:], ring[1][:], SCALE).then_inc(k_ready, 1)
                act.wait_ge(lsig_ready, b + 1)
                late(act, state_ready, HD * b)
                nc.scalar.activation(decay[:], lsig[:], ACT.Exp, scale=1.0 / NORMALIZER).then_inc(decay_ready, 1)
                for m in range(2):
                    act.wait_ge(v_ps, 2 * b + m + 1)
                    nc.scalar.copy(vT[0][:, m, :], ring[m][:]).then_inc(v_hi, 1)
                act.wait_ge(g_ready, 2 * (b + 1))
                late(act, silu_ready, b)
                nc.scalar.activation(g_den[:], g_sb[:], ACT.Exp, scale=-1.0).then_inc(g_exp, 1)

            def head_norm(b):
                act.wait_ge(gn_var, b + 1)
                nc.scalar.activation(o_sum[:, 2], o_sum[:, 1], ACT.Ln, scale=1.0 / HD, bias=eps[:, 0:1]).then_inc(gn_ln, 1)
                act.wait_ge(gn_ln, b + 1)
                nc.scalar.activation(o_sum[:, 3], o_sum[:, 2], ACT.Exp, scale=-0.5).then_inc(gn_rstd, 1)

            def out_proj(b):
                for kb in range(KB):
                    act.wait_ge(ogT_ps, KB * b + kb + 1)
                    nc.scalar.copy(ogT[0][:, kb, :], up_ps[kb][:]).then_inc(ogT_hi, 1)
                act.wait_ge(x1_ready, 2 * (b + 1))
                for t in range(TT):
                    nc.scalar.activation(x1_sq[:], x1[:, t, :], ACT.Square,
                                         accum_out=rms[:, 0, t:t + 1]).then_inc(x1_squares, 1)
                    act.wait_ge(x1_squares, TT * b + t + 1)
                nc.scalar.activation(rms[:, 1, :], rms[:, 0, :], ACT.Ln, scale=1.0 / D, bias=eps[:, 0:1]).then_inc(rms_ln, 1)
                act.wait_ge(rms_ln, b + 1)
                nc.scalar.activation(rms[:, 1, :], rms[:, 1, :], ACT.Exp, scale=-0.5).then_inc(rms_ready, 1)
                for kb in range(KB):
                    act.wait_ge(zn2T_ps, KB * b + kb + 1)
                    nc.scalar.activation(ogT[0][:, kb, :], up_ps[kb][:], ACT.Copy,
                                         scale=cols[:, LN2_C + kb:LN2_C + kb + 1]).then_inc(zn2T_hi, 1)

            def mlp(b, f):
                act.wait_ge(h1_ps, MB * b + f + 1)
                if f > 0:
                    act.wait_ge(prod_ready, MB * b + f)
                nc.scalar.activation(act1[:], up_ps[0][:], ACT.Silu).then_inc(act1_ready, 1)
                act.wait_ge(prod_ready, MB * b + f + 1)
                if f >= 2:
                    act.wait_ge(hT_used, MB * b + f - 1)
                nc.scalar.copy(hT[f % 2][0][:], prod[:]).then_inc(hT_hi, 1)

            def route(b):
                act.wait_ge(ln2_var, TT * (b + 1))
                nc.scalar.activation(small2[:, 0, :], mv2[:, :, 1], ACT.Ln, bias=eps[:, 0:1]).then_inc(ln2_ln, 1)
                act.wait_ge(ln2_ln, b + 1)
                nc.scalar.activation(small2[:, 1, :], small2[:, 0, :], ACT.Exp, scale=-0.5).then_inc(ln2_rstd, 1)
                for kb in range(KB):
                    act.wait_ge(x3T_ps, KB * b + kb + 1)
                    nc.scalar.copy(x3T[:, kb, :], up_ps[kb][:]).then_inc(x3T_ready, 1)
                act.wait_ge(score_diff, b + 1)
                nc.scalar.activation(score[:, 1, :], score[:, 0, :], ACT.Exp).then_inc(score_exp, 1)

            attn_norm(0)
            attn_in(0)
            for i, (raw, w, ld, n) in enumerate([(raw_o, wo, ld_o, 16), (raw_1, w1, ld_w1, 16), (raw_3, w3, ld_w3, 16)]):
                act.wait_ge(ld, n)
                if i == 1:
                    act.wait_ge(pads_set, 2)
                nc.scalar.copy(w[0][:], raw[:]).then_inc(w_mlp_hi, 1)
            act.wait_ge(ld_w2, 32)
            nc.scalar.copy(w2[0][:, 0:MB - 1, :], raw_2[:, 0:MB - 1, :])
            nc.scalar.copy(w2[0][0:MLAST, MB - 1, :], raw_2[0:MLAST, MB - 1, :]).then_inc(w_mlp_hi, 1)
            with act.Fori(0, B - 1) as b:
                attn_norm(b + 1)
                head_norm(b)
                attn_in(b + 1)
                out_proj(b)
                for f in range(MB):
                    mlp(b, f)
                route(b)
            head_norm(B - 1)
            out_proj(B - 1)
            for f in range(MB):
                mlp(B - 1, f)
            route(B - 1)

            def x_high(i):
                act.wait_ge(xT_ps, i + 1)
                nc.scalar.copy(xT[0][:], ring[0][:, 0:D].rearrange("p (k t) -> p k t", k=KB)).then_inc(xT_hi, 1)

            def gelu(i, e, first=False):
                for f in range(FB):
                    if f % (FB // 2) == 0:
                        act.wait_ge(fc1_ps, 2 * i + f // (FB // 2) + 1)
                        if not first:
                            act.wait_ge(hid_lo, i)
                    nc.scalar.activation(hid[:, f, :], up_ps[f // (FB // 2)][:, f % (FB // 2) * P:(f % (FB // 2) + 1) * P],
                                         ACT.Gelu, bias=cols[:, B1_C + e * FB + f:B1_C + e * FB + f + 1]).then_inc(gelu_done, 1)

            act.wait_ge(bounds_ready, 3)
            x_high(0)
            for e in range(E):
                start = first_tile(act, e)
                gelu(start, e, first=e == 0)
                x_high(start + 1)
                with act.Fori(start + 1, first_tile(act, e + 1)) as i:
                    gelu(i, e)
                    x_high(i + 1)

        @block.vector
        def _(dve):
            V = nc.vector
            V.memset(eps[:], EPS).then_inc(dve_set, 1)
            V.memset(unit[:], 1.0).then_inc(dve_set, 1)
            V.memset(taken[:], 0.0).then_inc(dve_set, 1)
            V.memset(taken_bf[:], 0.0).then_inc(dve_set, 1)
            raws = 0

            def attn_norm(b):
                dve.wait_ge(ld_x, 16 * (b + 1))
                for t in range(TT):
                    V.bn_stats(stats[:, t, :], xin[:, t, :]).then_inc(ln_stat, 1)
                for t in range(TT):
                    settled(dve, ln_stat, TT * b + t + 1)
                    V.bn_aggr(mv[:, t, :], stats[:, t, :]).then_inc(ln_var, 1)
                dve.wait_ge(ln_rstd, 3 * b + 2)
                V.tensor_tensor(small[:, 3, :], mv[:, :, 1], small[:, 1, :], ALU.mult).then_inc(ln_ms, 1)
                dve.wait_ge(ln_rstd, 3 * b + 3)
                late(dve, kept, 2 * b)
                for t in range(TT):
                    V.tensor_scalar(y[:, t, :], xin[:, t, :], mv[:, t, 0:1], small[:, 2, t:t + 1],
                                    ALU.subtract, ALU.mult).then_inc(y_ready, 1)
                dve.wait_ge(ln_rms, 2 * b + 2)
                late(dve, znT_ps, KB * b)
                for t in range(TT):
                    dve.wait_ge(y_ready, TT * b + t + 1)
                    V.tensor_scalar(zn[:, t, :], y[:, t, :], small[:, 5, t:t + 1], None, ALU.mult).then_inc(zn_ready, 1)

            def attn_split(b):
                for kb in range(KB):
                    dve.wait_ge(znT_hi, KB * b + kb + 1)
                    V.scalar_tensor_tensor(znT[1][:, kb, :], ring[kb][:], cols[:, LN1_C + kb:LN1_C + kb + 1],
                                           znT[0][:, kb, :].bitcast(F32), ALU.mult, ALU.subtract).then_inc(znT_lo, 1)

            def attn_decay(b):
                dve.wait_ge(z_abs, b + 1)
                late(dve, decay_ready, b)
                V.tensor_scalar(lsig[:], ring[0][:], cols[:, BK_C:BK_C + 1], 0.0, ALU.add, ALU.min).then_inc(z_min, 1)
                dve.wait_ge(z_ln, b + 1)
                dve.wait_ge(z_min, b + 1)
                V.tensor_tensor(lsig[:], lsig[:], soft[:], ALU.subtract).then_inc(lsig_ready, 1)
                for m in range(2):
                    dve.wait_ge(v_hi, 2 * b + m + 1)
                    V.tensor_tensor(vT[1][:, m, :], ring[m][:], vT[0][:, m, :].bitcast(F32), ALU.subtract).then_inc(v_lo, 1)

            def attn_gate(b):
                for m in range(2):
                    dve.wait_ge(g_ps, 2 * b + m + 1)
                    V.tensor_tensor(g_sb[:, 2 * m:2 * m + 2, :], ring[m][:].rearrange("p (t d) -> p t d", d=D),
                                    bg_bc[:].unsqueeze(1).broadcast_to([P, 2, D]), ALU.add).then_inc(g_ready, 1)
                dve.wait_ge(g_exp, b + 1)
                V.tensor_scalar(g_den[:], g_den[:], 1.0, None, ALU.add).then_inc(g_chain, 1)
                dve.wait_ge(g_chain, 2 * b + 1)
                V.reciprocal(g_den[:], g_den[:]).then_inc(g_chain, 1)
                dve.wait_ge(g_chain, 2 * b + 2)
                late(dve, og_ready, b)
                V.tensor_tensor(silu_g[:], g_sb[:], g_den[:], ALU.mult).then_inc(silu_ready, 1)

            def scan(b, d):
                n = HD * b + d
                dve.wait_ge(vrep_ps, n + 1)
                if d == 0:
                    dve.wait_ge(k_ready, b + 1)
                    dve.wait_ge(decay_ready, b + 1)
                late(dve, state_ready, n - 1)
                V.tensor_tensor(kv[d % 2][:], ring[d % 2][:], k_sb[:], ALU.mult).then_inc(kv_ready, 1)
                dve.wait_ge(kv_ready, n + 1)
                late(dve, qs_ready, n - 1)
                V.tensor_tensor_scan(state[d % 2][:], decay[:], kv[d % 2][:], 0.0, ALU.mult, ALU.add).then_inc(state_ready, 1)

            def head_norm(b):
                dve.wait_ge(qs_used, HD * (b + 1))
                late(dve, ogT_ps, KB * b)
                for m in range(2):
                    V.tensor_copy(o_sb[:, 2 * m:2 * m + 2].rearrange("p t h d -> p t d h"),
                                  mix_ps[:, 2 * m:2 * m + 2, :].rearrange("p t (d h) -> p t d h", h=H)).then_inc(o_copied, 1)
                dve.wait_ge(o_copied, 2 * (b + 1))
                o3 = o_sb[:].rearrange("p t h d -> p (t h) d")
                sq3 = o_sq[:].rearrange("p t h d -> p (t h) d")
                sm = o_sum[:].rearrange("p c t h -> p c (t h)")

                def over_d(v):
                    return v.unsqueeze(2).broadcast_to([P, TT * H, HD])

                V.tensor_reduce(sm[:, 0], o3, AX.X, ALU.add).then_inc(gn_chain, 1)
                dve.wait_ge(gn_chain, 4 * b + 1)
                V.scalar_tensor_tensor(o3, over_d(sm[:, 0]), -1.0 / HD, o3, ALU.mult, ALU.add).then_inc(gn_chain, 1)
                dve.wait_ge(gn_chain, 4 * b + 2)
                V.tensor_tensor(sq3, o3, o3, ALU.mult).then_inc(gn_chain, 1)
                dve.wait_ge(gn_chain, 4 * b + 3)
                V.tensor_reduce(sm[:, 1], sq3, AX.X, ALU.add).then_inc(gn_var, 1)
                dve.wait_ge(silu_ready, b + 1)
                V.tensor_tensor(o3, o3, silu_g[:].rearrange("p t (h d) -> p (t h) d", d=HD), ALU.mult).then_inc(gn_chain, 1)
                dve.wait_ge(gn_rstd, b + 1)
                dve.wait_ge(gn_chain, 4 * b + 4)
                V.tensor_tensor(o3, o3, over_d(sm[:, 3]), ALU.mult).then_inc(og_ready, 1)

            def out_proj(b):
                for kb in range(KB):
                    dve.wait_ge(ogT_hi, KB * b + kb + 1)
                    V.tensor_tensor(ogT[1][:, kb, :], up_ps[kb][:], ogT[0][:, kb, :].bitcast(F32),
                                    ALU.subtract).then_inc(ogT_lo, 1)
                late(dve, x1x_ready, b)
                for m in range(2):
                    dve.wait_ge(wo_ps, TT * b + 2 * m + 2)
                    if m == 0:
                        dve.wait_ge(kept, 2 * b + 1)
                    V.tensor_tensor(x1[:, 2 * m:2 * m + 2, :], res_ps[:, 2 * m:2 * m + 2, :],
                                    y_keep[:, 2 * m:2 * m + 2, :], ALU.add).then_inc(x1_ready, 1)
                dve.wait_ge(rms_ready, b + 1)
                dve.wait_ge(x1_ready, 2 * (b + 1))
                for t in range(TT):
                    V.tensor_scalar(zn2[:, t, :], x1[:, t, :], rms[:, 1, t:t + 1], None, ALU.mult).then_inc(zn2_ready, 1)
                for kb in range(KB):
                    dve.wait_ge(zn2T_hi, KB * b + kb + 1)
                    V.scalar_tensor_tensor(ogT[1][:, kb, :], up_ps[kb][:], cols[:, LN2_C + kb:LN2_C + kb + 1],
                                           ogT[0][:, kb, :].bitcast(F32), ALU.mult, ALU.subtract).then_inc(zn2T_lo, 1)

            def mlp(b, f):
                dve.wait_ge(act1_ready, MB * b + f + 1)
                dve.wait_ge(h3_ps, MB * b + f + 1)
                late(dve, hT_lo, MB * b + f)
                V.tensor_tensor(prod[:], up_ps[1][:], act1[:], ALU.mult).then_inc(prod_ready, 1)
                dve.wait_ge(hT_hi, MB * b + f + 1)
                V.tensor_tensor(hT[f % 2][1][:], prod[:], hT[f % 2][0][:].bitcast(F32), ALU.subtract).then_inc(hT_lo, 1)

            def residual(b):
                dve.wait_ge(hT_used, MB * (b + 1))
                dve.wait_ge(x1x_ready, b + 1)
                late(dve, x2_stored, 16 * b)
                for m in range(2):
                    V.tensor_tensor(x2[:, 2 * m:2 * m + 2, :], res_ps[:, 2 * m:2 * m + 2, :],
                                    x1x[:, 2 * m:2 * m + 2, :], ALU.add).then_inc(x2_ready, 1)

            RC = 34

            def route(b):
                c = [0]

                def link(ins):
                    c[0] += 1
                    ins.then_inc(route_chain, 1)
                    settled(dve, route_chain, RC * b + c[0])

                dve.wait_ge(x2_ready, 2 * (b + 1))
                for t in range(TT):
                    V.bn_stats(stats2[:, t, :], x2[:, t, :]).then_inc(ln2_stat, 1)
                for t in range(TT):
                    settled(dve, ln2_stat, TT * b + t + 1)
                    V.bn_aggr(mv2[:, t, :], stats2[:, t, :]).then_inc(ln2_var, 1)
                dve.wait_ge(ln2_rstd, b + 1)
                late(dve, x3_stored, 16 * b)
                for t in range(TT):
                    V.tensor_scalar(x3[:, t, :], x2[:, t, :], mv2[:, t, 0:1], small2[:, 1, t:t + 1],
                                    ALU.subtract, ALU.mult).then_inc(x3_ready, 1)
                dve.wait_ge(gate_ps, b + 1)
                link(V.tensor_tensor(logit[:], up_ps[0][:, 0:TT * E].rearrange("p (t e) -> p t e", e=E),
                                     gb_bc[:].unsqueeze(1).broadcast_to([P, TT, E]), ALU.add))
                for t in range(TT):
                    link(V.max(top[:, t, :], logit[:, t, :]))
                for t in range(TT):
                    link(V.max_index(topi[:, t, :], top[:, t, :], logit[:, t, :]))
                V.tensor_tensor(score[:, 0, :], top[:, :, 1], top[:, :, 0], ALU.subtract).then_inc(score_diff, 1)
                link(V.tensor_copy(topf[:], topi[:, :, 0:2]))
                for k in range(2):
                    link(V.tensor_tensor(chosen[:, k], eight[:].unsqueeze(1).broadcast_to([P, TT, E]),
                                         topf[:, :, k:k + 1].broadcast_to([P, TT, E]), ALU.is_equal))
                V.tensor_tensor(mask[:], chosen[:, 0], chosen[:, 1], ALU.add).then_inc(mask_ready, 1)
                dve.wait_ge(score_exp, b + 1)
                link(V.tensor_scalar(score[:, 2, :], score[:, 1, :], 1.0, None, ALU.add))
                link(V.reciprocal(score[:, 2, :], score[:, 2, :]))
                link(V.tensor_tensor(score[:, 3, :], score[:, 1, :], score[:, 2, :], ALU.mult))
                link(V.tensor_tensor(picked[:], chosen[:],
                                     al_bc[:].unsqueeze(1).unsqueeze(1).broadcast_to([P, 2, TT, E]), ALU.mult))
                link(V.tensor_reduce(score[:, 4:6, :], picked[:], AX.X, ALU.add))
                late(dve, recorded, 16 * 2 * TT * b)
                link(V.tensor_tensor(record[:, :, :, 2].bitcast(F32), score[:, 2:4, :], score[:, 4:6, :], ALU.mult))
                for k in range(2):
                    link(V.tensor_copy(record[:, k, :, 0:2],
                                       token_id[:, bass.ds(TT * b, TT)].unsqueeze(2).broadcast_to([P, TT, 2])))
                dve.wait_ge(slot_ps, b + 1)
                before = up_ps[1][:, 0:TT * E].rearrange("p (t e) -> p t e", e=E)
                for k in range(2):
                    link(V.tensor_tensor(picked[:, k], chosen[:, k], before, ALU.mult))
                link(V.tensor_reduce(pos[:, 0], picked[:], AX.X, ALU.add))
                for k in range(2):
                    link(V.tensor_tensor(picked[:, k], chosen[:, k],
                                         first_slot[:].unsqueeze(1).broadcast_to([P, TT, E]), ALU.mult))
                link(V.tensor_reduce(pos[:, 1], picked[:], AX.X, ALU.add))
                link(V.tensor_copy(pos_i[:, 0], pos[:, 0]))
                link(V.tensor_scalar(pos_i[:, 1], pos_i[:, 0], P - 1, None, ALU.bitwise_and))
                link(V.tensor_scalar(pos_i[:, 2], pos_i[:, 0], 7, None, ALU.arith_shift_right))
                link(V.tensor_copy(pos_f[:], pos_i[:, 1:3]))
                link(V.scalar_tensor_tensor(pos[:, 2], pos_f[:, 0], float(E * COLS), pos[:, 1], ALU.mult, ALU.add))
                link(V.tensor_tensor(pos[:, 0], pos[:, 2], pos_f[:, 1], ALU.add))
                V.tensor_copy(where[:], pos[:, 0]).then_inc(record_ready, 1)
                link(V.tensor_reduce(taken_t[:], mask[:].rearrange("p t e -> p e t"), AX.X, ALU.add))
                link(V.tensor_tensor(taken[:], taken[:], taken_t[:], ALU.add))
                V.tensor_copy(taken_bf[:], taken[:]).then_inc(mask_ready, 1)
                assert c[0] == RC, c[0]

            def low_part(w, raw, ready):
                return V.tensor_tensor(w[1][:], raw, w[0][:].bitcast(F32), ALU.subtract).then_inc(ready, 1)

            attn_norm(0)
            dve.wait_ge(ld_qk, 48)
            V.tensor_copy(wqk[0][:], raw_qk[:]).then_inc(split_raw, 1)
            kg1_in = raw_kg1[:].unsqueeze(2).broadcast_to([P, KB, P // LOWRANK, LOWRANK])
            V.tensor_copy(wkg1[0][:], kg1_in).then_inc(split_raw, 1)
            dve.wait_ge(split_raw, 2)
            low_part(wqk, raw_qk[:], w_attn)
            low_part(wkg1, kg1_in, w_attn)
            dve.wait_ge(vec_ready, 1)
            attn_split(0)
            dve.wait_ge(ld_v, 16)
            v_in = raw_v[:].rearrange("p k (h d) -> p k d h", d=HD)
            V.tensor_copy(wv[0][:], v_in).then_inc(split_raw, 1)
            dve.wait_ge(split_raw, 3)
            low_part(wv, v_in, w_attn)
            dve.wait_ge(ld_g, 16)
            V.tensor_copy(wg[0][:], raw_g[:]).then_inc(split_raw, 1)
            dve.wait_ge(split_raw, 4)
            low_part(wg, raw_g[:], w_attn)
            dve.wait_ge(const_ready, 2)
            V.tensor_copy(spread[:], spread_f[:]).then_inc(spread_ready, 1)
            attn_decay(0)
            dve.wait_ge(ld_small, 16 * 6)
            attn_gate(0)
            for d in range(HD):
                scan(0, d)
                if d in (3, 6, 9):
                    i = (3, 6, 9).index(d)
                    dve.wait_ge(w_mlp_hi, i + 1)
                    low_part([wo, w1, w3][i], [raw_o, raw_1, raw_3][i][:], w_mlp)
            dve.wait_ge(w_mlp_hi, 4)
            V.tensor_tensor(w2[1][:, 0:MB - 1, :], raw_2[:, 0:MB - 1, :], w2[0][:, 0:MB - 1, :].bitcast(F32), ALU.subtract)
            V.tensor_tensor(w2[1][0:MLAST, MB - 1, :], raw_2[0:MLAST, MB - 1, :],
                            w2[0][0:MLAST, MB - 1, :].bitcast(F32), ALU.subtract).then_inc(w_mlp, 1)
            dve.wait_ge(const_ready, 10)
            with dve.Fori(0, B - 1) as b:
                attn_norm(b + 1)
                head_norm(b)
                attn_split(b + 1)
                attn_decay(b + 1)
                attn_gate(b + 1)
                out_proj(b)
                for d in range(HD):
                    scan(b + 1, d)
                    if d % 2 == 1 and d // 2 < MB:
                        mlp(b, d // 2)
                residual(b)
                route(b)
            head_norm(B - 1)
            out_proj(B - 1)
            for f in range(MB):
                mlp(B - 1, f)
            residual(B - 1)
            route(B - 1)

            dve.wait_ge(mask_ready, 2 * B)
            V.memset(taken[:], 1.0).then_inc(bounds_chain, 1)
            dve.wait_ge(count_ps, 1)
            V.tensor_tensor(over[:], up_ps[1][:, 0:E].unsqueeze(2).broadcast_to([P, E, T // P]),
                            steps128[:].unsqueeze(1).broadcast_to([P, E, T // P]), ALU.is_gt).then_inc(bounds_chain, 1)
            dve.wait_ge(bounds_chain, 2)
            V.tensor_reduce(tiles_f[:], over[:], AX.X, ALU.add).then_inc(bounds_chain, 1)
            dve.wait_ge(bounds_chain, 3)
            V.tensor_scalar(tiles_f[:], tiles_f[:], float(MIN_TILES), None, ALU.max).then_inc(bounds_chain, 1)
            dve.wait_ge(bounds_chain, 4)
            V.tensor_tensor_scan(cum_f[:], taken[:], tiles_f[:], 0.0, ALU.mult, ALU.add).then_inc(bounds_chain, 1)
            dve.wait_ge(bounds_chain, 5)
            for less in range(3):
                V.tensor_scalar(bounds[:, less, 1:E + 1], cum_f[:], float(-less), None, ALU.add).then_inc(bounds_ready, 1)
            dve.wait_ge(bounds_ready, 3)

            dve.wait_ge(ld_table, 16)
            for e in range(E):
                if e > 0:
                    dve.wait_ge(packed, e)
                V.tensor_copy(table[:, bass.ds(first_tile(dve, e), COLS), :],
                              table_all[:, e * COLS:(e + 1) * COLS, :]).then_inc(packed, 1)
            V.memset(y_sum[:], 0.0).then_inc(y_summed, 1)
            V.memset(y_out[:], 0.0).then_inc(y_weighed, 1)

            def x_low(i):
                dve.wait_ge(xT_hi, i + 1)
                V.tensor_tensor(xT[1][:], ring[0][:, 0:D].rearrange("p (k t) -> p k t", k=KB),
                                xT[0][:].bitcast(F32), ALU.subtract).then_inc(xT_lo, 1)

            def hid_split(i, first=False):
                dve.wait_ge(gelu_done, FB * (i + 1))
                if not first:
                    dve.wait_ge(fc2_ps, i)
                V.tensor_copy(hidT[0][:], hid[:]).then_inc(hid_hi, 1)
                dve.wait_ge(hid_hi, i + 1)
                V.tensor_tensor(hidT[1][:], hid[:], hidT[0][:].bitcast(F32), ALU.subtract).then_inc(hid_lo, 1)

            def weigh(i, e):
                dve.wait_ge(fc2_ps, i + 1)
                dve.wait_ge(y_weighed, i + 1)
                V.tensor_tensor(y_sum[:], ring[1][:, 0:D], b2_bc[:, e, :], ALU.add).then_inc(y_summed, 1)
                dve.wait_ge(y_summed, i + 2)
                dve.wait_ge(y_free, i + 1)
                V.tensor_scalar(y_out[:], y_sum[:], table[:, bass.ds(i, 1), 2].bitcast(F32), None,
                                ALU.mult).then_inc(y_weighed, 1)

            dve.wait_ge(packed, E)
            x_low(0)
            for e in range(E):
                start = first_tile(dve, e)
                x_low(start + 1)
                hid_split(start, first=e == 0)
                if e > 0:
                    weigh(first_tile(dve, e, less=1), e - 1)
                with dve.Fori(start, first_tile(dve, e + 1, less=1)) as i:
                    x_low(i + 2)
                    hid_split(i + 1)
                    weigh(i, e)
            weigh(first_tile(dve, E, less=1), E - 1)


_INS = ['x', 'Wq', 'Wk', 'Wkg1', 'Wkg2', 'bkg2', 'Wv', 'Wg', 'bg', 'Wo', 'ln1_w', 'ln2_w', 'W1', 'W3', 'W2']
_INS = ['L0_attn_' + n for n in _INS]
_INS += ['L0_ffn_' + n for n in ['gate_w', 'gate_b', 'fc1_w', 'fc1_b', 'fc2_w', 'fc2_b', 'alpha']]


def kernel(**inputs):
    import numpy as _np
    import concourse.bacc as _bacc
    from concourse import mybir as _mybir
    from concourse.bass_utils import run_bass_kernel_spmd as _run

    nc = _bacc.Bacc("TRN2", target_bir_lowering=False, num_devices=1)
    arrays, args = {}, []
    for name in _INS:
        a = _np.ascontiguousarray(inputs[name])
        arrays[f"in_{name}_dram"] = a
        args.append(nc.dram_tensor(f"in_{name}_dram", a.shape, _mybir.dt.from_np(a.dtype), kind="ExternalInput").ap())
    shape = arrays["in_L0_attn_x_dram"].shape
    args.append(nc.dram_tensor("out_0_dram", shape, _mybir.dt.float32, kind="ExternalOutput").ap())
    build(nc, *args)
    r = _run(nc, [arrays], core_ids=[0])
    return r.results[0]["out_0_dram"]
```

```python
from contextlib import ExitStack

import concourse.bass as bass
from concourse import mybir

F32 = mybir.dt.float32
F32R = mybir.dt.float32r
BF16 = mybir.dt.bfloat16
I32 = mybir.dt.int32
U32 = mybir.dt.uint32
ALU = mybir.AluOpType
ACT = mybir.ActivationFunctionType
AX = mybir.AxisListType

P = 128
LN_EXP = "natural_log_exp_and_others"


def build(nc, x, Wq, Wk, Wkg1, Wkg2, bkg2, Wv, Wg, bg, Wo, ln1_w, ln2_w, W1, W3, W2,
          gate_w, gate_b, fc1_w, fc1_b, fc2_w, fc2_b, alpha, out):
    B, L, D = x.shape
    HK = Wq.shape[1]
    H = 16
    KD = HK // H
    HD = D // H
    MLP = W1.shape[1]
    E, _, F = fc1_w.shape
    T = B * L
    TT = L // P
    KB = D // P
    MB = -(-MLP // P)
    MLAST = MLP - (MB - 1) * P
    FB = F // P
    DB = P // H
    LOWRANK = Wkg1.shape[1]
    SCALE = float(HD) ** -0.5
    EPS = 1e-5
    NORMALIZER = 16.0
    MIN_TILES = 1
    PAIR = 2
    TILE = PAIR * P
    NV = E * FB + 2 * KB + 1
    COLS = T // P + 4 * PAIR
    NOWHERE = 1 << 20

    x_rows = x.rearrange("b l d -> (b l) d")
    out_rows = out.rearrange("b l d -> (b l) d")
    x_tiles = x_rows.rearrange("(n p) d -> p n d", p=P)
    out_tiles = out_rows.rearrange("(n p) d -> p n d", p=P)

    normed_dram = nc.dram_tensor("normed_rows", [T, D], F32, kind="Internal").ap()
    normed_tiles = normed_dram.rearrange("(n p) d -> p n d", p=P)
    table_dram = nc.dram_tensor("routing_table", [P * E * COLS, 4], I32, kind="Internal").ap()
    table_view = table_dram.rearrange("(p c) w -> p c w", p=P)

    with ExitStack() as ctx:
        names = set()

        def sb(name, shape, dt=F32, scope=ctx):
            return scope.enter_context(nc.sbuf_tensor(name, shape, dt))

        def psum(name, shape, dt=F32):
            return ctx.enter_context(nc.psum_tensor(name, shape, dt))

        def sem(name):
            return ctx.enter_context(nc.semaphore(name))

        ring = [psum("ring0", [P, L]), psum("ring1", [P, L])]
        mix_ps = psum("mix_ps", [P, TT, D])
        up_ps = [psum("up0_ps", [P, L]), psum("up1_ps", [P, L])]
        res_ps = psum("res_ps", [P, TT, D])

        fc1_out = [up_ps[f // 2][:, f % 2 * TILE:(f % 2 + 1) * TILE] if f < FB // 2 else mix_ps[:, f - FB // 2, :]
                   for f in range(FB)]
        fc2_out = [ring[1][:, 0:D], res_ps[:, 0, :]]

        ident = sb("ident", [P, P])
        cols = sb("cols", [P, E * FB + 2 * KB + 1])
        B1_C, LN1_C, LN2_C, BK_C = 0, E * FB, E * FB + KB, E * FB + 2 * KB
        b2_bc = sb("b2_bc", [P, E, D])
        bounds = sb("bounds", [P, 2, E + 1], I32)
        eps = sb("eps", [P, 1])
        unit = sb("unit", [P, 1])
        one = ExitStack()
        ctx.enter_context(one)

        def s1(name, shape, dt=F32):
            return sb(name, shape, dt, one)

        xin = s1("xin", [P, TT, D])
        y = s1("y", [P, TT, D])
        zn = s1("zn", [P, TT, D])
        znT = [s1(f"znT{i}", [P, KB, L], F32R) for i in range(2)]
        kg1_sb = s1("kg1_sb", [LOWRANK, L])
        soft = s1("soft", [P, L])
        lsig = s1("lsig", [P, L])
        decay = s1("decay", [P, L])
        vT = [s1(f"vT{i}", [P, KB, L], F32R) for i in range(2)]
        kv = [s1(f"kv{i}", [P, L]) for i in range(2)]
        k_sb = s1("k_sb", [P, L])
        g_sb = s1("g_sb", [P, TT, D])
        q_sb = s1("q_sb", [P, L])
        state = [s1(f"state{i}", [P, L]) for i in range(2)]
        qs = [s1(f"qs{i}", [P, L]) for i in range(2)]
        wqk = [s1(f"wqk{i}", [P, 2, KB, HK], F32R) for i in range(2)]
        wkg1 = [s1(f"wkg1{i}", [P, KB, P // LOWRANK, LOWRANK], F32R) for i in range(2)]
        wkg2 = s1("wkg2", [LOWRANK, HK])
        wv = [s1(f"wv{i}", [P, KB, HD, H], F32R) for i in range(2)]
        wg = [s1(f"wg{i}", [P, KB, D], F32R) for i in range(2)]
        spread = s1("spread", [P, DB, P], F32R)
        gather_k = s1("gather_k", [P, H])
        bg_bc = s1("bg_bc", [P, D])
        stats = s1("stats", [P, TT, 6])
        mv = s1("mv", [P, TT, 2])
        small = s1("small", [P, 8, TT])
        wo = [s1(f"wo{i}", [P, KB, D], F32R) for i in range(2)]
        w1 = [s1(f"w1{i}", [P, KB, MB * P], F32R) for i in range(2)]
        w3 = [s1(f"w3{i}", [P, KB, MB * P], F32R) for i in range(2)]
        w2 = [s1(f"w2{i}", [P, MB, D], F32R) for i in range(2)]
        silu_g = s1("silu_g", [P, TT, D])
        y_keep = s1("y_keep", [P, TT, D])
        x_keep = s1("x_keep", [P, TT, D])
        x1x = s1("x1x", [P, TT, D])
        gate_sb = s1("gate_sb", [P, KB, E])
        gb_bc = s1("gb_bc", [P, E])
        al_bc = s1("al_bc", [P, E])
        earlier = s1("earlier", [P, P], BF16)
        ones_bf = s1("ones_bf", [P, P], BF16)
        eight = s1("eight", [P, E])
        token_id = s1("token_id", [P, T // P], I32)
        tile_steps = s1("tile_steps", [P, T // TILE])
        first_slot = s1("first_slot", [P, E])
        o_sum = s1("o_sum", [P, 4, TT, H])
        rms = s1("rms", [P, 2, TT])
        x1_sq = s1("x1_sq", [P, D])
        stats2 = s1("stats2", [P, TT, 6])
        mv2 = s1("mv2", [P, TT, 2])
        small2 = s1("small2", [P, 2, TT])
        logit = s1("logit", [P, TT, E])
        top = s1("top", [P, TT, 8])
        topi = s1("topi", [P, TT, 8], U32)
        topf = s1("topf", [P, TT, 2])
        chosen = s1("chosen", [P, 2, TT, E])
        picked = s1("picked", [P, 2, TT, E])
        mask = s1("mask", [P, TT, E], BF16)
        taken = s1("taken", [P, E])
        taken_t = s1("taken_t", [P, E])
        taken_bf = s1("taken_bf", [P, E], BF16)
        score = s1("score", [P, 6, TT])
        pos = s1("pos", [P, 3, 2, TT])
        pos_i = s1("pos_i", [P, 3, 2, TT], I32)
        pos_f = s1("pos_f", [P, 2, 2, TT])
        where = s1("where", [P, 2, TT], I32)
        record = s1("record", [P, 2, TT, 4], I32)
        fill = s1("fill", [P, E * COLS, 4], I32)
        over = s1("over", [P, E, T // TILE])
        tiles_f = s1("tiles_f", [P, E])
        cum_f = s1("cum_f", [P, E])
        with ExitStack() as early:
            vec_rows = sb("vec_rows", [NV, P], F32, early)
            raw_qk = sb("raw_qk", [P, 2, KB, HK], F32, early)
            raw_kg1 = sb("raw_kg1", [P, KB, LOWRANK], F32, early)
            raw_v = sb("raw_v", [P, KB, D], F32, early)
            raw_g = sb("raw_g", [P, KB, D], F32, early)
            raw_o = sb("raw_o", [P, KB, D], F32, early)
            raw_1 = sb("raw_1", [P, KB, MB * P], F32, early)
            raw_3 = sb("raw_3", [P, KB, MB * P], F32, early)
            raw_2 = sb("raw_2", [P, MB, D], F32, early)
            spread_f = sb("spread_f", [P, DB, P], F32, early)
        o_sb = s1("o_sb", [P, TT, H, HD])
        o_sq = s1("o_sq", [P, TT, H, HD])
        ogT = [s1(f"ogT{i}", [P, KB, L], F32R) for i in range(2)]
        x1 = s1("x1", [P, TT, D])
        zn2 = s1("zn2", [P, TT, D])
        act1 = s1("act1", [P, L])
        prod = s1("prod", [P, L])
        hT = [[s1(f"hT{j}{i}", [P, L], F32R) for i in range(2)] for j in range(2)]
        x2 = s1("x2", [P, TT, D])
        x3 = s1("x3", [P, TT, D])
        x3T = s1("x3T", [P, KB, L])
        one.close()

        raw_e1 = sb("raw_e1", [P, KB, F])
        raw_e2 = sb("raw_e2", [P, FB, D])
        ew1 = [[sb(f"ew1_{s}{i}", [P, KB, F], F32R) for i in range(2)] for s in range(2)]
        ew2 = [[sb(f"ew2_{s}{i}", [P, FB, D], F32R) for i in range(2)] for s in range(2)]
        table_all = sb("table_all", [P, E * COLS, 4], I32)
        table = sb("table", [P, E * COLS, 4], I32)
        row_in = sb("row_in", [P, PAIR], I32)
        row_out = sb("row_out", [P, PAIR], I32)
        landing = sb("landing", [P, PAIR, D])
        xt = sb("xt", [P, PAIR, D])
        xT = [sb(f"xT{i}", [P, KB, TILE], F32R) for i in range(2)]
        hid = sb("hid", [P, FB, TILE])
        hidT = [sb(f"hidT{i}", [P, FB, TILE], F32R) for i in range(2)]
        y_sum = sb("y_sum", [P, PAIR, D])
        y_out = sb("y_out", [P, PAIR, D])

        ld_x = sem("ld_x")
        ld_vec = sem("ld_vec")
        ld_small = sem("ld_small")
        ld_qk = sem("ld_qk")
        ld_v = sem("ld_v")
        ld_g = sem("ld_g")
        ld_o = sem("ld_o")
        ld_w1 = sem("ld_w1")
        ld_w3 = sem("ld_w3")
        ld_w2 = sem("ld_w2")
        ones_set = sem("ones_set")
        dve_set = sem("dve_set")
        pads_set = sem("pads_set")
        const_ready = sem("const_ready")
        spread_ready = sem("spread_ready")
        vecT_ps = sem("vecT_ps")
        vec_ready = sem("vec_ready")
        split_a = sem("split_a")
        split_raw = sem("split_raw")
        w_attn = sem("w_attn")
        w_mlp = sem("w_mlp")
        w_mlp_raw = sem("w_mlp_raw")
        ln_stat = sem("ln_stat")
        ln_var = sem("ln_var")
        ln_ms = sem("ln_ms")
        ln_rstd = sem("ln_rstd")
        ln_rms = sem("ln_rms")
        y_ready = sem("y_ready")
        zn_ready = sem("zn_ready")
        znT_ps = sem("znT_ps")
        znT_hi = sem("znT_hi")
        znT_lo = sem("znT_lo")
        kg1_ps = sem("kg1_ps")
        kg1_ready = sem("kg1_ready")
        q_ps = sem("q_ps")
        q_ready = sem("q_ready")
        k_ps = sem("k_ps")
        k_ready = sem("k_ready")
        z_ps = sem("z_ps")
        z_abs = sem("z_abs")
        z_min = sem("z_min")
        z_exp = sem("z_exp")
        z_ln = sem("z_ln")
        lsig_ready = sem("lsig_ready")
        decay_ready = sem("decay_ready")
        v_ps = sem("v_ps")
        v_hi = sem("v_hi")
        v_lo = sem("v_lo")
        g_ps = sem("g_ps")
        g_ready = sem("g_ready")
        silu_ready = sem("silu_ready")
        kept = sem("kept")
        vrep_ps = sem("vrep_ps")
        kv_ready = sem("kv_ready")
        state_ready = sem("state_ready")
        qs_ready = sem("qs_ready")
        qs_used = sem("qs_used")
        o_copied = sem("o_copied")
        gn_chain = sem("gn_chain")
        gn_var = sem("gn_var")
        gn_ln = sem("gn_ln")
        gn_rstd = sem("gn_rstd")
        og_ready = sem("og_ready")
        ogT_ps = sem("ogT_ps")
        ogT_hi = sem("ogT_hi")
        ogT_lo = sem("ogT_lo")
        wo_ps = sem("wo_ps")
        x1_ready = sem("x1_ready")
        x1x_ready = sem("x1x_ready")
        x1_squares = sem("x1_squares")
        rms_ln = sem("rms_ln")
        rms_ready = sem("rms_ready")
        zn2_ready = sem("zn2_ready")
        zn2T_ps = sem("zn2T_ps")
        zn2T_hi = sem("zn2T_hi")
        zn2T_lo = sem("zn2T_lo")
        h1_ps = sem("h1_ps")
        h3_ps = sem("h3_ps")
        act1_ready = sem("act1_ready")
        prod_ready = sem("prod_ready")
        hT_hi = sem("hT_hi")
        hT_lo = sem("hT_lo")
        hT_used = sem("hT_used")
        x2_ready = sem("x2_ready")
        x2_stored = sem("x2_stored")
        ln2_stat = sem("ln2_stat")
        ln2_var = sem("ln2_var")
        ln2_ln = sem("ln2_ln")
        ln2_rstd = sem("ln2_rstd")
        x3_ready = sem("x3_ready")
        x3_stored = sem("x3_stored")
        x3T_ps = sem("x3T_ps")
        x3T_ready = sem("x3T_ready")
        gate_ps = sem("gate_ps")
        route_chain = sem("route_chain")
        score_diff = sem("score_diff")
        score_exp = sem("score_exp")
        mask_ready = sem("mask_ready")
        slot_ps = sem("slot_ps")
        record_ready = sem("record_ready")
        filled = sem("filled")
        recorded = sem("recorded")
        count_ps = sem("count_ps")
        bounds_ready = sem("bounds_ready")
        bounds_chain = sem("bounds_chain")
        w_mlp_hi = sem("w_mlp_hi")
        ld_e1 = sem("ld_e1")
        ld_e2 = sem("ld_e2")
        ld_table = sem("ld_table")
        packed = sem("packed")
        high_made = sem("high_made")
        ew1_hi = sem("ew1_hi")
        ew2_hi = sem("ew2_hi")
        ew1_split = sem("ew1_split")
        ew2_split = sem("ew2_split")
        row_in_ready = sem("row_in_ready")
        gathered = sem("gathered")
        xt_ready = sem("xt_ready")
        xT_ps = sem("xT_ps")
        xT_hi = sem("xT_hi")
        xT_lo = sem("xT_lo")
        fc1_ps = sem("fc1_ps")
        gelu_done = sem("gelu_done")
        hid_hi = sem("hid_hi")
        hid_lo = sem("hid_lo")
        fc2_ps = sem("fc2_ps")
        y_summed = sem("y_summed")
        y_weighed = sem("y_weighed")
        y_free = sem("y_free")
        row_out_ready = sem("row_out_ready")
        added = sem("added")

        passed = {e: sem(f"passed_{n}") for e, n in [
            (nc.sync.engine, "sp"), (nc.gpsimd.engine, "pool"), (nc.vector.engine, "dve"),
            (nc.scalar.engine, "act"), (nc.tensor.engine, "pe")]}

        def product(dst, a, b, start, stop, **kw):
            nc.tensor.matmul(dst, a[0], b[0], start=start, stop=False, **kw)
            nc.tensor.matmul(dst, a[0], b[1], start=False, stop=False, **kw)
            return nc.tensor.matmul(dst, a[1], b[0], start=False, stop=stop, **kw)

        def late(eng, s, v):
            if not (isinstance(v, int) and v <= 0):
                settled(eng, s, v)

        def settled(eng, s, v):
            eng.wait_ge(s, v)
            if not isinstance(v, int):
                eng.sem_inc(passed[eng.engine], 1)

        def first_tile(eng, e, less=0):
            if e == 0:
                return 0 - less
            most = 2 * T // TILE + MIN_TILES * E
            return eng.value_load(bounds[0:1, less, e:e + 1], min_val=MIN_TILES - less, max_val=most)

        block = ctx.enter_context(nc.Block())

        @block.sync
        def _(sp):
            sp.dma_start(xin[:], x_tiles[:, 0:TT, :]).then_inc(ld_x, 16)
            sp.dma_start(raw_qk[:, 0], Wq.rearrange("(k p) n -> p k n", p=P)).then_inc(ld_qk, 16)
            sp.dma_start(raw_qk[:, 1], Wk.rearrange("(k p) n -> p k n", p=P)).then_inc(ld_qk, 16)
            sp.dma_start(raw_kg1[:], Wkg1.rearrange("(k p) n -> p k n", p=P)).then_inc(ld_qk, 16)
            sp.dma_start(raw_v[:], Wv.rearrange("(k p) n -> p k n", p=P)).then_inc(ld_v, 16)
            nb = E * FB
            sp.dma_start(vec_rows[0:nb, :], fc1_b.rearrange("e (f p) -> (e f) p", p=P)).then_inc(ld_vec, 16)
            sp.dma_start(vec_rows[nb:nb + KB, :], ln1_w.rearrange("(k p) -> k p", p=P)).then_inc(ld_vec, 16)
            sp.dma_start(vec_rows[nb + KB:nb + 2 * KB, :], ln2_w.rearrange("(k p) -> k p", p=P)).then_inc(ld_vec, 16)
            sp.dma_start(vec_rows[nb + 2 * KB:NV, :], bkg2.rearrange("(k p) -> k p", p=P)).then_inc(ld_vec, 16)
            sp.dma_start(wkg2[:], Wkg2).then_inc(ld_small, 16)
            sp.dma_start(bg_bc[:], bg.partition_broadcast(P)).then_inc(ld_small, 16)
            sp.dma_start(gb_bc[:], gate_b.partition_broadcast(P)).then_inc(ld_small, 16)
            sp.dma_start(al_bc[:], alpha.partition_broadcast(P)).then_inc(ld_small, 16)
            sp.dma_start(gate_sb[:], gate_w.rearrange("(k p) n -> p k n", p=P)).then_inc(ld_small, 16)
            sp.dma_start(raw_g[:], Wg.rearrange("(k p) n -> p k n", p=P)).then_inc(ld_g, 16)
            sp.dma_start(raw_o[:], Wo.rearrange("(k p) n -> p k n", p=P)).then_inc(ld_o, 16)
            sp.dma_start(raw_1[:, :, 0:MLP], W1.rearrange("(k p) n -> p k n", p=P)).then_inc(ld_w1, 16)
            sp.dma_start(raw_3[:, :, 0:MLP], W3.rearrange("(k p) n -> p k n", p=P)).then_inc(ld_w3, 16)
            sp.dma_start(raw_2[:, 0:MB - 1, :],
                         W2[0:(MB - 1) * P, :].rearrange("(k p) n -> p k n", p=P)).then_inc(ld_w2, 16)
            sp.dma_start(raw_2[0:MLAST, MB - 1, :], W2[(MB - 1) * P:MLP, :]).then_inc(ld_w2, 16)
            sp.dma_start(b2_bc[:], fc2_b.partition_broadcast(P)).then_inc(ld_small, 16)
            sp.wait_ge(pads_set, 4)
            sp.dma_start(table_view, fill[:]).then_inc(filled, 16)

            def store(b):
                settled(sp, x2_ready, 2 * (b + 1))
                sp.dma_start(out_tiles[:, bass.ds(TT * b, TT), :], x2[:]).then_inc(x2_stored, 16)
                settled(sp, x3_ready, TT * (b + 1))
                sp.dma_start(normed_tiles[:, bass.ds(TT * b, TT), :], x3[:]).then_inc(x3_stored, 16)

            def load(b):
                settled(sp, kept, 2 * b)
                settled(sp, zn_ready, TT * b)
                sp.dma_start(xin[:], x_tiles[:, bass.ds(TT * b, TT), :]).then_inc(ld_x, 16)

            load(1)
            with sp.Fori(0, B - 2) as b:
                store(b)
                load(b + 2)
            store(B - 2)
            store(B - 1)

            for e in range(E):
                if e == 0:
                    sp.wait_ge(qs_used, HD * B)
                else:
                    sp.wait_ge(ew1_split, e)
                sp.dma_start(raw_e1[:], fc1_w[e].rearrange("(k p) n -> p k n", p=P)).then_inc(ld_e1, 16)
                if e > 0:
                    sp.wait_ge(ew2_split, e)
                sp.dma_start(raw_e2[:], fc2_w[e].rearrange("(k p) n -> p k n", p=P)).then_inc(ld_e2, 16)
                if e == 0:
                    sp.wait_ge(recorded, 16 * 2 * TT * B)
                    sp.dma_start(table_all[:], table_view).then_inc(ld_table, 16)

        @block.gpsimd
        def _(pool):
            nc.gpsimd.memset(spread_f[:], 1.0).then_inc(ones_set, 1)
            nc.gpsimd.memset(ident[:], 0.0).then_inc(ones_set, 1)
            nc.gpsimd.memset(gather_k[:], 1.0).then_inc(ones_set, 1)
            nc.gpsimd.memset(ones_bf[:], 1.0).then_inc(ones_set, 1)
            nc.gpsimd.memset(earlier[:], 1.0).then_inc(ones_set, 1)
            nc.gpsimd.memset(raw_1[:, :, MLP:MB * P], 0.0).then_inc(pads_set, 1)
            nc.gpsimd.memset(raw_3[:, :, MLP:MB * P], 0.0).then_inc(pads_set, 1)
            pool.wait_ge(ones_set, 5)
            nc.gpsimd.affine_select(out=ident[:], in_=ident[:], compare_op=ALU.not_equal, fill=1.0, base=0,
                                    pattern=[[-1, P]], channel_multiplier=1).then_inc(const_ready, 1)
            nc.gpsimd.affine_select(out=spread_f[:].rearrange("p j (h k) -> p j h k", k=KD),
                                    in_=spread_f[:].rearrange("p j (h k) -> p j h k", k=KD),
                                    compare_op=ALU.is_equal, fill=0.0, base=0,
                                    pattern=[[-H, DB], [-1, H], [0, KD]], channel_multiplier=1).then_inc(const_ready, 1)
            nc.gpsimd.affine_select(out=gather_k[:], in_=gather_k[:], compare_op=ALU.is_ge, fill=0.0, base=0,
                                    pattern=[[-KD, H]], channel_multiplier=1).then_inc(const_ready, 1)
            pool.wait_ge(const_ready, 3)
            nc.gpsimd.affine_select(out=gather_k[:], in_=gather_k[:], compare_op=ALU.is_ge, fill=0.0, base=KD - 1,
                                    pattern=[[KD, H]], channel_multiplier=-1).then_inc(const_ready, 1)
            nc.gpsimd.affine_select(out=earlier[:], in_=earlier[:], compare_op=ALU.is_gt, fill=0.0, base=0,
                                    pattern=[[1, P]], channel_multiplier=-1).then_inc(const_ready, 1)
            nc.gpsimd.iota(eight[:], pattern=[[1, E]], base=0, channel_multiplier=0,
                           allow_small_or_imprecise_dtypes=True).then_inc(const_ready, 1)
            nc.gpsimd.iota(tile_steps[:], pattern=[[TILE, T // TILE]], base=0, channel_multiplier=0,
                           allow_small_or_imprecise_dtypes=True).then_inc(const_ready, 1)
            nc.gpsimd.iota(first_slot[:], pattern=[[COLS, E]], base=0, channel_multiplier=0,
                           allow_small_or_imprecise_dtypes=True).then_inc(const_ready, 1)
            nc.gpsimd.iota(token_id[:], pattern=[[P, T // P]], base=0, channel_multiplier=1).then_inc(const_ready, 1)
            nc.gpsimd.memset(record[:], 0).then_inc(const_ready, 1)
            nc.gpsimd.memset(fill[:], 0).then_inc(pads_set, 1)
            pool.wait_ge(pads_set, 3)
            nc.gpsimd.memset(fill[:, :, 1:2], NOWHERE).then_inc(pads_set, 1)

            def keep(b):
                settled(pool, y_ready, TT * (b + 1))
                late(pool, x1_ready, 2 * b)
                nc.gpsimd.tensor_copy(y_keep[:], y[:]).then_inc(kept, 1)
                late(pool, x1x_ready, b)
                nc.gpsimd.tensor_copy(x_keep[:], xin[:]).then_inc(kept, 1)

            def query(b, d):
                settled(pool, state_ready, HD * b + d + 1)
                if d == 0:
                    settled(pool, q_ready, b + 1)
                late(pool, qs_used, HD * b + d - 1)
                nc.gpsimd.tensor_tensor(qs[d % 2][:], state[d % 2][:], q_sb[:], ALU.mult).then_inc(qs_ready, 1)

            def write_records(b):
                settled(pool, record_ready, b + 1)
                pool.wait_ge(filled, 16)
                for k in range(2):
                    for t in range(TT):
                        nc.gpsimd.indirect_dma_start(
                            out=table_dram, out_offset=bass.IndirectOffsetOnAxis(ap=where[:, k, t:t + 1], axis=0),
                            in_=record[:, k, t, :], in_offset=None).then_inc(recorded, 16)

            def residual(b):
                settled(pool, x1_ready, 2 * (b + 1))
                settled(pool, kept, 2 * (b + 1))
                late(pool, x2_ready, 2 * b)
                nc.gpsimd.tensor_tensor(x1x[:], x1[:], x_keep[:], ALU.add).then_inc(x1x_ready, 1)

            keep(0)
            for d in range(HD):
                query(0, d)
            with pool.Fori(0, B - 1) as b:
                residual(b)
                keep(b + 1)
                for d in range(HD):
                    query(b + 1, d)
                write_records(b)
            residual(B - 1)
            write_records(B - 1)

            def fetch(i, first=False):
                if not first:
                    settled(pool, xt_ready, i)
                nc.gpsimd.tensor_copy(row_in[:], table[:, bass.ds(PAIR * i, PAIR), 0]).then_inc(row_in_ready, 1)
                settled(pool, row_in_ready, i + 1)
                for h in range(PAIR):
                    nc.gpsimd.indirect_dma_start(
                        out=landing[:, h, :], out_offset=None, in_=normed_dram,
                        in_offset=bass.IndirectOffsetOnAxis(ap=row_in[:, h:h + 1], axis=0)).then_inc(gathered, 16)

            def add_rows(j, h):
                late(pool, added, 16 * (PAIR * j + h))
                if h == 0:
                    pool.sem_inc(y_free, 1)
                    nc.gpsimd.tensor_copy(row_out[:], table[:, bass.ds(PAIR * j, PAIR), 1]).then_inc(row_out_ready, 1)
                    settled(pool, row_out_ready, j + 1)
                settled(pool, y_weighed, PAIR * (j + 1) + h + 1)
                nc.gpsimd.indirect_dma_start(
                    out=out_rows, out_offset=bass.IndirectOffsetOnAxis(ap=row_out[:, h:h + 1], axis=0),
                    in_=y_out[:, h, :], in_offset=None, bounds_check=T - 1, oob_is_err=False,
                    compute_op=ALU.add).then_inc(added, 16)

            for raw, loaded, w, done in ((raw_e1, ld_e1, ew1, ew1_split), (raw_e2, ld_e2, ew2, ew2_split)):
                pool.wait_ge(loaded, 16)
                nc.gpsimd.tensor_copy(w[0][0][:], raw[:]).then_inc(high_made, 1)
                pool.wait_ge(high_made, 1 if w is ew1 else 2)
                nc.gpsimd.tensor_tensor(w[0][1][:], raw[:], w[0][0][:].bitcast(F32), ALU.subtract).then_inc(done, 1)

            pool.wait_ge(x3_stored, 16 * B)
            pool.wait_ge(x2_stored, 16 * B)
            pool.wait_ge(packed, E)
            fetch(0, first=True)
            fetch(1)
            fetch(2)
            fetch(3)
            last = first_tile(pool, E, less=1)
            add_rows(0, 0)
            fetch(4)
            add_rows(0, 1)
            with pool.Fori(1, last) as i:
                add_rows(i, 0)
                fetch(i + 4)
                add_rows(i, 1)
            for h in range(PAIR):
                add_rows(last, h)
            settled(pool, gathered, 16 * PAIR * (last + 4))
            settled(pool, added, 16 * PAIR * (last + 1))

        @block.tensor
        def _(pe):
            pe.wait_ge(ld_vec, 64)
            pe.wait_ge(const_ready, 9)
            nc.tensor.transpose(up_ps[0][:, 0:NV], vec_rows[:], ident[0:NV, 0:NV]).then_inc(vecT_ps, 1)

            def attn_in(b):
                pe.wait_ge(zn_ready, TT * (b + 1))
                for kb in range(KB):
                    late(pe, kv_ready, HD * b)
                    for t in range(TT):
                        last = nc.tensor.transpose(ring[kb][:, t * P:(t + 1) * P], zn[:, t, kb * P:(kb + 1) * P], ident[:])
                    last.then_inc(znT_ps, 1)
                pe.wait_ge(znT_lo, KB * (b + 1))
                if isinstance(b, int) and b == 0:
                    pe.wait_ge(w_attn, 2)
                for kb in range(KB):
                    last = product(ring[0][:], [w[:, kb].rearrange("p r c -> p (r c)") for w in wkg1],
                                   [z[:, kb, :] for z in znT], kb == 0, kb == KB - 1)
                last.then_inc(kg1_ps, 1)
                for kb in range(KB):
                    last = product(ring[1][:], [w[:, 0, kb, :] for w in wqk], [z[:, kb, :] for z in znT],
                                   kb == 0, kb == KB - 1)
                last.then_inc(q_ps, 1)
                pe.wait_ge(kg1_ready, b + 1)
                pe.wait_ge(ld_small, 16 * 6)
                nc.tensor.matmul(ring[0][:], wkg2[:], kg1_sb[:], start=True, stop=True).then_inc(z_ps, 1)
                pe.wait_ge(q_ready, b + 1)
                for kb in range(KB):
                    last = product(ring[1][:], [w[:, 1, kb, :] for w in wqk], [z[:, kb, :] for z in znT],
                                   kb == 0, kb == KB - 1)
                last.then_inc(k_ps, 1)
                for m in range(2):
                    if m == 0:
                        pe.wait_ge(z_min, b + 1)
                        if isinstance(b, int) and b == 0:
                            pe.wait_ge(w_attn, 3)
                    else:
                        pe.wait_ge(k_ready, b + 1)
                    for kb in range(KB):
                        last = product(ring[m][:],
                                       [w[:, kb, m * DB:(m + 1) * DB, :].rearrange("p d h -> p (d h)") for w in wv],
                                       [z[:, kb, :] for z in znT], kb == 0, kb == KB - 1)
                    last.then_inc(v_ps, 1)
                for m in range(2):
                    pe.wait_ge(v_lo, 2 * b + m + 1)
                    if m == 0 and isinstance(b, int) and b == 0:
                        pe.wait_ge(w_attn, 4)
                    for t in range(2 * m, 2 * m + 2):
                        for kb in range(KB):
                            last = product(ring[m][:, (t % 2) * D:(t % 2 + 1) * D],
                                           [z[:, kb, t * P:(t + 1) * P] for z in znT],
                                           [w[:, kb, :] for w in wg], kb == 0, kb == KB - 1)
                    last.then_inc(g_ps, 1)

            def spread_v(b, d):
                if d < 2:
                    pe.wait_ge(g_ready, 2 * b + d + 1)
                else:
                    pe.wait_ge(kv_ready, HD * b + d - 1)
                if d == 0 and isinstance(b, int) and b == 0:
                    pe.wait_ge(spread_ready, 1)
                m, j = divmod(d, DB)
                nc.tensor.matmul(ring[d % 2][:], spread[:, j, :], vT[0][:, m, :], start=True, stop=False)
                nc.tensor.matmul(ring[d % 2][:], spread[:, j, :], vT[1][:, m, :],
                                 start=False, stop=True).then_inc(vrep_ps, 1)

            def sum_keys(b, d):
                pe.wait_ge(qs_ready, HD * b + d + 1)
                if d == 0:
                    late(pe, o_copied, 2 * b)
                for t in range(TT):
                    last = nc.tensor.matmul(mix_ps[:, t, d * H:(d + 1) * H], qs[d % 2][:, t * P:(t + 1) * P],
                                            gather_k[:], start=True, stop=True)
                last.then_inc(qs_used, 1)

            def out_proj(b):
                pe.wait_ge(og_ready, b + 1)
                for kb in range(KB):
                    if kb == 0:
                        late(pe, record_ready, b)
                    for t in range(TT):
                        last = nc.tensor.transpose(
                            up_ps[kb][:, t * P:(t + 1) * P],
                            o_sb[:, t].rearrange("p h d -> p (h d)")[:, kb * P:(kb + 1) * P], ident[:])
                    last.then_inc(ogT_ps, 1)
                pe.wait_ge(ogT_lo, KB * (b + 1))
                late(pe, x2_ready, 2 * b)
                for t in range(TT):
                    for kb in range(KB):
                        last = product(res_ps[:, t, :], [z[:, kb, t * P:(t + 1) * P] for z in ogT],
                                       [w[:, kb, :] for w in wo], kb == 0, kb == KB - 1)
                    last.then_inc(wo_ps, 1)

            def mlp_in(b):
                pe.wait_ge(zn2_ready, TT * (b + 1))
                for kb in range(KB):
                    for t in range(TT):
                        last = nc.tensor.transpose(up_ps[kb][:, t * P:(t + 1) * P], zn2[:, t, kb * P:(kb + 1) * P], ident[:])
                    last.then_inc(zn2T_ps, 1)
                pe.wait_ge(zn2T_lo, KB * (b + 1))

            def mlp_up(b, f):
                if f > 0:
                    pe.wait_ge(act1_ready, MB * b + f)
                for kb in range(KB):
                    last = product(up_ps[0][:], [w[:, kb, f * P:(f + 1) * P] for w in w1], [z[:, kb, :] for z in ogT],
                                   kb == 0, kb == KB - 1)
                last.then_inc(h1_ps, 1)

            def mlp_gate(b, f):
                if f > 0:
                    pe.wait_ge(prod_ready, MB * b + f)
                for kb in range(KB):
                    last = product(up_ps[1][:], [w[:, kb, f * P:(f + 1) * P] for w in w3], [z[:, kb, :] for z in ogT],
                                   kb == 0, kb == KB - 1)
                last.then_inc(h3_ps, 1)

            def mlp_down(b, f):
                pe.wait_ge(hT_lo, MB * b + f + 1)
                if f == 0:
                    pe.wait_ge(x1_ready, 2 * (b + 1))
                K = P if f < MB - 1 else MLAST
                for t in range(TT):
                    last = product(res_ps[:, t, :], [z[0:K, t * P:(t + 1) * P] for z in hT[f % 2]],
                                   [w[0:K, f, :] for w in w2], f == 0 and t % 2 == 0, f == MB - 1,
                                   skip_group_check=True)
                last.then_inc(hT_used, 1)

            def route(b):
                pe.wait_ge(x3_ready, TT * (b + 1))
                pe.wait_ge(prod_ready, MB * (b + 1))
                for kb in range(KB):
                    for t in range(TT):
                        last = nc.tensor.transpose(up_ps[kb][:, t * P:(t + 1) * P], x3[:, t, kb * P:(kb + 1) * P], ident[:])
                    last.then_inc(x3T_ps, 1)
                pe.wait_ge(x3T_ready, KB * (b + 1))
                for t in range(TT):
                    for kb in range(KB):
                        last = nc.tensor.matmul(up_ps[0][:, t * E:(t + 1) * E], x3T[:, kb, t * P:(t + 1) * P],
                                                gate_sb[:, kb, :], start=kb == 0, stop=kb == KB - 1)
                last.then_inc(gate_ps, 1)
                pe.wait_ge(mask_ready, 2 * b + 1)
                for t in range(TT):
                    dst = up_ps[1][:, t * E:(t + 1) * E]
                    nc.tensor.matmul(dst, earlier[:], mask[:, t, :], start=True, stop=False)
                    for t2 in range(t):
                        nc.tensor.matmul(dst, ones_bf[:], mask[:, t2, :], start=False, stop=False)
                    last = nc.tensor.matmul(dst, ones_bf[:], taken_bf[:], start=False, stop=True)
                last.then_inc(slot_ps, 1)

            attn_in(0)
            for d in range(HD):
                spread_v(0, d)
                if d >= 1:
                    sum_keys(0, d - 1)
            sum_keys(0, HD - 1)

            def ffn_step(b, d):
                f = d // 2
                if f < MB:
                    if d % 2 == 0:
                        mlp_up(b, f)
                    else:
                        mlp_gate(b, f)
                        if f >= 1:
                            mlp_down(b, f - 1)
                elif d == 2 * MB:
                    mlp_down(b, MB - 1)

            pe.wait_ge(w_mlp, 4)
            with pe.Fori(0, B - 1) as b:
                attn_in(b + 1)
                out_proj(b)
                mlp_in(b)
                for d in range(HD):
                    spread_v(b + 1, d)
                    if d >= 1:
                        sum_keys(b + 1, d - 1)
                    ffn_step(b, d)
                sum_keys(b + 1, HD - 1)
                route(b)
            out_proj(B - 1)
            mlp_in(B - 1)
            for d in range(HD):
                ffn_step(B - 1, d)
            route(B - 1)
            pe.wait_ge(mask_ready, 2 * B)
            pe.wait_ge(record_ready, B)
            nc.tensor.matmul(up_ps[1][:, 0:E], ones_bf[:], taken_bf[:], start=True, stop=True).then_inc(count_ps, 1)

            def turn(i, first=False):
                pe.wait_ge(xt_ready, i + 1)
                if not first:
                    pe.wait_ge(xT_lo, i)
                for kb in range(KB):
                    for h in range(PAIR):
                        c = kb * TILE + h * P
                        last = nc.tensor.transpose(ring[0][:, c:c + P], xt[:, h, kb * P:(kb + 1) * P], ident[:])
                last.then_inc(xT_ps, 1)

            def fc1(before, e):
                pe.wait_ge(xT_lo, before + 2)
                for half in range(2):
                    late(pe, gelu_done, FB * before + FB // 2 * (1 + half))
                    for f in range(FB // 2 * half, FB // 2 * (half + 1)):
                        for kb in range(KB):
                            last = product(fc1_out[f], [w[:, kb, f * P:(f + 1) * P] for w in ew1[e % 2]],
                                           [z[:, kb, :] for z in xT], kb == 0, kb == KB - 1)
                    last.then_inc(fc1_ps, 1)

            def fc2(i, e):
                pe.wait_ge(hid_lo, 2 * (i + 1))
                for h in range(PAIR):
                    pe.wait_ge(y_summed, PAIR * i + h + 1)
                    for f in range(FB):
                        last = product(fc2_out[h], [z[:, f, h * P:(h + 1) * P] for z in hidT],
                                       [w[:, f, :] for w in ew2[e % 2]], f == 0, f == FB - 1)
                    last.then_inc(fc2_ps, 1)

            pe.wait_ge(packed, E)
            turn(0, first=True)
            for e in range(E):
                before = first_tile(pe, e, less=1)
                pe.wait_ge(ew1_split, e + 1)
                fc1(before, e)
                turn(before + 2)
                if e > 0:
                    fc2(before, e - 1)
                pe.wait_ge(ew2_split, e + 1)
                start, last = first_tile(pe, e), first_tile(pe, e + 1, less=1)
                with pe.If(last > start):
                    with pe.Fori(start, last) as i:
                        fc1(i, e)
                        turn(i + 2)
                        fc2(i, e)
            fc2(first_tile(pe, E, less=1), E - 1)

        @block.scalar
        def _(act):
            act.wait_ge(vecT_ps, 1)
            nc.scalar.copy(cols[:], up_ps[0][:, 0:NV]).then_inc(vec_ready, 1)
            act.wait_ge(vec_ready, 1)

            def attn_norm(b):
                act.wait_ge(ln_var, TT * (b + 1))
                nc.scalar.activation(small[:, 0, :], mv[:, :, 1], ACT.Ln, bias=eps[:, 0:1]).then_inc(ln_rstd, 1)
                act.wait_ge(ln_rstd, 3 * b + 1)
                nc.scalar.activation(small[:, 1, :], small[:, 0, :], ACT.Exp, scale=-1.0).then_inc(ln_rstd, 1)
                nc.scalar.activation(small[:, 2, :], small[:, 0, :], ACT.Exp, scale=-0.5).then_inc(ln_rstd, 1)
                act.wait_ge(ln_ms, b + 1)
                nc.scalar.activation(small[:, 4, :], small[:, 3, :], ACT.Ln, bias=eps[:, 0:1]).then_inc(ln_rms, 1)
                act.wait_ge(ln_rms, 2 * b + 1)
                nc.scalar.activation(small[:, 5, :], small[:, 4, :], ACT.Exp, scale=-0.5).then_inc(ln_rms, 1)

            def attn_in(b):
                for kb in range(KB):
                    act.wait_ge(znT_ps, KB * b + kb + 1)
                    nc.scalar.activation(znT[0][:, kb, :], ring[kb][:], ACT.Copy,
                                         scale=cols[:, LN1_C + kb:LN1_C + kb + 1]).then_inc(znT_hi, 1)
                act.wait_ge(kg1_ps, b + 1)
                nc.scalar.copy(kg1_sb[:], ring[0][0:LOWRANK, :]).then_inc(kg1_ready, 1)
                act.wait_ge(q_ps, b + 1)
                late(act, qs_ready, HD * b)
                nc.scalar.copy(q_sb[:], ring[1][:]).then_inc(q_ready, 1)
                act.wait_ge(z_ps, b + 1)
                late(act, lsig_ready, b)
                nc.scalar.activation(soft[:], ring[0][:], ACT.Abs, bias=cols[:, BK_C:BK_C + 1]).then_inc(z_abs, 1)
                act.wait_ge(z_abs, b + 1)
                nc.scalar.activation(soft[:], soft[:], ACT.Exp, scale=-1.0).then_inc(z_exp, 1)
                act.wait_ge(z_exp, b + 1)
                nc.scalar.activation(soft[:], soft[:], ACT.Ln, bias=unit[:, 0:1]).then_inc(z_ln, 1)
                act.wait_ge(k_ps, b + 1)
                late(act, kv_ready, HD * b)
                nc.scalar.mul(k_sb[:], ring[1][:], SCALE).then_inc(k_ready, 1)
                act.wait_ge(lsig_ready, b + 1)
                late(act, state_ready, HD * b)
                nc.scalar.activation(decay[:], lsig[:], ACT.Exp, scale=1.0 / NORMALIZER).then_inc(decay_ready, 1)
                for m in range(2):
                    act.wait_ge(v_ps, 2 * b + m + 1)
                    nc.scalar.copy(vT[0][:, m, :], ring[m][:]).then_inc(v_hi, 1)

            def head_norm(b):
                act.wait_ge(gn_var, b + 1)
                nc.scalar.activation(o_sum[:, 2], o_sum[:, 1], ACT.Ln, scale=1.0 / HD, bias=eps[:, 0:1]).then_inc(gn_ln, 1)
                act.wait_ge(gn_ln, b + 1)
                nc.scalar.activation(o_sum[:, 3], o_sum[:, 2], ACT.Exp, scale=-0.5).then_inc(gn_rstd, 1)

            def out_proj(b):
                for kb in range(KB):
                    act.wait_ge(ogT_ps, KB * b + kb + 1)
                    nc.scalar.copy(ogT[0][:, kb, :], up_ps[kb][:]).then_inc(ogT_hi, 1)
                act.wait_ge(x1_ready, 2 * (b + 1))
                for t in range(TT):
                    nc.scalar.activation(x1_sq[:], x1[:, t, :], ACT.Square,
                                         accum_out=rms[:, 0, t:t + 1]).then_inc(x1_squares, 1)
                    act.wait_ge(x1_squares, TT * b + t + 1)
                nc.scalar.activation(rms[:, 1, :], rms[:, 0, :], ACT.Ln, scale=1.0 / D, bias=eps[:, 0:1]).then_inc(rms_ln, 1)
                act.wait_ge(rms_ln, b + 1)
                nc.scalar.activation(rms[:, 1, :], rms[:, 1, :], ACT.Exp, scale=-0.5).then_inc(rms_ready, 1)
                for kb in range(KB):
                    act.wait_ge(zn2T_ps, KB * b + kb + 1)
                    nc.scalar.activation(ogT[0][:, kb, :], up_ps[kb][:], ACT.Copy,
                                         scale=cols[:, LN2_C + kb:LN2_C + kb + 1]).then_inc(zn2T_hi, 1)

            def silu_gate(b):
                act.wait_ge(g_ready, 2 * (b + 1))
                late(act, og_ready, b)
                nc.scalar.activation(silu_g[:], g_sb[:], ACT.Silu).then_inc(silu_ready, 1)

            def mlp(b, f):
                act.wait_ge(h1_ps, MB * b + f + 1)
                if f > 0:
                    act.wait_ge(prod_ready, MB * b + f)
                nc.scalar.activation(act1[:], up_ps[0][:], ACT.Silu).then_inc(act1_ready, 1)
                act.wait_ge(prod_ready, MB * b + f + 1)
                if f >= 2:
                    act.wait_ge(hT_used, MB * b + f - 1)
                nc.scalar.copy(hT[f % 2][0][:], prod[:]).then_inc(hT_hi, 1)

            def route(b):
                act.wait_ge(ln2_var, TT * (b + 1))
                nc.scalar.activation(small2[:, 0, :], mv2[:, :, 1], ACT.Ln, bias=eps[:, 0:1]).then_inc(ln2_ln, 1)
                act.wait_ge(ln2_ln, b + 1)
                nc.scalar.activation(small2[:, 1, :], small2[:, 0, :], ACT.Exp, scale=-0.5).then_inc(ln2_rstd, 1)
                for kb in range(KB):
                    act.wait_ge(x3T_ps, KB * b + kb + 1)
                    nc.scalar.copy(x3T[:, kb, :], up_ps[kb][:]).then_inc(x3T_ready, 1)
                act.wait_ge(score_diff, b + 1)
                nc.scalar.activation(score[:, 1, :], score[:, 0, :], ACT.Exp).then_inc(score_exp, 1)

            nc.scalar.preload_act_table_set(LN_EXP)
            attn_norm(0)
            attn_in(0)
            silu_gate(0)
            for i, (raw, w, ld, n) in enumerate([(raw_o, wo, ld_o, 16), (raw_1, w1, ld_w1, 16), (raw_3, w3, ld_w3, 16)]):
                act.wait_ge(ld, n)
                if i == 1:
                    act.wait_ge(pads_set, 2)
                nc.scalar.copy(w[0][:], raw[:]).then_inc(w_mlp_hi, 1)
            act.wait_ge(ld_w2, 32)
            nc.scalar.copy(w2[0][:, 0:MB - 1, :], raw_2[:, 0:MB - 1, :])
            nc.scalar.copy(w2[0][0:MLAST, MB - 1, :], raw_2[0:MLAST, MB - 1, :]).then_inc(w_mlp_hi, 1)
            with act.Fori(0, B - 1) as b:
                nc.scalar.preload_act_table_set(LN_EXP)
                attn_norm(b + 1)
                head_norm(b)
                attn_in(b + 1)
                out_proj(b)
                silu_gate(b + 1)
                for f in range(MB):
                    mlp(b, f)
                nc.scalar.preload_act_table_set(LN_EXP)
                route(b)
            head_norm(B - 1)
            out_proj(B - 1)
            for f in range(MB):
                mlp(B - 1, f)
            nc.scalar.preload_act_table_set(LN_EXP)
            route(B - 1)

            def x_high(i):
                act.wait_ge(xT_ps, i + 1)
                nc.scalar.copy(xT[0][:], ring[0][:].rearrange("p (k t) -> p k t", k=KB)).then_inc(xT_hi, 1)

            def gelu(i, e, first=False):
                for f in range(FB):
                    half = f // (FB // 2)
                    if f % (FB // 2) == 0:
                        act.wait_ge(fc1_ps, 2 * i + half + 1)
                        if not first and half == 0:
                            act.wait_ge(hid_lo, 2 * i)
                    nc.scalar.activation(hid[:, f, :], fc1_out[f], ACT.Gelu,
                                         bias=cols[:, B1_C + e * FB + f:B1_C + e * FB + f + 1]).then_inc(gelu_done, 1)

            act.wait_ge(bounds_ready, 2)
            x_high(0)
            for e in range(E):
                start = first_tile(act, e)
                gelu(start, e, first=e == 0)
                x_high(start + 1)
                if e + 1 < E:
                    late(act, fc2_ps, PAIR * start)
                    act.wait_ge(ld_e1, 16 * (e + 2))
                    nc.scalar.copy(ew1[(e + 1) % 2][0][:], raw_e1[:]).then_inc(ew1_hi, 1)
                last = first_tile(act, e + 1, less=1)
                with act.If(last > start):
                    with act.Fori(start, last) as i:
                        gelu(i + 1, e)
                        x_high(i + 2)
                if e + 1 < E:
                    act.wait_ge(ld_e2, 16 * (e + 2))
                    nc.scalar.copy(ew2[(e + 1) % 2][0][:], raw_e2[:]).then_inc(ew2_hi, 1)

        @block.vector
        def _(dve):
            V = nc.vector
            V.memset(eps[:], EPS).then_inc(dve_set, 1)
            V.memset(unit[:], 1.0).then_inc(dve_set, 1)
            V.memset(taken[:], 0.0).then_inc(dve_set, 1)
            V.memset(taken_bf[:], 0.0).then_inc(dve_set, 1)
            raws = 0

            def attn_norm(b):
                dve.wait_ge(ld_x, 16 * (b + 1))
                for t in range(TT):
                    V.bn_stats(stats[:, t, :], xin[:, t, :]).then_inc(ln_stat, 1)
                for t in range(TT):
                    settled(dve, ln_stat, TT * b + t + 1)
                    V.bn_aggr(mv[:, t, :], stats[:, t, :]).then_inc(ln_var, 1)
                dve.wait_ge(ln_rstd, 3 * b + 2)
                V.tensor_tensor(small[:, 3, :], mv[:, :, 1], small[:, 1, :], ALU.mult).then_inc(ln_ms, 1)
                dve.wait_ge(ln_rstd, 3 * b + 3)
                late(dve, kept, 2 * b)
                for t in range(TT):
                    V.tensor_scalar(y[:, t, :], xin[:, t, :], mv[:, t, 0:1], small[:, 2, t:t + 1],
                                    ALU.subtract, ALU.mult).then_inc(y_ready, 1)
                dve.wait_ge(ln_rms, 2 * b + 2)
                late(dve, znT_ps, KB * b)
                for t in range(TT):
                    dve.wait_ge(y_ready, TT * b + t + 1)
                    V.tensor_scalar(zn[:, t, :], y[:, t, :], small[:, 5, t:t + 1], None, ALU.mult).then_inc(zn_ready, 1)

            def attn_split(b):
                for kb in range(KB):
                    dve.wait_ge(znT_hi, KB * b + kb + 1)
                    V.scalar_tensor_tensor(znT[1][:, kb, :], ring[kb][:], cols[:, LN1_C + kb:LN1_C + kb + 1],
                                           znT[0][:, kb, :].bitcast(F32), ALU.mult, ALU.subtract).then_inc(znT_lo, 1)

            def attn_decay(b):
                dve.wait_ge(z_abs, b + 1)
                late(dve, decay_ready, b)
                V.tensor_scalar(lsig[:], ring[0][:], cols[:, BK_C:BK_C + 1], 0.0, ALU.add, ALU.min).then_inc(z_min, 1)
                dve.wait_ge(z_ln, b + 1)
                dve.wait_ge(z_min, b + 1)
                V.tensor_tensor(lsig[:], lsig[:], soft[:], ALU.subtract).then_inc(lsig_ready, 1)
                for m in range(2):
                    dve.wait_ge(v_hi, 2 * b + m + 1)
                    V.tensor_tensor(vT[1][:, m, :], ring[m][:], vT[0][:, m, :].bitcast(F32), ALU.subtract).then_inc(v_lo, 1)

            def attn_gate(b):
                late(dve, silu_ready, b)
                for m in range(2):
                    dve.wait_ge(g_ps, 2 * b + m + 1)
                    V.tensor_tensor(g_sb[:, 2 * m:2 * m + 2, :], ring[m][:].rearrange("p (t d) -> p t d", d=D),
                                    bg_bc[:].unsqueeze(1).broadcast_to([P, 2, D]), ALU.add).then_inc(g_ready, 1)

            def scan(b, d):
                n = HD * b + d
                dve.wait_ge(vrep_ps, n + 1)
                if d == 0:
                    dve.wait_ge(k_ready, b + 1)
                    dve.wait_ge(decay_ready, b + 1)
                late(dve, state_ready, n - 1)
                V.tensor_tensor(kv[d % 2][:], ring[d % 2][:], k_sb[:], ALU.mult).then_inc(kv_ready, 1)
                dve.wait_ge(kv_ready, n + 1)
                late(dve, qs_ready, n - 1)
                V.tensor_tensor_scan(state[d % 2][:], decay[:], kv[d % 2][:], 0.0, ALU.mult, ALU.add).then_inc(state_ready, 1)

            def head_norm(b):
                dve.wait_ge(qs_used, HD * (b + 1))
                late(dve, ogT_ps, KB * b)
                for m in range(2):
                    V.tensor_copy(o_sb[:, 2 * m:2 * m + 2].rearrange("p t h d -> p t d h"),
                                  mix_ps[:, 2 * m:2 * m + 2, :].rearrange("p t (d h) -> p t d h", h=H)).then_inc(o_copied, 1)
                dve.wait_ge(o_copied, 2 * (b + 1))
                o3 = o_sb[:].rearrange("p t h d -> p (t h) d")
                sq3 = o_sq[:].rearrange("p t h d -> p (t h) d")
                sm = o_sum[:].rearrange("p c t h -> p c (t h)")

                def over_d(v):
                    return v.unsqueeze(2).broadcast_to([P, TT * H, HD])

                V.tensor_reduce(sm[:, 0], o3, AX.X, ALU.add).then_inc(gn_chain, 1)
                dve.wait_ge(gn_chain, 4 * b + 1)
                V.scalar_tensor_tensor(o3, over_d(sm[:, 0]), -1.0 / HD, o3, ALU.mult, ALU.add).then_inc(gn_chain, 1)
                dve.wait_ge(gn_chain, 4 * b + 2)
                V.tensor_tensor(sq3, o3, o3, ALU.mult).then_inc(gn_chain, 1)
                dve.wait_ge(gn_chain, 4 * b + 3)
                V.tensor_reduce(sm[:, 1], sq3, AX.X, ALU.add).then_inc(gn_var, 1)
                dve.wait_ge(silu_ready, b + 1)
                V.tensor_tensor(o3, o3, silu_g[:].rearrange("p t (h d) -> p (t h) d", d=HD), ALU.mult).then_inc(gn_chain, 1)
                dve.wait_ge(gn_rstd, b + 1)
                dve.wait_ge(gn_chain, 4 * b + 4)
                V.tensor_tensor(o3, o3, over_d(sm[:, 3]), ALU.mult).then_inc(og_ready, 1)

            def out_proj(b):
                for kb in range(KB):
                    dve.wait_ge(ogT_hi, KB * b + kb + 1)
                    V.tensor_tensor(ogT[1][:, kb, :], up_ps[kb][:], ogT[0][:, kb, :].bitcast(F32),
                                    ALU.subtract).then_inc(ogT_lo, 1)
                late(dve, x1x_ready, b)
                for m in range(2):
                    dve.wait_ge(wo_ps, TT * b + 2 * m + 2)
                    if m == 0:
                        dve.wait_ge(kept, 2 * b + 1)
                    V.tensor_tensor(x1[:, 2 * m:2 * m + 2, :], res_ps[:, 2 * m:2 * m + 2, :],
                                    y_keep[:, 2 * m:2 * m + 2, :], ALU.add).then_inc(x1_ready, 1)
                dve.wait_ge(rms_ready, b + 1)
                dve.wait_ge(x1_ready, 2 * (b + 1))
                for t in range(TT):
                    V.tensor_scalar(zn2[:, t, :], x1[:, t, :], rms[:, 1, t:t + 1], None, ALU.mult).then_inc(zn2_ready, 1)
                for kb in range(KB):
                    dve.wait_ge(zn2T_hi, KB * b + kb + 1)
                    V.scalar_tensor_tensor(ogT[1][:, kb, :], up_ps[kb][:], cols[:, LN2_C + kb:LN2_C + kb + 1],
                                           ogT[0][:, kb, :].bitcast(F32), ALU.mult, ALU.subtract).then_inc(zn2T_lo, 1)

            def mlp(b, f):
                dve.wait_ge(act1_ready, MB * b + f + 1)
                dve.wait_ge(h3_ps, MB * b + f + 1)
                late(dve, hT_lo, MB * b + f)
                V.tensor_tensor(prod[:], up_ps[1][:], act1[:], ALU.mult).then_inc(prod_ready, 1)
                dve.wait_ge(hT_hi, MB * b + f + 1)
                V.tensor_tensor(hT[f % 2][1][:], prod[:], hT[f % 2][0][:].bitcast(F32), ALU.subtract).then_inc(hT_lo, 1)

            def residual(b):
                dve.wait_ge(hT_used, MB * (b + 1))
                dve.wait_ge(x1x_ready, b + 1)
                late(dve, x2_stored, 16 * b)
                for m in range(2):
                    V.tensor_tensor(x2[:, 2 * m:2 * m + 2, :], res_ps[:, 2 * m:2 * m + 2, :],
                                    x1x[:, 2 * m:2 * m + 2, :], ALU.add).then_inc(x2_ready, 1)

            RC = 34

            def route(b):
                c = [0]

                def link(ins):
                    c[0] += 1
                    ins.then_inc(route_chain, 1)
                    settled(dve, route_chain, RC * b + c[0])

                dve.wait_ge(x2_ready, 2 * (b + 1))
                for t in range(TT):
                    V.bn_stats(stats2[:, t, :], x2[:, t, :]).then_inc(ln2_stat, 1)
                for t in range(TT):
                    settled(dve, ln2_stat, TT * b + t + 1)
                    V.bn_aggr(mv2[:, t, :], stats2[:, t, :]).then_inc(ln2_var, 1)
                dve.wait_ge(ln2_rstd, b + 1)
                late(dve, x3_stored, 16 * b)
                for t in range(TT):
                    V.tensor_scalar(x3[:, t, :], x2[:, t, :], mv2[:, t, 0:1], small2[:, 1, t:t + 1],
                                    ALU.subtract, ALU.mult).then_inc(x3_ready, 1)
                dve.wait_ge(gate_ps, b + 1)
                link(V.tensor_tensor(logit[:], up_ps[0][:, 0:TT * E].rearrange("p (t e) -> p t e", e=E),
                                     gb_bc[:].unsqueeze(1).broadcast_to([P, TT, E]), ALU.add))
                for t in range(TT):
                    link(V.max(top[:, t, :], logit[:, t, :]))
                for t in range(TT):
                    link(V.max_index(topi[:, t, :], top[:, t, :], logit[:, t, :]))
                V.tensor_tensor(score[:, 0, :], top[:, :, 1], top[:, :, 0], ALU.subtract).then_inc(score_diff, 1)
                link(V.tensor_copy(topf[:], topi[:, :, 0:2]))
                for k in range(2):
                    link(V.tensor_tensor(chosen[:, k], eight[:].unsqueeze(1).broadcast_to([P, TT, E]),
                                         topf[:, :, k:k + 1].broadcast_to([P, TT, E]), ALU.is_equal))
                V.tensor_tensor(mask[:], chosen[:, 0], chosen[:, 1], ALU.add).then_inc(mask_ready, 1)
                dve.wait_ge(score_exp, b + 1)
                link(V.tensor_scalar(score[:, 2, :], score[:, 1, :], 1.0, None, ALU.add))
                link(V.reciprocal(score[:, 2, :], score[:, 2, :]))
                link(V.tensor_tensor(score[:, 3, :], score[:, 1, :], score[:, 2, :], ALU.mult))
                link(V.tensor_tensor(picked[:], chosen[:],
                                     al_bc[:].unsqueeze(1).unsqueeze(1).broadcast_to([P, 2, TT, E]), ALU.mult))
                link(V.tensor_reduce(score[:, 4:6, :], picked[:], AX.X, ALU.add))
                late(dve, recorded, 16 * 2 * TT * b)
                link(V.tensor_tensor(record[:, :, :, 2].bitcast(F32), score[:, 2:4, :], score[:, 4:6, :], ALU.mult))
                for k in range(2):
                    link(V.tensor_copy(record[:, k, :, 0:2],
                                       token_id[:, bass.ds(TT * b, TT)].unsqueeze(2).broadcast_to([P, TT, 2])))
                dve.wait_ge(slot_ps, b + 1)
                before = up_ps[1][:, 0:TT * E].rearrange("p (t e) -> p t e", e=E)
                for k in range(2):
                    link(V.tensor_tensor(picked[:, k], chosen[:, k], before, ALU.mult))
                link(V.tensor_reduce(pos[:, 0], picked[:], AX.X, ALU.add))
                for k in range(2):
                    link(V.tensor_tensor(picked[:, k], chosen[:, k],
                                         first_slot[:].unsqueeze(1).broadcast_to([P, TT, E]), ALU.mult))
                link(V.tensor_reduce(pos[:, 1], picked[:], AX.X, ALU.add))
                link(V.tensor_copy(pos_i[:, 0], pos[:, 0]))
                link(V.tensor_scalar(pos_i[:, 1], pos_i[:, 0], P - 1, None, ALU.bitwise_and))
                link(V.tensor_scalar(pos_i[:, 2], pos_i[:, 0], 7, None, ALU.arith_shift_right))
                link(V.tensor_copy(pos_f[:], pos_i[:, 1:3]))
                link(V.scalar_tensor_tensor(pos[:, 2], pos_f[:, 0], float(E * COLS), pos[:, 1], ALU.mult, ALU.add))
                link(V.tensor_tensor(pos[:, 0], pos[:, 2], pos_f[:, 1], ALU.add))
                V.tensor_copy(where[:], pos[:, 0]).then_inc(record_ready, 1)
                link(V.tensor_reduce(taken_t[:], mask[:].rearrange("p t e -> p e t"), AX.X, ALU.add))
                link(V.tensor_tensor(taken[:], taken[:], taken_t[:], ALU.add))
                V.tensor_copy(taken_bf[:], taken[:]).then_inc(mask_ready, 1)
                assert c[0] == RC, c[0]

            def low_part(w, raw, ready):
                return V.tensor_tensor(w[1][:], raw, w[0][:].bitcast(F32), ALU.subtract).then_inc(ready, 1)

            attn_norm(0)
            dve.wait_ge(ld_qk, 48)
            V.tensor_copy(wqk[0][:], raw_qk[:]).then_inc(split_raw, 1)
            kg1_in = raw_kg1[:].unsqueeze(2).broadcast_to([P, KB, P // LOWRANK, LOWRANK])
            V.tensor_copy(wkg1[0][:], kg1_in).then_inc(split_raw, 1)
            dve.wait_ge(split_raw, 2)
            low_part(wqk, raw_qk[:], w_attn)
            low_part(wkg1, kg1_in, w_attn)
            dve.wait_ge(vec_ready, 1)
            attn_split(0)
            dve.wait_ge(ld_v, 16)
            v_in = raw_v[:].rearrange("p k (h d) -> p k d h", d=HD)
            V.tensor_copy(wv[0][:], v_in).then_inc(split_raw, 1)
            dve.wait_ge(split_raw, 3)
            low_part(wv, v_in, w_attn)
            dve.wait_ge(ld_g, 16)
            V.tensor_copy(wg[0][:], raw_g[:]).then_inc(split_raw, 1)
            dve.wait_ge(split_raw, 4)
            low_part(wg, raw_g[:], w_attn)
            dve.wait_ge(const_ready, 2)
            V.tensor_copy(spread[:], spread_f[:]).then_inc(spread_ready, 1)
            attn_decay(0)
            dve.wait_ge(ld_small, 16 * 6)
            attn_gate(0)
            for d in range(HD):
                scan(0, d)
                if d in (3, 6, 9):
                    i = (3, 6, 9).index(d)
                    dve.wait_ge(w_mlp_hi, i + 1)
                    low_part([wo, w1, w3][i], [raw_o, raw_1, raw_3][i][:], w_mlp)
            dve.wait_ge(w_mlp_hi, 4)
            V.tensor_tensor(w2[1][:, 0:MB - 1, :], raw_2[:, 0:MB - 1, :], w2[0][:, 0:MB - 1, :].bitcast(F32), ALU.subtract)
            V.tensor_tensor(w2[1][0:MLAST, MB - 1, :], raw_2[0:MLAST, MB - 1, :],
                            w2[0][0:MLAST, MB - 1, :].bitcast(F32), ALU.subtract).then_inc(w_mlp, 1)
            dve.wait_ge(const_ready, 10)
            with dve.Fori(0, B - 1) as b:
                attn_norm(b + 1)
                head_norm(b)
                attn_split(b + 1)
                attn_decay(b + 1)
                attn_gate(b + 1)
                out_proj(b)
                for d in range(HD):
                    scan(b + 1, d)
                    if d % 2 == 1 and d // 2 < MB:
                        mlp(b, d // 2)
                residual(b)
                route(b)
            head_norm(B - 1)
            out_proj(B - 1)
            for f in range(MB):
                mlp(B - 1, f)
            residual(B - 1)
            route(B - 1)

            dve.wait_ge(mask_ready, 2 * B)
            V.memset(taken[:], 1.0).then_inc(bounds_chain, 1)
            dve.wait_ge(count_ps, 1)
            V.tensor_tensor(over[:], up_ps[1][:, 0:E].unsqueeze(2).broadcast_to([P, E, T // TILE]),
                            tile_steps[:].unsqueeze(1).broadcast_to([P, E, T // TILE]), ALU.is_gt).then_inc(bounds_chain, 1)
            dve.wait_ge(bounds_chain, 2)
            V.tensor_reduce(tiles_f[:], over[:], AX.X, ALU.add).then_inc(bounds_chain, 1)
            dve.wait_ge(bounds_chain, 3)
            V.tensor_scalar(tiles_f[:], tiles_f[:], float(MIN_TILES), None, ALU.max).then_inc(bounds_chain, 1)
            dve.wait_ge(bounds_chain, 4)
            V.tensor_tensor_scan(cum_f[:], taken[:], tiles_f[:], 0.0, ALU.mult, ALU.add).then_inc(bounds_chain, 1)
            dve.wait_ge(bounds_chain, 5)
            for less in range(2):
                V.tensor_scalar(bounds[:, less, 1:E + 1], cum_f[:], float(-less), None, ALU.add).then_inc(bounds_ready, 1)
            dve.wait_ge(bounds_ready, 2)

            dve.wait_ge(ld_table, 16)
            for e in range(E):
                if e > 0:
                    dve.wait_ge(packed, e)
                V.tensor_copy(table[:, bass.ds(PAIR * first_tile(dve, e), COLS), :],
                              table_all[:, e * COLS:(e + 1) * COLS, :]).then_inc(packed, 1)
            V.memset(y_sum[:], 0.0).then_inc(y_summed, PAIR)
            V.memset(y_out[:], 0.0).then_inc(y_weighed, PAIR)

            def x_low(i):
                dve.wait_ge(xT_hi, i + 1)
                V.tensor_tensor(xT[1][:], ring[0][:].rearrange("p (k t) -> p k t", k=KB),
                                xT[0][:].bitcast(F32), ALU.subtract).then_inc(xT_lo, 1)

            def hand_over(i, first=False):
                dve.wait_ge(gathered, 16 * PAIR * (i + 1))
                if not first:
                    dve.wait_ge(xT_ps, i)
                V.tensor_copy(xt[:], landing[:]).then_inc(xt_ready, 1)

            def hid_split(i, first=False):
                for half in range(2):
                    fs = slice(half * FB // 2, (half + 1) * FB // 2)
                    dve.wait_ge(gelu_done, FB * i + FB // 2 * (half + 1))
                    if not first and half == 0:
                        dve.wait_ge(fc2_ps, PAIR * i)
                    V.tensor_copy(hidT[0][:, fs, :], hid[:, fs, :]).then_inc(hid_hi, 1)
                    dve.wait_ge(hid_hi, 2 * i + half + 1)
                    V.tensor_tensor(hidT[1][:, fs, :], hid[:, fs, :], hidT[0][:, fs, :].bitcast(F32),
                                    ALU.subtract).then_inc(hid_lo, 1)

            def weigh(i, e):
                for h in range(PAIR):
                    dve.wait_ge(fc2_ps, PAIR * i + h + 1)
                    dve.wait_ge(y_weighed, PAIR * i + h + 1)
                    V.tensor_tensor(y_sum[:, h, :], fc2_out[h], b2_bc[:, e, :], ALU.add).then_inc(y_summed, 1)
                dve.wait_ge(y_free, i + 1)
                for h in range(PAIR):
                    dve.wait_ge(y_summed, PAIR * (i + 1) + h + 1)
                    V.tensor_scalar(y_out[:, h, :], y_sum[:, h, :], table[:, bass.ds(PAIR * i + h, 1), 2].bitcast(F32),
                                    None, ALU.mult).then_inc(y_weighed, 1)

            dve.wait_ge(packed, E)
            hand_over(0, first=True)
            x_low(0)
            hand_over(1)
            for e in range(E):
                start = first_tile(dve, e)
                x_low(start + 1)
                hid_split(start, first=e == 0)
                hand_over(start + 2)
                if e > 0:
                    weigh(first_tile(dve, e, less=1), e - 1)
                if e + 1 < E:
                    dve.wait_ge(ew1_hi, e + 1)
                    V.tensor_tensor(ew1[(e + 1) % 2][1][:], raw_e1[:], ew1[(e + 1) % 2][0][:].bitcast(F32),
                                    ALU.subtract).then_inc(ew1_split, 1)
                last = first_tile(dve, e + 1, less=1)
                with dve.If(last > start):
                    with dve.Fori(start, last) as i:
                        x_low(i + 2)
                        hid_split(i + 1)
                        hand_over(i + 3)
                        weigh(i, e)
                if e + 1 < E:
                    dve.wait_ge(ew2_hi, e + 1)
                    V.tensor_tensor(ew2[(e + 1) % 2][1][:], raw_e2[:], ew2[(e + 1) % 2][0][:].bitcast(F32),
                                    ALU.subtract).then_inc(ew2_split, 1)
            weigh(first_tile(dve, E, less=1), E - 1)


_INS = ['x', 'Wq', 'Wk', 'Wkg1', 'Wkg2', 'bkg2', 'Wv', 'Wg', 'bg', 'Wo', 'ln1_w', 'ln2_w', 'W1', 'W3', 'W2']
_INS = ['L0_attn_' + n for n in _INS]
_INS += ['L0_ffn_' + n for n in ['gate_w', 'gate_b', 'fc1_w', 'fc1_b', 'fc2_w', 'fc2_b', 'alpha']]


def kernel(**inputs):
    import numpy as _np
    import concourse.bacc as _bacc
    from concourse import mybir as _mybir
    from concourse.bass_utils import run_bass_kernel_spmd as _run

    nc = _bacc.Bacc("TRN2", target_bir_lowering=False, num_devices=1)
    arrays, args = {}, []
    for name in _INS:
        a = _np.ascontiguousarray(inputs[name])
        arrays[f"in_{name}_dram"] = a
        args.append(nc.dram_tensor(f"in_{name}_dram", a.shape, _mybir.dt.from_np(a.dtype), kind="ExternalInput").ap())
    shape = arrays["in_L0_attn_x_dram"].shape
    args.append(nc.dram_tensor("out_0_dram", shape, _mybir.dt.float32, kind="ExternalOutput").ap())
    build(nc, *args)
    r = _run(nc, [arrays], core_ids=[0])
    return r.results[0]["out_0_dram"]
```

```python
from contextlib import ExitStack

import concourse.bass as bass
from concourse import mybir

F32 = mybir.dt.float32
F32R = mybir.dt.float32r
BF16 = mybir.dt.bfloat16
I32 = mybir.dt.int32
U32 = mybir.dt.uint32
ALU = mybir.AluOpType
ACT = mybir.ActivationFunctionType
AX = mybir.AxisListType

P = 128
LN_EXP = "natural_log_exp_and_others"


def build(nc, x, Wq, Wk, Wkg1, Wkg2, bkg2, Wv, Wg, bg, Wo, ln1_w, ln2_w, W1, W3, W2,
          gate_w, gate_b, fc1_w, fc1_b, fc2_w, fc2_b, alpha, out):
    B, L, D = x.shape
    HK = Wq.shape[1]
    H = 16
    KD = HK // H
    HD = D // H
    MLP = W1.shape[1]
    E, _, F = fc1_w.shape
    T = B * L
    TT = L // P
    KB = D // P
    MB = -(-MLP // P)
    MLAST = MLP - (MB - 1) * P
    FB = F // P
    DB = P // H
    LOWRANK = Wkg1.shape[1]
    SCALE = float(HD) ** -0.5
    EPS = 1e-5
    NORMALIZER = 16.0
    MIN_TILES = 1
    LEAD = HD - 2 * MB
    PAIR = 2
    TILE = PAIR * P
    NV = E * FB + 2 * KB + 1
    COLS = T // P + 4 * PAIR
    NOWHERE = 1 << 20

    x_rows = x.rearrange("b l d -> (b l) d")
    out_rows = out.rearrange("b l d -> (b l) d")
    x_tiles = x_rows.rearrange("(n p) d -> p n d", p=P)
    out_tiles = out_rows.rearrange("(n p) d -> p n d", p=P)

    normed_dram = nc.dram_tensor("normed_rows", [T, D], F32, kind="Internal").ap()
    normed_tiles = normed_dram.rearrange("(n p) d -> p n d", p=P)
    table_dram = nc.dram_tensor("routing_table", [P * E * COLS, 4], I32, kind="Internal").ap()
    table_view = table_dram.rearrange("(p c) w -> p c w", p=P)

    with ExitStack() as ctx:
        def sb(name, shape, dt=F32, scope=ctx):
            return scope.enter_context(nc.sbuf_tensor(name, shape, dt))

        def psum(name, shape, dt=F32):
            return ctx.enter_context(nc.psum_tensor(name, shape, dt))

        def sem(name):
            return ctx.enter_context(nc.semaphore(name))

        ring = [psum("ring0", [P, L]), psum("ring1", [P, L])]
        mix_ps = psum("mix_ps", [P, TT, D])
        up_ps = [psum("up0_ps", [P, L]), psum("up1_ps", [P, L])]
        res_ps = psum("res_ps", [P, TT, D])

        fc1_out = [up_ps[f // 2][:, f % 2 * TILE:(f % 2 + 1) * TILE] if f < FB // 2 else mix_ps[:, f - FB // 2, :]
                   for f in range(FB)]
        x3_ps = [mix_ps[:, 2 * kb:2 * kb + 2, :].rearrange("p t d -> p (t d)") for kb in range(KB)]
        fc2_out = [ring[1][:, 0:D], res_ps[:, 0, :]]

        ident = sb("ident", [P, P])
        cols = sb("cols", [P, E * FB + 2 * KB + 1])
        B1_C, LN1_C, LN2_C, BK_C = 0, E * FB, E * FB + KB, E * FB + 2 * KB
        b2_bc = sb("b2_bc", [P, E, D])
        bounds = sb("bounds", [P, 2, E + 1], I32)
        eps = sb("eps", [P, 1])
        full = sb("full", [P, E], I32)
        unit = sb("unit", [P, 1])
        one = ExitStack()
        ctx.enter_context(one)

        def s1(name, shape, dt=F32):
            return sb(name, shape, dt, one)

        xin = s1("xin", [P, TT, D])
        y = s1("y", [P, TT, D])
        zn = s1("zn", [P, TT, D])
        znT = [s1(f"znT{i}", [P, KB, L], F32R) for i in range(2)]
        kg1_sb = s1("kg1_sb", [LOWRANK, L])
        soft = s1("soft", [P, L])
        lsig = s1("lsig", [P, L])
        decay = s1("decay", [P, L])
        vT = [s1(f"vT{i}", [P, KB, L], F32R) for i in range(2)]
        kv = [s1(f"kv{i}", [P, L]) for i in range(2)]
        k_sb = s1("k_sb", [P, L])
        g_sb = s1("g_sb", [P, TT, D])
        q_sb = s1("q_sb", [P, L])
        state = [s1(f"state{i}", [P, L]) for i in range(2)]
        qs = [s1(f"qs{i}", [P, L]) for i in range(2)]
        wqk = [s1(f"wqk{i}", [P, 2, KB, HK], F32R) for i in range(2)]
        wkg1 = [s1(f"wkg1{i}", [P, KB, P // LOWRANK, LOWRANK], F32R) for i in range(2)]
        wkg2 = s1("wkg2", [LOWRANK, HK])
        wv = [s1(f"wv{i}", [P, KB, HD, H], F32R) for i in range(2)]
        wg = [s1(f"wg{i}", [P, KB, D], F32R) for i in range(2)]
        spread = s1("spread", [P, DB, P], F32R)
        gather_k = s1("gather_k", [P, H])
        bg_bc = s1("bg_bc", [P, D])
        stats = s1("stats", [P, TT, 6])
        mv = s1("mv", [P, TT, 2])
        small = s1("small", [P, 8, TT])
        wo = [s1(f"wo{i}", [P, KB, D], F32R) for i in range(2)]
        w1 = [s1(f"w1{i}", [P, KB, MB * P], F32R) for i in range(2)]
        w3 = [s1(f"w3{i}", [P, KB, MB * P], F32R) for i in range(2)]
        w2 = [s1(f"w2{i}", [P, MB, D], F32R) for i in range(2)]
        silu_g = s1("silu_g", [P, TT, D])
        y_keep = s1("y_keep", [P, TT, D])
        x_keep = s1("x_keep", [P, TT, D])
        x1x = s1("x1x", [P, TT, D])
        gate_sb = s1("gate_sb", [P, KB, E])
        gb_bc = s1("gb_bc", [P, E])
        al_bc = s1("al_bc", [P, E])
        earlier = s1("earlier", [P, P], BF16)
        ones_bf = s1("ones_bf", [P, P], BF16)
        eight = s1("eight", [P, E])
        token_id = s1("token_id", [P, T // P], I32)
        column_steps = s1("column_steps", [P, T // P])
        first_number = s1("first_number", [P, E])
        o_sum = s1("o_sum", [P, 4, TT, H])
        rms = s1("rms", [P, 2, TT])
        stats2 = s1("stats2", [P, TT, 6])
        mv2 = s1("mv2", [P, TT, 2])
        small2 = s1("small2", [P, 2, TT])
        logit = s1("logit", [P, TT, E])
        top = s1("top", [P, TT, 8])
        topi = s1("topi", [P, TT, 8], U32)
        topf = s1("topf", [P, TT, 2])
        chosen = s1("chosen", [P, 2, TT, E])
        picked = s1("picked", [P, 2, TT, E])
        mask = s1("mask", [P, TT, E], BF16)
        taken = s1("taken", [P, E])
        taken_t = s1("taken_t", [P, E])
        taken_bf = s1("taken_bf", [P, E], BF16)
        scores = s1("scores", [P, 6, TT])
        number = s1("number", [P, TT, E])
        numbered = s1("numbered", [P, 2, TT, E])
        pos = s1("pos", [P, 2, TT])
        pos_i = s1("pos_i", [P, 3, 2, TT], I32)
        where = s1("where", [P, 2, TT], I32)
        record = s1("record", [P, 2, TT, 4], I32)
        fill = s1("fill", [P, E * COLS, 4], I32)
        over = s1("over", [P, E, T // P])
        columns_f = s1("columns_f", [P, E])
        full_f = s1("full_f", [P, E])
        tiles_f = s1("tiles_f", [P, E])
        cum_f = s1("cum_f", [P, E])
        with ExitStack() as early:
            vec_rows = sb("vec_rows", [NV, P], F32, early)
            raw_qk = sb("raw_qk", [P, 2, KB, HK], F32, early)
            raw_kg1 = sb("raw_kg1", [P, KB, LOWRANK], F32, early)
            raw_v = sb("raw_v", [P, KB, D], F32, early)
            raw_g = sb("raw_g", [P, KB, D], F32, early)
            raw_o = sb("raw_o", [P, KB, D], F32, early)
            raw_1 = sb("raw_1", [P, KB, MB * P], F32, early)
            raw_3 = sb("raw_3", [P, KB, MB * P], F32, early)
            raw_2 = sb("raw_2", [P, MB, D], F32, early)
            spread_f = sb("spread_f", [P, DB, P], F32, early)
        o_sb = s1("o_sb", [P, TT, H, HD])
        o_sq = s1("o_sq", [P, TT, H, HD])
        ogT = [s1(f"ogT{i}", [P, KB, L], F32R) for i in range(2)]
        x1 = s1("x1", [P, TT, D])
        zn2 = s1("zn2", [P, TT, D])
        act1 = s1("act1", [P, L])
        prod = s1("prod", [P, L])
        hT = [[s1(f"hT{j}{i}", [P, L], F32R) for i in range(2)] for j in range(2)]
        x2 = s1("x2", [P, TT, D])
        x3 = s1("x3", [P, TT, D])
        x3T = s1("x3T", [P, KB, L])
        one.close()

        raw_e1 = sb("raw_e1", [P, KB, F])
        raw_e2 = sb("raw_e2", [P, FB, D])
        ew1, ew2 = [], []
        for s in range(2):
            ew1.append([sb(f"ew1_{s}{i}", [P, KB, F], F32R) for i in range(2)])
            ew2.append([sb(f"ew2_{s}{i}", [P, FB, D], F32R) for i in range(2)])
        table_all = sb("table_all", [P, E * COLS, 4], I32)
        table = sb("table", [P, E * COLS, 4], I32)
        row_in = sb("row_in", [P, PAIR], I32)
        row_out = sb("row_out", [P, PAIR], I32)
        landing = sb("landing", [P, PAIR, D])
        xt = sb("xt", [P, PAIR, D])
        xT = [sb(f"xT{i}", [P, KB, TILE], F32R) for i in range(2)]
        hid = sb("hid", [P, FB, TILE])
        hidT = [sb(f"hidT{i}", [P, FB, TILE], F32R) for i in range(2)]
        y_sum = sb("y_sum", [P, PAIR, D])
        y_out = sb("y_out", [P, PAIR, D])

        ld_x = sem("ld_x")
        ld_vec = sem("ld_vec")
        ld_small = sem("ld_small")
        ld_qk = sem("ld_qk")
        ld_v = sem("ld_v")
        ld_g = sem("ld_g")
        ld_o = sem("ld_o")
        ld_w1 = sem("ld_w1")
        ld_w3 = sem("ld_w3")
        ld_w2 = sem("ld_w2")
        ones_set = sem("ones_set")
        dve_set = sem("dve_set")
        pads_set = sem("pads_set")
        const_ready = sem("const_ready")
        spread_ready = sem("spread_ready")
        vecT_ps = sem("vecT_ps")
        vec_ready = sem("vec_ready")
        split_raw = sem("split_raw")
        w_attn = sem("w_attn")
        w_mlp = sem("w_mlp")
        ln_stat = sem("ln_stat")
        ln_var = sem("ln_var")
        ln_ms = sem("ln_ms")
        ln_rstd = sem("ln_rstd")
        ln_rms = sem("ln_rms")
        y_ready = sem("y_ready")
        zn_ready = sem("zn_ready")
        znT_ps = sem("znT_ps")
        znT_hi = sem("znT_hi")
        znT_lo = sem("znT_lo")
        kg1_ps = sem("kg1_ps")
        kg1_ready = sem("kg1_ready")
        q_ps = sem("q_ps")
        q_ready = sem("q_ready")
        k_ps = sem("k_ps")
        k_ready = sem("k_ready")
        z_ps = sem("z_ps")
        z_abs = sem("z_abs")
        z_min = sem("z_min")
        z_exp = sem("z_exp")
        z_ln = sem("z_ln")
        lsig_ready = sem("lsig_ready")
        decay_ready = sem("decay_ready")
        v_ps = sem("v_ps")
        v_hi = sem("v_hi")
        v_lo = sem("v_lo")
        g_ps = sem("g_ps")
        g_ready = sem("g_ready")
        silu_ready = sem("silu_ready")
        kept_y = sem("kept_y")
        kept_x = sem("kept_x")
        vrep_ps = sem("vrep_ps")
        kv_ready = sem("kv_ready")
        state_ready = sem("state_ready")
        qs_ready = sem("qs_ready")
        qs_used = sem("qs_used")
        o_copied = sem("o_copied")
        gn_chain = sem("gn_chain")
        gn_var = sem("gn_var")
        gn_ln = sem("gn_ln")
        gn_rstd = sem("gn_rstd")
        og_ready = sem("og_ready")
        ogT_ps = sem("ogT_ps")
        ogT_hi = sem("ogT_hi")
        ogT_lo = sem("ogT_lo")
        wo_ps = sem("wo_ps")
        x1_ready = sem("x1_ready")
        x1x_ready = sem("x1x_ready")
        x1_squares = sem("x1_squares")
        rms_ln = sem("rms_ln")
        rms_ready = sem("rms_ready")
        zn2_ready = sem("zn2_ready")
        zn2T_ps = sem("zn2T_ps")
        zn2T_hi = sem("zn2T_hi")
        zn2T_lo = sem("zn2T_lo")
        h1_ps = sem("h1_ps")
        h3_ps = sem("h3_ps")
        act1_ready = sem("act1_ready")
        prod_ready = sem("prod_ready")
        hT_hi = sem("hT_hi")
        hT_lo = sem("hT_lo")
        hT_used = sem("hT_used")
        x2_ready = sem("x2_ready")
        x2_stored = sem("x2_stored")
        ln2_stat = sem("ln2_stat")
        ln2_var = sem("ln2_var")
        ln2_ln = sem("ln2_ln")
        ln2_rstd = sem("ln2_rstd")
        x3_ready = sem("x3_ready")
        x3_stored = sem("x3_stored")
        x23_free = sem("x23_free")
        record_free = sem("record_free")
        x3T_ps = sem("x3T_ps")
        x3T_ready = sem("x3T_ready")
        gate_ps = sem("gate_ps")
        route_chain = sem("route_chain")
        logits_read = sem("logits_read")
        number_read = sem("number_read")
        score_diff = sem("score_diff")
        score_exp = sem("score_exp")
        mask_ready = sem("mask_ready")
        slot_ps = sem("slot_ps")
        record_ready = sem("record_ready")
        filled = sem("filled")
        recorded = sem("recorded")
        count_ps = sem("count_ps")
        bounds_ready = sem("bounds_ready")
        bounds_chain = sem("bounds_chain")
        w_mlp_hi = sem("w_mlp_hi")
        ld_e1 = sem("ld_e1")
        ld_e2 = sem("ld_e2")
        ld_table = sem("ld_table")
        packed = sem("packed")
        ew1_hi = sem("ew1_hi")
        ew2_hi = sem("ew2_hi")
        ew1_split = sem("ew1_split")
        ew2_split = sem("ew2_split")
        row_in_ready = sem("row_in_ready")
        gathered = sem("gathered")
        xt_ready = sem("xt_ready")
        xT_ps = sem("xT_ps")
        xT_hi = sem("xT_hi")
        xT_lo = sem("xT_lo")
        fc1_ps = sem("fc1_ps")
        gelu_done = sem("gelu_done")
        hid_hi = sem("hid_hi")
        hid_lo = sem("hid_lo")
        fc2_ps = sem("fc2_ps")
        y_summed = sem("y_summed")
        y_weighed = sem("y_weighed")
        y_free = sem("y_free")
        row_out_ready = sem("row_out_ready")
        added = sem("added")

        passed = {e: sem(f"passed_{n}") for e, n in [
            (nc.sync.engine, "sp"), (nc.gpsimd.engine, "pool"), (nc.vector.engine, "dve"),
            (nc.scalar.engine, "act"), (nc.tensor.engine, "pe")]}

        def product(dst, a, b, start, stop, **kw):
            nc.tensor.matmul(dst, a[0], b[0], start=start, stop=False, **kw)
            nc.tensor.matmul(dst, a[0], b[1], start=False, stop=False, **kw)
            return nc.tensor.matmul(dst, a[1], b[0], start=False, stop=stop, **kw)

        def only(b, n):
            return isinstance(b, int) and b == n

        def late(eng, s, v):
            if not (isinstance(v, int) and v <= 0):
                settled(eng, s, v)

        def settled(eng, s, v):
            eng.wait_ge(s, v)
            if not isinstance(v, int):
                eng.sem_inc(passed[eng.engine], 1)

        def first_tile(eng, e, less=0):
            if e == 0:
                return 0 - less
            most = 2 * T // TILE + MIN_TILES * E
            return eng.value_load(bounds[0:1, less, e:e + 1], min_val=MIN_TILES - less, max_val=most)

        block = ctx.enter_context(nc.Block())

        @block.sync
        def _(sp):
            sp.dma_start(xin[:], x_tiles[:, 0:TT, :]).then_inc(ld_x, 16)
            sp.dma_start(raw_qk[:, 0], Wq.rearrange("(k p) n -> p k n", p=P)).then_inc(ld_qk, 16)
            sp.dma_start(raw_qk[:, 1], Wk.rearrange("(k p) n -> p k n", p=P)).then_inc(ld_qk, 16)
            sp.dma_start(raw_kg1[:], Wkg1.rearrange("(k p) n -> p k n", p=P)).then_inc(ld_qk, 16)
            sp.dma_start(raw_v[:], Wv.rearrange("(k p) n -> p k n", p=P)).then_inc(ld_v, 16)
            nb = E * FB
            sp.dma_start(vec_rows[0:nb, :], fc1_b.rearrange("e (f p) -> (e f) p", p=P)).then_inc(ld_vec, 16)
            sp.dma_start(vec_rows[nb:nb + KB, :], ln1_w.rearrange("(k p) -> k p", p=P)).then_inc(ld_vec, 16)
            sp.dma_start(vec_rows[nb + KB:nb + 2 * KB, :], ln2_w.rearrange("(k p) -> k p", p=P)).then_inc(ld_vec, 16)
            sp.dma_start(vec_rows[nb + 2 * KB:NV, :], bkg2.rearrange("(k p) -> k p", p=P)).then_inc(ld_vec, 16)
            sp.dma_start(wkg2[:], Wkg2).then_inc(ld_small, 16)
            sp.dma_start(bg_bc[:], bg.partition_broadcast(P)).then_inc(ld_small, 16)
            sp.dma_start(gb_bc[:], gate_b.partition_broadcast(P)).then_inc(ld_small, 16)
            sp.dma_start(al_bc[:], alpha.partition_broadcast(P)).then_inc(ld_small, 16)
            sp.dma_start(gate_sb[:], gate_w.rearrange("(k p) n -> p k n", p=P)).then_inc(ld_small, 16)
            sp.dma_start(raw_g[:], Wg.rearrange("(k p) n -> p k n", p=P)).then_inc(ld_g, 16)
            sp.dma_start(raw_o[:], Wo.rearrange("(k p) n -> p k n", p=P)).then_inc(ld_o, 16)
            sp.dma_start(raw_1[:, :, 0:MLP], W1.rearrange("(k p) n -> p k n", p=P)).then_inc(ld_w1, 16)
            sp.dma_start(raw_3[:, :, 0:MLP], W3.rearrange("(k p) n -> p k n", p=P)).then_inc(ld_w3, 16)
            sp.dma_start(raw_2[:, 0:MB - 1, :],
                         W2[0:(MB - 1) * P, :].rearrange("(k p) n -> p k n", p=P)).then_inc(ld_w2, 16)
            sp.dma_start(raw_2[0:MLAST, MB - 1, :], W2[(MB - 1) * P:MLP, :]).then_inc(ld_w2, 16)
            sp.dma_start(b2_bc[:], fc2_b.partition_broadcast(P)).then_inc(ld_small, 16)
            sp.wait_ge(pads_set, 4)
            sp.dma_start(table_view, fill[:]).then_inc(filled, 16)

            def store(b):
                settled(sp, x2_ready, 2 * (b + 1))
                sp.dma_start(out_tiles[:, bass.ds(TT * b, TT), :], x2[:]).then_inc(x2_stored, 16)
                settled(sp, x3_ready, TT * (b + 1))
                sp.dma_start(normed_tiles[:, bass.ds(TT * b, TT), :], x3[:]).then_inc(x3_stored, 16)

            def free_stored(b):
                settled(sp, x2_stored, 16 * (b + 1))
                settled(sp, x3_stored, 16 * (b + 1))
                sp.sem_inc(x23_free, 1)

            def keep(b):
                settled(sp, y_ready, TT * (b + 1))
                late(sp, x1_ready, 2 * b)
                sp.dma_start(y_keep[:], y[:]).then_inc(kept_y, 16)
                late(sp, x1x_ready, b)
                sp.dma_start(x_keep[:], xin[:]).then_inc(kept_x, 16)

            def load(b):
                settled(sp, kept_x, 16 * b)
                settled(sp, zn_ready, TT * b)
                sp.dma_start(xin[:], x_tiles[:, bass.ds(TT * b, TT), :]).then_inc(ld_x, 16)

            keep(0)
            sp.sem_inc(x23_free, 1)
            load(1)
            keep(1)
            load(2)
            with sp.Fori(0, B - 3) as b:
                store(b)
                free_stored(b)
                keep(b + 2)
                load(b + 3)
            store(B - 3)
            free_stored(B - 3)
            keep(B - 1)
            store(B - 2)
            free_stored(B - 2)

            def load_expert(e):
                if e == 0:
                    sp.wait_ge(qs_used, HD * B)
                else:
                    sp.wait_ge(ew1_split, e)
                sp.dma_start(raw_e1[:], fc1_w[e].rearrange("(k p) n -> p k n", p=P)).then_inc(ld_e1, 16)
                if e > 0:
                    sp.wait_ge(ew2_split, e)
                sp.dma_start(raw_e2[:], fc2_w[e].rearrange("(k p) n -> p k n", p=P)).then_inc(ld_e2, 16)

            load_expert(0)
            store(B - 1)
            load_expert(1)
            sp.wait_ge(recorded, 16 * 2 * TT * B)
            sp.dma_start(table_all[:], table_view).then_inc(ld_table, 16)
            for e in range(2, E):
                load_expert(e)

        @block.gpsimd
        def _(pool):
            nc.gpsimd.memset(spread_f[:], 1.0).then_inc(ones_set, 1)
            nc.gpsimd.memset(ident[:], 0.0).then_inc(ones_set, 1)
            nc.gpsimd.memset(gather_k[:], 1.0).then_inc(ones_set, 1)
            nc.gpsimd.memset(ones_bf[:], 1.0).then_inc(ones_set, 1)
            nc.gpsimd.memset(earlier[:], 1.0).then_inc(ones_set, 1)
            nc.gpsimd.memset(raw_1[:, :, MLP:MB * P], 0.0).then_inc(pads_set, 1)
            nc.gpsimd.memset(raw_3[:, :, MLP:MB * P], 0.0).then_inc(pads_set, 1)
            pool.wait_ge(ones_set, 5)
            nc.gpsimd.affine_select(out=ident[:], in_=ident[:], compare_op=ALU.not_equal, fill=1.0, base=0,
                                    pattern=[[-1, P]], channel_multiplier=1).then_inc(const_ready, 1)
            nc.gpsimd.affine_select(out=spread_f[:].rearrange("p j (h k) -> p j h k", k=KD),
                                    in_=spread_f[:].rearrange("p j (h k) -> p j h k", k=KD),
                                    compare_op=ALU.is_equal, fill=0.0, base=0,
                                    pattern=[[-H, DB], [-1, H], [0, KD]], channel_multiplier=1).then_inc(const_ready, 1)
            nc.gpsimd.affine_select(out=gather_k[:], in_=gather_k[:], compare_op=ALU.is_ge, fill=0.0, base=0,
                                    pattern=[[-KD, H]], channel_multiplier=1).then_inc(const_ready, 1)
            pool.wait_ge(const_ready, 3)
            nc.gpsimd.affine_select(out=gather_k[:], in_=gather_k[:], compare_op=ALU.is_ge, fill=0.0, base=KD - 1,
                                    pattern=[[KD, H]], channel_multiplier=-1).then_inc(const_ready, 1)
            nc.gpsimd.affine_select(out=earlier[:], in_=earlier[:], compare_op=ALU.is_gt, fill=0.0, base=0,
                                    pattern=[[1, P]], channel_multiplier=-1).then_inc(const_ready, 1)
            nc.gpsimd.iota(eight[:], pattern=[[1, E]], base=0, channel_multiplier=0,
                           allow_small_or_imprecise_dtypes=True).then_inc(const_ready, 1)
            nc.gpsimd.iota(column_steps[:], pattern=[[P, T // P]], base=0, channel_multiplier=0,
                           allow_small_or_imprecise_dtypes=True).then_inc(const_ready, 1)
            nc.gpsimd.iota(first_number[:], pattern=[[COLS * P, E]], base=0, channel_multiplier=0,
                           allow_small_or_imprecise_dtypes=True).then_inc(const_ready, 1)
            nc.gpsimd.iota(token_id[:], pattern=[[P, T // P]], base=0, channel_multiplier=1).then_inc(const_ready, 1)
            nc.gpsimd.memset(record[:], 0).then_inc(const_ready, 1)
            nc.gpsimd.memset(fill[:], 0).then_inc(pads_set, 1)
            pool.wait_ge(pads_set, 3)
            nc.gpsimd.memset(fill[:, :, 1:2], NOWHERE).then_inc(pads_set, 1)

            def query(b, d):
                settled(pool, state_ready, HD * b + d + 1)
                if d == 0:
                    settled(pool, q_ready, b + 1)
                late(pool, qs_used, HD * b + d - 1)
                nc.gpsimd.tensor_tensor(qs[d % 2][:], state[d % 2][:], q_sb[:], ALU.mult).then_inc(qs_ready, 1)

            def write_record(b, j):
                k, t = divmod(j, TT)
                if j == 0:
                    settled(pool, record_ready, b + 1)
                    pool.wait_ge(filled, 16)
                nc.gpsimd.indirect_dma_start(
                    out=table_dram, out_offset=bass.IndirectOffsetOnAxis(ap=where[:, k, t:t + 1], axis=0),
                    in_=record[:, k, t, :], in_offset=None).then_inc(recorded, 16)

            def residual(b):
                settled(pool, x1_ready, 2 * (b + 1))
                settled(pool, kept_x, 16 * (b + 1))
                late(pool, x2_ready, 2 * b)
                nc.gpsimd.tensor_tensor(x1x[:], x1[:], x_keep[:], ALU.add).then_inc(x1x_ready, 1)

            def free_records(b):
                settled(pool, recorded, 16 * 2 * TT * (b + 1))
                pool.sem_inc(record_free, 1)

            MIDDLE = LEAD + 2 * TT
            pool.sem_inc(record_free, 1)
            for d in range(HD):
                query(0, d)
            for d in range(LEAD):
                query(1, d)
            residual(0)
            for d in range(LEAD, MIDDLE):
                query(1, d)
            with pool.Fori(0, B - 2) as b:
                for d in range(MIDDLE, HD):
                    query(b + 1, d)
                for d in range(LEAD):
                    query(b + 2, d)
                residual(b + 1)
                for d in range(LEAD, MIDDLE):
                    query(b + 2, d)
                    write_record(b, d - LEAD)
                free_records(b)
            for d in range(MIDDLE, HD):
                query(B - 1, d)
            residual(B - 1)
            for b in (B - 2, B - 1):
                for j in range(2 * TT):
                    write_record(b, j)
                if b == B - 2:
                    free_records(b)

            def fetch(i, columns=table):
                late(pool, xt_ready, i)
                nc.gpsimd.tensor_copy(row_in[:], columns[:, bass.ds(PAIR * i, PAIR), 0]).then_inc(row_in_ready, 1)
                settled(pool, row_in_ready, i + 1)
                for h in range(PAIR):
                    nc.gpsimd.indirect_dma_start(
                        out=landing[:, h, :], out_offset=None, in_=normed_dram,
                        in_offset=bass.IndirectOffsetOnAxis(ap=row_in[:, h:h + 1], axis=0)).then_inc(gathered, 16)

            def add_rows(j, h):
                if h == 0:
                    late(pool, added, 16 * PAIR * j)
                    pool.sem_inc(y_free, 1)
                    nc.gpsimd.tensor_copy(row_out[:], table[:, bass.ds(PAIR * j, PAIR), 1]).then_inc(row_out_ready, 1)
                    settled(pool, row_out_ready, j + 1)
                settled(pool, y_weighed, PAIR * (j + 1) + h + 1)
                nc.gpsimd.indirect_dma_start(
                    out=out_rows, out_offset=bass.IndirectOffsetOnAxis(ap=row_out[:, h:h + 1], axis=0),
                    in_=y_out[:, h, :], in_offset=None, bounds_check=T - 1, oob_is_err=False,
                    compute_op=ALU.add).then_inc(added, 16)

            pool.wait_ge(x3_stored, 16 * B)
            pool.wait_ge(x2_stored, 16 * B)
            pool.wait_ge(ld_table, 16)
            fetch(0, table_all)
            pool.wait_ge(packed, E)
            fetch(1)
            fetch(2)
            fetch(3)
            last = first_tile(pool, E, less=1)
            add_rows(0, 0)
            fetch(4)
            add_rows(0, 1)
            with pool.Fori(1, last) as i:
                add_rows(i, 0)
                fetch(i + 4)
                add_rows(i, 1)
            for h in range(PAIR):
                add_rows(last, h)
            settled(pool, gathered, 16 * PAIR * (last + 4))
            settled(pool, added, 16 * PAIR * (last + 1))

        @block.tensor
        def _(pe):
            pe.wait_ge(ld_vec, 64)
            pe.wait_ge(const_ready, 9)
            nc.tensor.transpose(up_ps[0][:, 0:NV], vec_rows[:], ident[0:NV, 0:NV]).then_inc(vecT_ps, 1)

            def zn_turn(b):
                pe.wait_ge(zn_ready, TT * (b + 1))
                for kb in range(KB):
                    if not (isinstance(b, int) and b <= 1):
                        pe.wait_ge([act1_ready, prod_ready][kb], MB * (b - 1))
                    for t in range(TT):
                        last = nc.tensor.transpose(up_ps[kb][:, t * P:(t + 1) * P], zn[:, t, kb * P:(kb + 1) * P], ident[:])
                    last.then_inc(znT_ps, 1)

            def attn_first(b):
                pe.wait_ge(znT_lo, KB * (b + 1))
                if only(b, 0):
                    pe.wait_ge(w_attn, 2)
                for kb in range(KB):
                    last = product(up_ps[0][:], [w[:, kb].rearrange("p r c -> p (r c)") for w in wkg1],
                                   [z[:, kb, :] for z in znT], kb == 0, kb == KB - 1)
                last.then_inc(kg1_ps, 1)

            def attn_in(b):
                for kb in range(KB):
                    last = product(up_ps[1][:], [w[:, 0, kb, :] for w in wqk], [z[:, kb, :] for z in znT],
                                   kb == 0, kb == KB - 1)
                last.then_inc(q_ps, 1)
                pe.wait_ge(kg1_ready, b + 1)
                pe.wait_ge(ld_small, 16 * 6)
                nc.tensor.matmul(up_ps[0][:], wkg2[:], kg1_sb[:], start=True, stop=True).then_inc(z_ps, 1)
                pe.wait_ge(q_ready, b + 1)
                for kb in range(KB):
                    last = product(up_ps[1][:], [w[:, 1, kb, :] for w in wqk], [z[:, kb, :] for z in znT],
                                   kb == 0, kb == KB - 1)
                last.then_inc(k_ps, 1)

            def values(b):
                for m in range(2):
                    if m == 0:
                        pe.wait_ge(z_min, b + 1)
                        if only(b, 0):
                            pe.wait_ge(w_attn, 3)
                    else:
                        pe.wait_ge(k_ready, b + 1)
                    for kb in range(KB):
                        last = product(up_ps[m][:],
                                       [w[:, kb, m * DB:(m + 1) * DB, :].rearrange("p d h -> p (d h)") for w in wv],
                                       [z[:, kb, :] for z in znT], kb == 0, kb == KB - 1)
                    last.then_inc(v_ps, 1)

            def gates(b):
                for m in range(2):
                    pe.wait_ge(v_lo, 2 * b + m + 1)
                    if m == 0 and only(b, 0):
                        pe.wait_ge(w_attn, 4)
                    for t in range(2 * m, 2 * m + 2):
                        for kb in range(KB):
                            last = product(up_ps[m][:, (t % 2) * D:(t % 2 + 1) * D],
                                           [z[:, kb, t * P:(t + 1) * P] for z in znT],
                                           [w[:, kb, :] for w in wg], kb == 0, kb == KB - 1)
                    last.then_inc(g_ps, 1)

            def spread_v(b, d):
                if d < 2:
                    late(pe, kv_ready, HD * b)
                else:
                    pe.wait_ge(kv_ready, HD * b + d - 1)
                if d == 0 and only(b, 0):
                    pe.wait_ge(spread_ready, 1)
                m, j = divmod(d, DB)
                nc.tensor.matmul(ring[d % 2][:], spread[:, j, :], vT[0][:, m, :], start=True, stop=False)
                nc.tensor.matmul(ring[d % 2][:], spread[:, j, :], vT[1][:, m, :],
                                 start=False, stop=True).then_inc(vrep_ps, 1)

            def sum_keys(b, d):
                pe.wait_ge(qs_ready, HD * b + d + 1)
                if d == 0:
                    late(pe, o_copied, b)
                    late(pe, logits_read, b - 1)
                for t in range(TT):
                    last = nc.tensor.matmul(mix_ps[:, t, d * H:(d + 1) * H], qs[d % 2][:, t * P:(t + 1) * P],
                                            gather_k[:], start=True, stop=True)
                last.then_inc(qs_used, 1)

            def out_turn(b):
                pe.wait_ge(og_ready, b + 1)
                if not only(b, B - 1):
                    pe.wait_ge(g_ready, 2 * (b + 2))
                for kb in range(KB):
                    for t in range(TT):
                        last = nc.tensor.transpose(
                            up_ps[kb][:, t * P:(t + 1) * P],
                            o_sb[:, t].rearrange("p h d -> p (h d)")[:, kb * P:(kb + 1) * P], ident[:])
                    last.then_inc(ogT_ps, 1)

            def out_proj(b):
                pe.wait_ge(ogT_lo, KB * (b + 1))
                late(pe, x2_ready, 2 * b)
                for t in range(TT):
                    for kb in range(KB):
                        last = product(res_ps[:, t, :], [z[:, kb, t * P:(t + 1) * P] for z in ogT],
                                       [w[:, kb, :] for w in wo], kb == 0, kb == KB - 1)
                    last.then_inc(wo_ps, 1)

            def mlp_in(b):
                pe.wait_ge(zn2_ready, TT * (b + 1))
                for kb in range(KB):
                    for t in range(TT):
                        last = nc.tensor.transpose(up_ps[kb][:, t * P:(t + 1) * P], zn2[:, t, kb * P:(kb + 1) * P], ident[:])
                    last.then_inc(zn2T_ps, 1)

            def mlp_up(b, f):
                if f > 0:
                    pe.wait_ge(act1_ready, MB * b + f)
                for kb in range(KB):
                    last = product(up_ps[0][:], [w[:, kb, f * P:(f + 1) * P] for w in w1], [z[:, kb, :] for z in ogT],
                                   kb == 0, kb == KB - 1)
                last.then_inc(h1_ps, 1)

            def mlp_gate(b, f):
                if f > 0:
                    pe.wait_ge(prod_ready, MB * b + f)
                for kb in range(KB):
                    last = product(up_ps[1][:], [w[:, kb, f * P:(f + 1) * P] for w in w3], [z[:, kb, :] for z in ogT],
                                   kb == 0, kb == KB - 1)
                last.then_inc(h3_ps, 1)

            def mlp_down(b, f):
                pe.wait_ge(hT_lo, MB * b + f + 1)
                if f == 0:
                    pe.wait_ge(x1_ready, 2 * (b + 1))
                    pe.wait_ge(number_read, b + 1)
                K = P if f < MB - 1 else MLAST
                for t in range(TT):
                    last = product(res_ps[:, t, :], [z[0:K, t * P:(t + 1) * P] for z in hT[f % 2]],
                                   [w[0:K, f, :] for w in w2], f == 0 and t % 2 == 0, f == MB - 1,
                                   skip_group_check=True)
                last.then_inc(hT_used, 1)

            def x3_turn(b):
                pe.wait_ge(x3_ready, TT * (b + 1))
                pe.wait_ge(o_copied, min(b + 2, B) if isinstance(b, int) else b + 2)
                for kb in range(KB):
                    for t in range(TT):
                        last = nc.tensor.transpose(x3_ps[kb][:, t * P:(t + 1) * P], x3[:, t, kb * P:(kb + 1) * P], ident[:])
                    last.then_inc(x3T_ps, 1)

            def gate(b):
                pe.wait_ge(x3T_ready, KB * (b + 1))
                for t in range(TT):
                    for kb in range(KB):
                        last = nc.tensor.matmul(mix_ps[:, 0, t * E:(t + 1) * E], x3T[:, kb, t * P:(t + 1) * P],
                                                gate_sb[:, kb, :], start=kb == 0, stop=kb == KB - 1)
                last.then_inc(gate_ps, 1)

            def slots(b):
                pe.wait_ge(mask_ready, 2 * b + 1)
                if only(b, B - 1):
                    pe.wait_ge(x2_ready, 2 * B)
                else:
                    pe.wait_ge(x1_ready, 2 * (b + 2))
                for t in range(TT):
                    dst = res_ps[:, 2, t * E:(t + 1) * E]
                    nc.tensor.matmul(dst, earlier[:], mask[:, t, :], start=True, stop=False)
                    for t2 in range(t):
                        nc.tensor.matmul(dst, ones_bf[:], mask[:, t2, :], start=False, stop=False)
                    last = nc.tensor.matmul(dst, ones_bf[:], taken_bf[:], start=False, stop=True)
                last.then_inc(slot_ps, 1)

            def ffn_step(b, step):
                f = step // 2
                if f < MB:
                    if step % 2 == 0:
                        mlp_up(b, f)
                    else:
                        mlp_gate(b, f)
                        if f >= 1:
                            mlp_down(b, f - 1)
                elif step == 2 * MB:
                    mlp_down(b, MB - 1)

            def scan_and_mlp(b, attended):
                for d in range(LEAD, HD):
                    spread_v(b + 1, d)
                    sum_keys(b + 1, d - 2)
                    ffn_step(b, d - LEAD + 2)
                    if attended is not None:
                        if d == HD - 2:
                            zn_turn(attended)
                        elif d == HD - 1:
                            attn_first(attended)
                sum_keys(b + 1, HD - 2)

            def between(routed, projected, attended):
                sum_keys(projected, HD - 1)
                if attended is not None:
                    attn_in(attended)
                    values(attended)
                    gates(attended)
                out_turn(projected)
                if attended is not None:
                    spread_v(attended, 0)
                    spread_v(attended, 1)
                out_proj(projected)
                if routed is not None:
                    x3_turn(routed)
                if attended is not None:
                    spread_v(attended, 2)
                mlp_in(projected)
                if routed is not None:
                    gate(routed)
                pe.wait_ge(zn2T_lo, KB * (projected + 1))
                ffn_step(projected, 0)
                if attended is not None:
                    sum_keys(attended, 0)
                    spread_v(attended, 3)
                ffn_step(projected, 1)
                if attended is not None:
                    sum_keys(attended, 1)
                if routed is not None:
                    slots(routed)

            pe.wait_ge(vec_ready, 1)
            zn_turn(0)
            attn_first(0)
            attn_in(0)
            values(0)
            gates(0)
            for d in range(HD):
                spread_v(0, d)
                if d >= 2:
                    sum_keys(0, d - 2)
                if d == HD - 2:
                    zn_turn(1)
                elif d == HD - 1:
                    attn_first(1)
            sum_keys(0, HD - 2)
            pe.wait_ge(w_mlp, 4)
            between(None, 0, 1)
            with pe.Fori(0, B - 2) as b:
                scan_and_mlp(b, b + 2)
                between(b, b + 1, b + 2)
            scan_and_mlp(B - 2, None)
            between(B - 2, B - 1, None)
            for step in range(2, 2 * MB + 1):
                ffn_step(B - 1, step)
            x3_turn(B - 1)
            gate(B - 1)
            slots(B - 1)
            pe.wait_ge(mask_ready, 2 * B)
            pe.wait_ge(record_ready, B)
            nc.tensor.matmul(up_ps[1][:, 0:E], ones_bf[:], taken_bf[:], start=True, stop=True).then_inc(count_ps, 1)

            def turn(i, first=False):
                pe.wait_ge(xt_ready, i + 1)
                if not first:
                    pe.wait_ge(xT_lo, i)
                for kb in range(KB):
                    for h in range(PAIR):
                        c = kb * TILE + h * P
                        last = nc.tensor.transpose(ring[0][:, c:c + P], xt[:, h, kb * P:(kb + 1) * P], ident[:])
                last.then_inc(xT_ps, 1)

            def fc1(before, e):
                pe.wait_ge(xT_lo, before + 2)
                for half in range(2):
                    late(pe, gelu_done, FB * before + FB // 2 * (1 + half))
                    for f in range(FB // 2 * half, FB // 2 * (half + 1)):
                        for kb in range(KB):
                            last = product(fc1_out[f], [w[:, kb, f * P:(f + 1) * P] for w in ew1[e % 2]],
                                           [z[:, kb, :] for z in xT], kb == 0, kb == KB - 1)
                    last.then_inc(fc1_ps, 1)

            def fc2_half(i, e, h):
                pe.wait_ge(y_summed, PAIR * i + h + 1)
                for f in range(FB):
                    if h == 0 and f % (FB // 2) == 0:
                        pe.wait_ge(hid_lo, 2 * i + f // (FB // 2) + 1)
                    last = product(fc2_out[h], [z[:, f, h * P:(h + 1) * P] for z in hidT],
                                   [w[:, f, :] for w in ew2[e % 2]], f == 0, f == FB - 1)
                last.then_inc(fc2_ps, 1)

            def fc2(i, e):
                for h in range(PAIR):
                    fc2_half(i, e, h)

            def fc2_last(i, e):
                fc2_half(i, e, 0)
                with pe.If(both[e] > 0):
                    fc2_half(i, e, 1)
                with pe.If(both[e] < 1):
                    pe.wait_ge(fc2_ps, PAIR * i + 1)
                    pe.sem_inc(fc2_ps, 1)

            pe.wait_ge(bounds_ready, 3)
            starts = [first_tile(pe, e) for e in range(E)]
            lasts = [first_tile(pe, e + 1, less=1) for e in range(E)]
            both = [pe.value_load(full[0:1, e:e + 1], min_val=0, max_val=1) for e in range(E)]
            pe.wait_ge(packed, E)
            turn(0, first=True)
            for e in range(E):
                before = lasts[e - 1] if e > 0 else -1
                pe.wait_ge(ew1_split, e + 1)
                fc1(before, e)
                turn(before + 2)
                if e > 0:
                    fc2_last(before, e - 1)
                pe.wait_ge(ew2_split, e + 1)
                with pe.If(lasts[e] > starts[e]):
                    with pe.Fori(starts[e], lasts[e]) as i:
                        fc1(i, e)
                        turn(i + 2)
                        fc2(i, e)
            fc2_last(lasts[E - 1], E - 1)

        @block.scalar
        def _(act):
            act.wait_ge(vecT_ps, 1)
            nc.scalar.copy(cols[:], up_ps[0][:, 0:NV]).then_inc(vec_ready, 1)
            act.wait_ge(vec_ready, 1)

            def attn_norm(b):
                act.wait_ge(ln_var, TT * (b + 1))
                nc.scalar.activation(small[:, 0, :], mv[:, :, 1], ACT.Ln, bias=eps[:, 0:1]).then_inc(ln_rstd, 1)
                act.wait_ge(ln_rstd, 3 * b + 1)
                nc.scalar.activation(small[:, 1, :], small[:, 0, :], ACT.Exp, scale=-1.0).then_inc(ln_rstd, 1)
                nc.scalar.activation(small[:, 2, :], small[:, 0, :], ACT.Exp, scale=-0.5).then_inc(ln_rstd, 1)
                act.wait_ge(ln_ms, b + 1)
                nc.scalar.activation(small[:, 4, :], small[:, 3, :], ACT.Ln, bias=eps[:, 0:1]).then_inc(ln_rms, 1)
                act.wait_ge(ln_rms, 2 * b + 1)
                nc.scalar.activation(small[:, 5, :], small[:, 4, :], ACT.Exp, scale=-0.5).then_inc(ln_rms, 1)

            def zn_high(b):
                for kb in range(KB):
                    act.wait_ge(znT_ps, KB * b + kb + 1)
                    nc.scalar.activation(znT[0][:, kb, :], up_ps[kb][:], ACT.Copy,
                                         scale=cols[:, LN1_C + kb:LN1_C + kb + 1]).then_inc(znT_hi, 1)

            def attn_in(b):
                act.wait_ge(kg1_ps, b + 1)
                nc.scalar.copy(kg1_sb[:], up_ps[0][0:LOWRANK, :]).then_inc(kg1_ready, 1)
                act.wait_ge(q_ps, b + 1)
                late(act, qs_ready, HD * b)
                nc.scalar.copy(q_sb[:], up_ps[1][:]).then_inc(q_ready, 1)
                act.wait_ge(z_ps, b + 1)
                late(act, lsig_ready, b)
                nc.scalar.activation(soft[:], up_ps[0][:], ACT.Abs, bias=cols[:, BK_C:BK_C + 1]).then_inc(z_abs, 1)
                act.wait_ge(z_abs, b + 1)
                nc.scalar.activation(soft[:], soft[:], ACT.Exp, scale=-1.0).then_inc(z_exp, 1)
                act.wait_ge(z_exp, b + 1)
                nc.scalar.activation(soft[:], soft[:], ACT.Ln, bias=unit[:, 0:1]).then_inc(z_ln, 1)
                act.wait_ge(k_ps, b + 1)
                late(act, kv_ready, HD * b)
                nc.scalar.mul(k_sb[:], up_ps[1][:], SCALE).then_inc(k_ready, 1)
                act.wait_ge(lsig_ready, b + 1)
                late(act, state_ready, HD * b)
                nc.scalar.activation(decay[:], lsig[:], ACT.Exp, scale=1.0 / NORMALIZER).then_inc(decay_ready, 1)

            def values(b):
                for m in range(2):
                    act.wait_ge(v_ps, 2 * b + m + 1)
                    nc.scalar.copy(vT[0][:, m, :], up_ps[m][:]).then_inc(v_hi, 1)

            def head_norm(b):
                act.wait_ge(gn_var, b + 1)
                nc.scalar.activation(o_sum[:, 2], o_sum[:, 1], ACT.Ln, scale=1.0 / HD, bias=eps[:, 0:1]).then_inc(gn_ln, 1)
                act.wait_ge(gn_ln, b + 1)
                nc.scalar.activation(o_sum[:, 3], o_sum[:, 2], ACT.Exp, scale=-0.5).then_inc(gn_rstd, 1)

            def out_high(b):
                for kb in range(KB):
                    act.wait_ge(ogT_ps, KB * b + kb + 1)
                    nc.scalar.copy(ogT[0][:, kb, :], up_ps[kb][:]).then_inc(ogT_hi, 1)

            def mlp_norm(b):
                for t in range(TT):
                    if t % 2 == 0:
                        act.wait_ge(x1_ready, 2 * b + t // 2 + 1)
                    nc.scalar.activation(o_sq[:, t].rearrange("p h d -> p (h d)"), x1[:, t, :], ACT.Square,
                                         accum_out=rms[:, 0, t:t + 1]).then_inc(x1_squares, 1)
                act.wait_ge(x1_squares, TT * (b + 1))
                nc.scalar.activation(rms[:, 1, :], rms[:, 0, :], ACT.Ln, scale=1.0 / D, bias=eps[:, 0:1]).then_inc(rms_ln, 1)
                act.wait_ge(rms_ln, b + 1)
                nc.scalar.activation(rms[:, 1, :], rms[:, 1, :], ACT.Exp, scale=-0.5).then_inc(rms_ready, 1)
                act.wait_ge(rms_ready, b + 1)
                for t in range(TT):
                    nc.scalar.activation(zn2[:, t, :], x1[:, t, :], ACT.Copy, scale=rms[:, 1, t:t + 1]).then_inc(zn2_ready, 1)

            def mlp_high(b):
                for kb in range(KB):
                    act.wait_ge(zn2T_ps, KB * b + kb + 1)
                    nc.scalar.activation(ogT[0][:, kb, :], up_ps[kb][:], ACT.Copy,
                                         scale=cols[:, LN2_C + kb:LN2_C + kb + 1]).then_inc(zn2T_hi, 1)

            def silu_gate(b):
                act.wait_ge(g_ready, 2 * (b + 1))
                late(act, og_ready, b)
                nc.scalar.activation(silu_g[:], g_sb[:], ACT.Silu).then_inc(silu_ready, 1)

            def mlp(b, f):
                act.wait_ge(h1_ps, MB * b + f + 1)
                if f > 0:
                    act.wait_ge(prod_ready, MB * b + f)
                nc.scalar.activation(act1[:], up_ps[0][:], ACT.Silu).then_inc(act1_ready, 1)
                act.wait_ge(prod_ready, MB * b + f + 1)
                if f >= 2:
                    act.wait_ge(hT_used, MB * b + f - 1)
                nc.scalar.copy(hT[f % 2][0][:], prod[:]).then_inc(hT_hi, 1)

            def route_norm(b):
                act.wait_ge(ln2_var, TT * (b + 1))
                nc.scalar.activation(small2[:, 0, :], mv2[:, :, 1], ACT.Ln, bias=eps[:, 0:1]).then_inc(ln2_ln, 1)
                act.wait_ge(ln2_ln, b + 1)
                nc.scalar.activation(small2[:, 1, :], small2[:, 0, :], ACT.Exp, scale=-0.5).then_inc(ln2_rstd, 1)

            def x3_copy(b):
                for kb in range(KB):
                    act.wait_ge(x3T_ps, KB * b + kb + 1)
                    nc.scalar.copy(x3T[:, kb, :], x3_ps[kb]).then_inc(x3T_ready, 1)

            def score(b):
                act.wait_ge(score_diff, b + 1)
                nc.scalar.activation(scores[:, 1, :], scores[:, 0, :], ACT.Exp).then_inc(score_exp, 1)

            nc.scalar.preload_act_table_set(LN_EXP)
            attn_norm(0)
            zn_high(0)
            attn_in(0)
            values(0)
            silu_gate(0)
            for i, (raw, w, ld, n) in enumerate([(raw_o, wo, ld_o, 16), (raw_1, w1, ld_w1, 16), (raw_3, w3, ld_w3, 16)]):
                act.wait_ge(ld, n)
                if i == 1:
                    act.wait_ge(pads_set, 2)
                nc.scalar.copy(w[0][:], raw[:]).then_inc(w_mlp_hi, 1)
            act.wait_ge(ld_w2, 32)
            nc.scalar.copy(w2[0][:, 0:MB - 1, :], raw_2[:, 0:MB - 1, :])
            nc.scalar.copy(w2[0][0:MLAST, MB - 1, :], raw_2[0:MLAST, MB - 1, :]).then_inc(w_mlp_hi, 1)
            def between(routed, projected, attended):
                if attended is not None:
                    zn_high(attended)
                    attn_in(attended)
                    values(attended)
                head_norm(projected)
                out_high(projected)
                if routed is not None:
                    route_norm(routed)
                mlp_norm(projected)
                if routed is not None:
                    x3_copy(routed)
                mlp_high(projected)
                if routed is not None:
                    score(routed)
                mlp(projected, 0)
                if attended is not None:
                    silu_gate(attended)

            nc.scalar.preload_act_table_set(LN_EXP)
            attn_norm(1)
            between(None, 0, 1)
            with act.Fori(0, B - 2) as b:
                for f in range(1, MB):
                    mlp(b, f)
                    if f == 4:
                        nc.scalar.preload_act_table_set(LN_EXP)
                        attn_norm(b + 2)
                nc.scalar.preload_act_table_set(LN_EXP)
                between(b, b + 1, b + 2)
            for f in range(1, MB):
                mlp(B - 2, f)
            nc.scalar.preload_act_table_set(LN_EXP)
            between(B - 2, B - 1, None)

            def high_part(w, raw, loaded, e, done):
                act.wait_ge(loaded, 16 * (e + 1))
                nc.scalar.copy(w[e % 2][0][:], raw[:]).then_inc(done, 1)

            for f in range(1, MB):
                mlp(B - 1, f)
                if f == 2:
                    high_part(ew1, raw_e1, ld_e1, 0, ew1_hi)
                elif f == 4:
                    high_part(ew2, raw_e2, ld_e2, 0, ew2_hi)
            nc.scalar.preload_act_table_set(LN_EXP)
            route_norm(B - 1)
            x3_copy(B - 1)
            score(B - 1)

            def x_high(i):
                act.wait_ge(xT_ps, i + 1)
                nc.scalar.copy(xT[0][:], ring[0][:].rearrange("p (k t) -> p k t", k=KB)).then_inc(xT_hi, 1)

            def gelu(i, e, first=False):
                for f in range(FB):
                    half = f // (FB // 2)
                    if f % (FB // 2) == 0:
                        act.wait_ge(fc1_ps, 2 * i + half + 1)
                        if not first and half == 0:
                            act.wait_ge(hid_lo, 2 * i)
                    nc.scalar.activation(hid[:, f, :], fc1_out[f], ACT.Gelu,
                                         bias=cols[:, B1_C + e * FB + f:B1_C + e * FB + f + 1]).then_inc(gelu_done, 1)

            def hid_high(i, first=False):
                if not first:
                    act.wait_ge(fc2_ps, PAIR * i)
                for half in range(2):
                    fs = slice(half * FB // 2, (half + 1) * FB // 2)
                    act.wait_ge(gelu_done, FB * i + FB // 2 * (half + 1))
                    nc.scalar.copy(hidT[0][:, fs, :], hid[:, fs, :]).then_inc(hid_hi, 1)

            act.wait_ge(bounds_ready, 3)
            starts = [first_tile(act, e) for e in range(E)]
            lasts = [first_tile(act, e + 1, less=1) for e in range(E)]
            x_high(0)
            for e in range(E):
                start, last = starts[e], lasts[e]
                if e + 1 < E:
                    late(act, fc1_ps, 2 * start)
                    high_part(ew1, raw_e1, ld_e1, e + 1, ew1_hi)
                gelu(start, e, first=e == 0)
                x_high(start + 1)
                hid_high(start, first=e == 0)
                if e + 1 < E:
                    late(act, fc2_ps, PAIR * start)
                    high_part(ew2, raw_e2, ld_e2, e + 1, ew2_hi)
                with act.If(last > start):
                    with act.Fori(start, last) as i:
                        gelu(i + 1, e)
                        x_high(i + 2)
                        hid_high(i + 1)

        @block.vector
        def _(dve):
            V = nc.vector
            V.memset(eps[:], EPS).then_inc(dve_set, 1)
            V.memset(unit[:], 1.0).then_inc(dve_set, 1)
            V.memset(taken[:], 0.0).then_inc(dve_set, 1)
            V.memset(taken_bf[:], 0.0).then_inc(dve_set, 1)
            dve.sem_inc(number_read, 1)

            def attn_stats(b):
                dve.wait_ge(ld_x, 16 * (b + 1))
                for t in range(TT):
                    V.bn_stats(stats[:, t, :], xin[:, t, :]).then_inc(ln_stat, 1)
                settled(dve, ln_stat, TT * (b + 1))
                for t in range(TT):
                    V.bn_aggr(mv[:, t, :], stats[:, t, :]).then_inc(ln_var, 1)

            def attn_norm(b):
                dve.wait_ge(ln_rstd, 3 * b + 2)
                V.tensor_tensor(small[:, 3, :], mv[:, :, 1], small[:, 1, :], ALU.mult).then_inc(ln_ms, 1)
                dve.wait_ge(ln_rstd, 3 * b + 3)
                late(dve, kept_y, 16 * b)
                for t in range(TT):
                    V.tensor_scalar(y[:, t, :], xin[:, t, :], mv[:, t, 0:1], small[:, 2, t:t + 1],
                                    ALU.subtract, ALU.mult).then_inc(y_ready, 1)
                dve.wait_ge(ln_rms, 2 * b + 2)
                late(dve, znT_ps, KB * b)
                for t in range(TT):
                    dve.wait_ge(y_ready, TT * b + t + 1)
                    V.tensor_scalar(zn[:, t, :], y[:, t, :], small[:, 5, t:t + 1], None, ALU.mult).then_inc(zn_ready, 1)

            def attn_split(b):
                for kb in range(KB):
                    dve.wait_ge(znT_hi, KB * b + kb + 1)
                    V.scalar_tensor_tensor(znT[1][:, kb, :], up_ps[kb][:], cols[:, LN1_C + kb:LN1_C + kb + 1],
                                           znT[0][:, kb, :].bitcast(F32), ALU.mult, ALU.subtract).then_inc(znT_lo, 1)

            def decay_min(b):
                dve.wait_ge(z_abs, b + 1)
                late(dve, decay_ready, b)
                V.tensor_scalar(lsig[:], up_ps[0][:], cols[:, BK_C:BK_C + 1], 0.0, ALU.add, ALU.min).then_inc(z_min, 1)

            def decay_log(b):
                dve.wait_ge(z_ln, b + 1)
                dve.wait_ge(z_min, b + 1)
                V.tensor_tensor(lsig[:], lsig[:], soft[:], ALU.subtract).then_inc(lsig_ready, 1)

            def v_low(b):
                for m in range(2):
                    dve.wait_ge(v_hi, 2 * b + m + 1)
                    V.tensor_tensor(vT[1][:, m, :], up_ps[m][:], vT[0][:, m, :].bitcast(F32), ALU.subtract).then_inc(v_lo, 1)

            def attn_gate(b):
                late(dve, silu_ready, b)
                for m in range(2):
                    dve.wait_ge(g_ps, 2 * b + m + 1)
                    V.tensor_tensor(g_sb[:, 2 * m:2 * m + 2, :], up_ps[m][:].rearrange("p (t d) -> p t d", d=D),
                                    bg_bc[:].unsqueeze(1).broadcast_to([P, 2, D]), ALU.add).then_inc(g_ready, 1)

            def scan(b, d):
                n = HD * b + d
                dve.wait_ge(vrep_ps, n + 1)
                if d == 0:
                    dve.wait_ge(k_ready, b + 1)
                    dve.wait_ge(decay_ready, b + 1)
                late(dve, state_ready, n - 1)
                V.tensor_tensor(kv[d % 2][:], ring[d % 2][:], k_sb[:], ALU.mult).then_inc(kv_ready, 1)
                dve.wait_ge(kv_ready, n + 1)
                late(dve, qs_ready, n - 1)
                V.tensor_tensor_scan(state[d % 2][:], decay[:], kv[d % 2][:], 0.0, ALU.mult, ALU.add).then_inc(state_ready, 1)

            o3 = o_sb[:].rearrange("p t h d -> p (t h) d")
            sq3 = o_sq[:].rearrange("p t h d -> p (t h) d")
            sm = o_sum[:].rearrange("p c t h -> p c (t h)")

            def over_d(v):
                return v.unsqueeze(2).broadcast_to([P, TT * H, HD])

            def take_heads(b):
                dve.wait_ge(qs_used, HD * (b + 1))
                late(dve, ogT_ps, KB * b)
                heads = mix_ps[:].rearrange("p t (d h) -> p t h d", h=H)
                V.tensor_reduce(o_sum[:, 0], heads, AX.X, ALU.add).then_inc(gn_chain, 1)
                dve.wait_ge(gn_chain, 4 * b + 1)
                V.tensor_scalar(o_sum[:, 0], o_sum[:, 0], 1.0 / HD, None, ALU.mult).then_inc(gn_chain, 1)
                dve.wait_ge(gn_chain, 4 * b + 2)
                V.tensor_tensor(o_sb[:], heads, o_sum[:, 0].unsqueeze(3).broadcast_to([P, TT, H, HD]),
                                ALU.subtract).then_inc(o_copied, 1)

            def head_var(b):
                dve.wait_ge(o_copied, b + 1)
                late(dve, x1_squares, TT * b)
                V.tensor_tensor(sq3, o3, o3, ALU.mult).then_inc(gn_chain, 1)
                dve.wait_ge(gn_chain, 4 * b + 3)
                V.tensor_reduce(sm[:, 1], sq3, AX.X, ALU.add).then_inc(gn_var, 1)

            def head_scale(b):
                dve.wait_ge(silu_ready, b + 1)
                V.tensor_tensor(o3, o3, silu_g[:].rearrange("p t (h d) -> p (t h) d", d=HD), ALU.mult).then_inc(gn_chain, 1)
                dve.wait_ge(gn_rstd, b + 1)
                dve.wait_ge(gn_chain, 4 * b + 4)
                V.tensor_tensor(o3, o3, over_d(sm[:, 3]), ALU.mult).then_inc(og_ready, 1)

            def out_proj(b):
                for kb in range(KB):
                    dve.wait_ge(ogT_hi, KB * b + kb + 1)
                    V.tensor_tensor(ogT[1][:, kb, :], up_ps[kb][:], ogT[0][:, kb, :].bitcast(F32),
                                    ALU.subtract).then_inc(ogT_lo, 1)

            def first_sum(b):
                late(dve, x1x_ready, b)
                for m in range(2):
                    dve.wait_ge(wo_ps, TT * b + 2 * m + 2)
                    if m == 0:
                        dve.wait_ge(kept_y, 16 * (b + 1))
                    V.tensor_tensor(x1[:, 2 * m:2 * m + 2, :], res_ps[:, 2 * m:2 * m + 2, :],
                                    y_keep[:, 2 * m:2 * m + 2, :], ALU.add).then_inc(x1_ready, 1)

            def mlp_split(b):
                for kb in range(KB):
                    dve.wait_ge(zn2T_hi, KB * b + kb + 1)
                    V.scalar_tensor_tensor(ogT[1][:, kb, :], up_ps[kb][:], cols[:, LN2_C + kb:LN2_C + kb + 1],
                                           ogT[0][:, kb, :].bitcast(F32), ALU.mult, ALU.subtract).then_inc(zn2T_lo, 1)

            def mlp(b, f):
                dve.wait_ge(act1_ready, MB * b + f + 1)
                dve.wait_ge(h3_ps, MB * b + f + 1)
                late(dve, hT_lo, MB * b + f)
                V.tensor_tensor(prod[:], up_ps[1][:], act1[:], ALU.mult).then_inc(prod_ready, 1)
                dve.wait_ge(hT_hi, MB * b + f + 1)
                V.tensor_tensor(hT[f % 2][1][:], prod[:], hT[f % 2][0][:].bitcast(F32), ALU.subtract).then_inc(hT_lo, 1)

            def residual(b):
                dve.wait_ge(hT_used, MB * (b + 1))
                dve.wait_ge(x1x_ready, b + 1)
                dve.wait_ge(x23_free, b + 1)
                for m in range(2):
                    V.tensor_tensor(x2[:, 2 * m:2 * m + 2, :], res_ps[:, 2 * m:2 * m + 2, :],
                                    x1x[:, 2 * m:2 * m + 2, :], ALU.add).then_inc(x2_ready, 1)

            RC = 28

            def need(b, n):
                settled(dve, route_chain, RC * b + n)

            def route_norm(b):
                dve.wait_ge(x2_ready, 2 * (b + 1))
                for t in range(TT):
                    V.bn_stats(stats2[:, t, :], x2[:, t, :]).then_inc(ln2_stat, 1)
                settled(dve, ln2_stat, TT * (b + 1))
                for t in range(TT):
                    V.bn_aggr(mv2[:, t, :], stats2[:, t, :]).then_inc(ln2_var, 1)

            def route_x3(b):
                dve.wait_ge(ln2_rstd, b + 1)
                dve.wait_ge(x23_free, b + 1)
                for t in range(TT):
                    V.tensor_scalar(x3[:, t, :], x2[:, t, :], mv2[:, t, 0:1], small2[:, 1, t:t + 1],
                                    ALU.subtract, ALU.mult).then_inc(x3_ready, 1)

            def choose(b):
                dve.wait_ge(gate_ps, b + 1)
                V.tensor_tensor(logit[:], mix_ps[:, 0, 0:TT * E].rearrange("p (t e) -> p t e", e=E),
                                gb_bc[:].unsqueeze(1).broadcast_to([P, TT, E]), ALU.add).then_inc(logits_read, 1)
                settled(dve, logits_read, b + 1)
                for t in range(TT):
                    V.max(top[:, t, :], logit[:, t, :]).then_inc(route_chain, 1)
                need(b, 4)
                for t in range(TT):
                    V.max_index(topi[:, t, :], top[:, t, :], logit[:, t, :]).then_inc(route_chain, 1)
                V.tensor_tensor(scores[:, 0, :], top[:, :, 1], top[:, :, 0], ALU.subtract).then_inc(score_diff, 1)
                need(b, 8)
                V.tensor_copy(topf[:], topi[:, :, 0:2]).then_inc(route_chain, 1)
                need(b, 9)
                for k in range(2):
                    V.tensor_tensor(chosen[:, k], eight[:].unsqueeze(1).broadcast_to([P, TT, E]),
                                    topf[:, :, k:k + 1].broadcast_to([P, TT, E]), ALU.is_equal).then_inc(route_chain, 1)
                need(b, 11)
                V.tensor_tensor(mask[:], chosen[:, 0], chosen[:, 1], ALU.add).then_inc(mask_ready, 1)
                V.tensor_tensor(picked[:], chosen[:], al_bc[:].unsqueeze(1).unsqueeze(1).broadcast_to([P, 2, TT, E]),
                                ALU.mult).then_inc(route_chain, 1)

            def place(b):
                dve.wait_ge(score_exp, b + 1)
                V.tensor_scalar(scores[:, 2, :], scores[:, 1, :], 1.0, None, ALU.add).then_inc(route_chain, 1)
                dve.wait_ge(slot_ps, b + 1)
                V.tensor_tensor(number[:], res_ps[:, 2, 0:TT * E].rearrange("p (t e) -> p t e", e=E),
                                first_number[:].unsqueeze(1).broadcast_to([P, TT, E]), ALU.add).then_inc(number_read, 1)
                need(b, 13)
                V.reciprocal(scores[:, 2, :], scores[:, 2, :]).then_inc(route_chain, 1)
                V.tensor_reduce(scores[:, 4:6, :], picked[:], AX.X, ALU.add).then_inc(route_chain, 1)
                V.tensor_reduce(taken_t[:], mask[:].rearrange("p t e -> p e t"), AX.X, ALU.add).then_inc(route_chain, 1)
                settled(dve, number_read, b + 2)
                for k in range(2):
                    V.tensor_tensor(numbered[:, k], chosen[:, k], number[:], ALU.mult).then_inc(route_chain, 1)
                need(b, 18)
                V.tensor_tensor(scores[:, 3, :], scores[:, 1, :], scores[:, 2, :], ALU.mult).then_inc(route_chain, 1)
                V.tensor_reduce(pos[:], numbered[:], AX.X, ALU.add).then_inc(route_chain, 1)
                V.tensor_tensor(taken[:], taken[:], taken_t[:], ALU.add).then_inc(route_chain, 1)
                dve.wait_ge(record_free, b + 1)
                for k in range(2):
                    V.tensor_copy(record[:, k, :, 0:2],
                                  token_id[:, bass.ds(TT * b, TT)].unsqueeze(2).broadcast_to([P, TT, 2])
                                  ).then_inc(route_chain, 1)
                need(b, 20)
                V.tensor_copy(pos_i[:, 0], pos[:]).then_inc(route_chain, 1)
                V.tensor_tensor(record[:, :, :, 2].bitcast(F32), scores[:, 2:4, :], scores[:, 4:6, :],
                                ALU.mult).then_inc(route_chain, 1)
                need(b, 24)
                V.tensor_scalar(pos_i[:, 1], pos_i[:, 0], P - 1, None, ALU.bitwise_and).then_inc(route_chain, 1)
                V.tensor_scalar(pos_i[:, 2], pos_i[:, 0], 7, None, ALU.arith_shift_right).then_inc(route_chain, 1)
                V.tensor_copy(taken_bf[:], taken[:]).then_inc(mask_ready, 1)
                need(b, 27)
                V.scalar_tensor_tensor(pos[:], pos_i[:, 1], float(E * COLS), pos_i[:, 2], ALU.mult,
                                       ALU.add).then_inc(route_chain, 1)
                need(b, 28)
                V.tensor_copy(where[:], pos[:]).then_inc(record_ready, 1)

            def low_part(w, raw, ready):
                return V.tensor_tensor(w[1][:], raw, w[0][:].bitcast(F32), ALU.subtract).then_inc(ready, 1)

            attn_stats(0)
            attn_norm(0)
            dve.wait_ge(ld_qk, 48)
            V.tensor_copy(wqk[0][:], raw_qk[:]).then_inc(split_raw, 1)
            kg1_in = raw_kg1[:].unsqueeze(2).broadcast_to([P, KB, P // LOWRANK, LOWRANK])
            V.tensor_copy(wkg1[0][:], kg1_in).then_inc(split_raw, 1)
            dve.wait_ge(split_raw, 2)
            low_part(wqk, raw_qk[:], w_attn)
            low_part(wkg1, kg1_in, w_attn)
            dve.wait_ge(vec_ready, 1)
            attn_split(0)
            dve.wait_ge(ld_v, 16)
            v_in = raw_v[:].rearrange("p k (h d) -> p k d h", d=HD)
            V.tensor_copy(wv[0][:], v_in).then_inc(split_raw, 1)
            dve.wait_ge(split_raw, 3)
            low_part(wv, v_in, w_attn)
            dve.wait_ge(ld_g, 16)
            V.tensor_copy(wg[0][:], raw_g[:]).then_inc(split_raw, 1)
            dve.wait_ge(split_raw, 4)
            low_part(wg, raw_g[:], w_attn)
            dve.wait_ge(const_ready, 2)
            V.tensor_copy(spread[:], spread_f[:]).then_inc(spread_ready, 1)
            decay_min(0)
            decay_log(0)
            v_low(0)
            dve.wait_ge(ld_small, 16 * 6)
            attn_gate(0)
            for d in range(HD):
                scan(0, d)
                if d in (3, 6, 9):
                    i = (3, 6, 9).index(d)
                    dve.wait_ge(w_mlp_hi, i + 1)
                    low_part([wo, w1, w3][i], [raw_o, raw_1, raw_3][i][:], w_mlp)
                elif d == 11:
                    attn_stats(1)
                elif d == 12:
                    attn_norm(1)
                elif d == HD - 2:
                    attn_split(1)
            dve.wait_ge(w_mlp_hi, 4)
            V.tensor_tensor(w2[1][:, 0:MB - 1, :], raw_2[:, 0:MB - 1, :], w2[0][:, 0:MB - 1, :].bitcast(F32), ALU.subtract)
            V.tensor_tensor(w2[1][0:MLAST, MB - 1, :], raw_2[0:MLAST, MB - 1, :],
                            w2[0][0:MLAST, MB - 1, :].bitcast(F32), ALU.subtract).then_inc(w_mlp, 1)
            dve.wait_ge(const_ready, 10)

            def between(routed, projected, attended):
                if routed is not None:
                    residual(routed)
                take_heads(projected)
                if attended is not None:
                    decay_min(attended)
                    decay_log(attended)
                head_var(projected)
                if attended is not None:
                    v_low(attended)
                head_scale(projected)
                if attended is not None:
                    attn_gate(attended)
                out_proj(projected)
                if routed is not None:
                    route_norm(routed)
                first_sum(projected)
                if routed is not None:
                    route_x3(routed)
                if attended is not None:
                    scan(attended, 0)
                    scan(attended, 1)
                mlp_split(projected)
                if routed is not None:
                    choose(routed)
                if attended is not None:
                    scan(attended, 2)
                mlp(projected, 0)
                if attended is not None:
                    scan(attended, 3)
                if routed is not None:
                    place(routed)

            between(None, 0, 1)
            with dve.Fori(0, B - 2) as b:
                for d in range(LEAD, HD):
                    scan(b + 1, d)
                    step = d - LEAD + 2
                    if step % 2 == 1 and step < 2 * MB:
                        mlp(b, step // 2)
                    elif step == 4:
                        attn_stats(b + 2)
                    elif step == 10:
                        attn_norm(b + 2)
                    elif step == 12:
                        attn_split(b + 2)
                between(b, b + 1, b + 2)
            for d in range(LEAD, HD):
                scan(B - 1, d)
                step = d - LEAD + 2
                if step % 2 == 1 and step < 2 * MB:
                    mlp(B - 2, step // 2)
            between(B - 2, B - 1, None)

            def expert_low(w, raw, high, e, done):
                dve.wait_ge(high, e + 1)
                V.tensor_tensor(w[e % 2][1][:], raw[:], w[e % 2][0][:].bitcast(F32), ALU.subtract).then_inc(done, 1)

            for f in range(1, MB):
                mlp(B - 1, f)
                if f == 2:
                    expert_low(ew1, raw_e1, ew1_hi, 0, ew1_split)
                elif f == 4:
                    expert_low(ew2, raw_e2, ew2_hi, 0, ew2_split)
            residual(B - 1)
            route_norm(B - 1)
            route_x3(B - 1)
            choose(B - 1)
            place(B - 1)

            dve.wait_ge(mask_ready, 2 * B)
            V.memset(taken[:], 1.0).then_inc(bounds_chain, 1)
            dve.wait_ge(count_ps, 1)
            V.tensor_tensor(over[:], up_ps[1][:, 0:E].unsqueeze(2).broadcast_to([P, E, T // P]),
                            column_steps[:].unsqueeze(1).broadcast_to([P, E, T // P]), ALU.is_gt).then_inc(bounds_chain, 1)
            dve.wait_ge(bounds_chain, 2)
            V.tensor_reduce(tiles_f[:], over[:].rearrange("p e (n h) -> p e n h", h=PAIR)[:, :, :, 0], AX.X,
                            ALU.add).then_inc(bounds_chain, 1)
            V.tensor_reduce(columns_f[:], over[:], AX.X, ALU.add).then_inc(bounds_chain, 1)
            dve.wait_ge(bounds_chain, 3)
            V.tensor_scalar(tiles_f[:], tiles_f[:], float(MIN_TILES), None, ALU.max).then_inc(bounds_chain, 1)
            dve.wait_ge(bounds_chain, 5)
            V.tensor_tensor_scan(cum_f[:], taken[:], tiles_f[:], 0.0, ALU.mult, ALU.add).then_inc(bounds_chain, 1)
            V.scalar_tensor_tensor(full_f[:], tiles_f[:], float(PAIR), columns_f[:], ALU.mult,
                                   ALU.subtract).then_inc(bounds_chain, 1)
            dve.wait_ge(bounds_chain, 6)
            for less in range(2):
                V.tensor_scalar(bounds[:, less, 1:E + 1], cum_f[:], float(-less), None, ALU.add).then_inc(bounds_ready, 1)
            dve.wait_ge(bounds_chain, 7)
            V.tensor_scalar(full[:], full_f[:], 0.0, None, ALU.is_equal).then_inc(bounds_ready, 1)
            dve.wait_ge(bounds_ready, 3)

            starts = [first_tile(dve, e) for e in range(E)]
            lasts = [first_tile(dve, e + 1, less=1) for e in range(E)]
            dve.wait_ge(ld_table, 16)
            for e in range(E):
                if e > 0:
                    dve.wait_ge(packed, e)
                V.tensor_copy(table[:, bass.ds(PAIR * starts[e], COLS), :],
                              table_all[:, e * COLS:(e + 1) * COLS, :]).then_inc(packed, 1)

            def x_low(i):
                dve.wait_ge(xT_hi, i + 1)
                V.tensor_tensor(xT[1][:], ring[0][:].rearrange("p (k t) -> p k t", k=KB),
                                xT[0][:].bitcast(F32), ALU.subtract).then_inc(xT_lo, 1)

            def hand_over(i, first=False):
                dve.wait_ge(gathered, 16 * PAIR * (i + 1))
                if not first:
                    dve.wait_ge(xT_ps, i)
                V.tensor_copy(xt[:], landing[:]).then_inc(xt_ready, 1)

            def hid_low(i):
                for half in range(2):
                    fs = slice(half * FB // 2, (half + 1) * FB // 2)
                    dve.wait_ge(hid_hi, 2 * i + half + 1)
                    V.tensor_tensor(hidT[1][:, fs, :], hid[:, fs, :], hidT[0][:, fs, :].bitcast(F32),
                                    ALU.subtract).then_inc(hid_lo, 1)

            def add_bias(i, e):
                for h in range(PAIR):
                    dve.wait_ge(fc2_ps, PAIR * i + h + 1)
                    dve.wait_ge(y_weighed, PAIR * i + h + 1)
                    V.tensor_tensor(y_sum[:, h, :], fc2_out[h], b2_bc[:, e, :], ALU.add).then_inc(y_summed, 1)

            def weigh(i):
                dve.wait_ge(y_free, i + 1)
                for h in range(PAIR):
                    dve.wait_ge(y_summed, PAIR * (i + 1) + h + 1)
                    V.tensor_scalar(y_out[:, h, :], y_sum[:, h, :], table[:, bass.ds(PAIR * i + h, 1), 2].bitcast(F32),
                                    None, ALU.mult).then_inc(y_weighed, 1)

            dve.sem_inc(y_summed, PAIR)
            dve.sem_inc(y_weighed, PAIR)
            dve.wait_ge(packed, E)
            hand_over(0, first=True)
            x_low(0)
            hand_over(1)
            for e in range(E):
                start, last = starts[e], lasts[e]
                if e + 1 < E:
                    expert_low(ew1, raw_e1, ew1_hi, e + 1, ew1_split)
                x_low(start + 1)
                if e > 0:
                    add_bias(lasts[e - 1], e - 1)
                hid_low(start)
                hand_over(start + 2)
                if e > 0:
                    weigh(lasts[e - 1])
                if e + 1 < E:
                    expert_low(ew2, raw_e2, ew2_hi, e + 1, ew2_split)
                with dve.If(last > start):
                    with dve.Fori(start, last) as i:
                        x_low(i + 2)
                        add_bias(i, e)
                        hid_low(i + 1)
                        hand_over(i + 3)
                        weigh(i)
            add_bias(lasts[E - 1], E - 1)
            weigh(lasts[E - 1])


_INS = ['x', 'Wq', 'Wk', 'Wkg1', 'Wkg2', 'bkg2', 'Wv', 'Wg', 'bg', 'Wo', 'ln1_w', 'ln2_w', 'W1', 'W3', 'W2']
_INS = ['L0_attn_' + n for n in _INS]
_INS += ['L0_ffn_' + n for n in ['gate_w', 'gate_b', 'fc1_w', 'fc1_b', 'fc2_w', 'fc2_b', 'alpha']]


def kernel(**inputs):
    import numpy as _np
    import concourse.bacc as _bacc
    from concourse import mybir as _mybir
    from concourse.bass_utils import run_bass_kernel_spmd as _run

    nc = _bacc.Bacc("TRN2", target_bir_lowering=False, num_devices=1)
    arrays, args = {}, []
    for name in _INS:
        a = _np.ascontiguousarray(inputs[name])
        arrays[f"in_{name}_dram"] = a
        args.append(nc.dram_tensor(f"in_{name}_dram", a.shape, _mybir.dt.from_np(a.dtype), kind="ExternalInput").ap())
    shape = arrays["in_L0_attn_x_dram"].shape
    args.append(nc.dram_tensor("out_0_dram", shape, _mybir.dt.float32, kind="ExternalOutput").ap())
    build(nc, *args)
    r = _run(nc, [arrays], core_ids=[0])
    return r.results[0]["out_0_dram"]
```
